# Optimizing a Trainium2 kernel written in Bass

```python
import numpy as np
import jax
import jax.numpy as jnp

def _softmax(x, axis=-1):
    return jax.nn.softmax(x, axis=axis)

def _gelu(x):
    return jax.nn.gelu(x, approximate=True)

def _silu(x):
    return jax.nn.silu(x)

def _sigmoid(x):
    return jax.nn.sigmoid(x)

def _layernorm(x, axis=-1, eps=1e-05):
    m = jnp.mean(x, axis=axis, keepdims=True)
    v = jnp.var(x, axis=axis, keepdims=True)
    return (x - m) / jnp.sqrt(v + eps)

def _scatter_add(tgt, idx, src, axis=0):
    return tgt.at[idx].add(src)

def _segment_sum(src, seg, n):
    return jax.ops.segment_sum(src, seg, n)
kernel_name = 'mk_gnn_resnorm_d2_gnn_r8_6b7390'

def setup_inputs(seed: int=0):
    np.random.seed(seed)
    _w = jnp.asarray

    def _rec_inputs():
        import jax
        import jax.numpy as jnp
        _gk = jax.random.key(seed)
        x = -0.0002949 + 1 * jax.random.normal(jax.random.fold_in(_gk, 1), (1250, 512), jnp.float32)
        _s = jax.random.randint(jax.random.fold_in(_gk, 2), (10000,), 0, 1250, jnp.int32)
        _d = jax.random.randint(jax.random.fold_in(_gk, 3), (10000,), 0, 1250, jnp.int32)
        _loop = jnp.arange(1250, dtype=jnp.int32)
        src = jnp.concatenate([_s, _d, _loop])
        dst = jnp.concatenate([_d, _s, _loop])
        _o = jnp.argsort(dst, stable=True)
        src = src[_o]
        dst = dst[_o]
        edge_weight = jax.random.uniform(jax.random.fold_in(_gk, 13), (21250,), jnp.float32, 0.0, 0.999994)
        node_vec1 = jax.random.uniform(jax.random.fold_in(_gk, 14), (1250, 1), jnp.float32, 0.0, 0.999957)
        return (x, src, dst, edge_weight, node_vec1)
    x, src, dst, edge_weight, node_vec1 = _rec_inputs()

    def _L0_gnn_setup():
        import jax, jax.numpy as jnp
        import numpy as np
        N_NODES = 40962
        LATENT_DIM = 512
        N_EDGES = 81924
        NUM_BLOCKS = 4
        NUM_HEADS = 4
        NUM_FREQ = 32
        BASE_PERIOD = 16
        NOISE_EMB_DIM = 16
        EPS = 1e-05

        def _cond_layer_norm(x, cond, sw, sb, bw, bb):
            mu = jnp.mean(x, axis=-1, keepdims=True)
            var = jnp.var(x, axis=-1, keepdims=True)
            xn = (x - mu) * jax.lax.rsqrt(var + EPS)
            scale = cond @ sw + sb
            bias = cond @ bw + bb
            return xn * (1.0 + scale) + bias

        def _sparse_attention(x, src, dst, wq, bq, wk, bk, wv, bv, wo, bo):
            N, D = x.shape
            H, Dh = (NUM_HEADS, D // NUM_HEADS)
            q = (x @ wq + bq).reshape(N, H, Dh) * Dh ** (-0.5)
            k = (x @ wk + bk).reshape(N, H, Dh)
            v = (x @ wv + bv).reshape(N, H, Dh)
            scores = jnp.einsum('ehd,ehd->eh', q[src], k[dst])
            smax = jax.ops.segment_max(scores, src, num_segments=N)
            ex = jnp.exp(scores - smax[src])
            denom = jax.ops.segment_sum(ex, src, num_segments=N)
            attn = ex / denom[src]
            out = jax.ops.segment_sum(attn[:, :, None] * v[dst], src, num_segments=N)
            return out.reshape(N, D) @ wo + bo

        def _forward(x, edge_index, noise_levels, f_w1, f_b1, f_w2, f_b2, s1_w, s1_b, b1_w, b1_b, wq, bq, wk, bk, wv, bv, wo, bo, s2_w, s2_b, b2_w, b2_b, m_w1, m_b1, m_w2, m_b2):
            src, dst = (edge_index[0], edge_index[1])
            freqs = jnp.arange(1, NUM_FREQ + 1, dtype=x.dtype) * (2.0 * np.pi / BASE_PERIOD)
            ph = noise_levels * freqs
            emb = jnp.concatenate([jnp.sin(ph), jnp.cos(ph)], axis=-1)
            cond = jax.nn.silu(emb @ f_w1 + f_b1) @ f_w2 + f_b2
            for i in range(NUM_BLOCKS):
                y = _cond_layer_norm(x, cond, s1_w[i], s1_b[i], b1_w[i], b1_b[i])
                y = _sparse_attention(y, src, dst, wq[i], bq[i], wk[i], bk[i], wv[i], bv[i], wo[i], bo[i])
                x = x + y
                y = _cond_layer_norm(x, cond, s2_w[i], s2_b[i], b2_w[i], b2_b[i])
                y = jax.nn.relu(y @ m_w1[i] + m_b1[i]) @ m_w2[i] + m_b2[i]
                x = x + y
            return x
        key = jax.random.key(seed)
        ks = jax.random.split(key, 20)

        def w(k, shape, s=0.02):
            return jax.random.normal(k, shape, dtype=jnp.float32) * s
        D, B, C = (LATENT_DIM, NUM_BLOCKS, NOISE_EMB_DIM)
        z = lambda *s: jnp.zeros(s, jnp.float32)
        return {'latent_mesh_nodes': jax.random.normal(ks[0], (N_NODES, D), dtype=jnp.float32), 'edge_index': jax.random.randint(ks[1], (2, N_EDGES), 0, N_NODES, dtype=jnp.int32), 'noise_levels': jax.random.uniform(ks[2], (N_NODES, 1), dtype=jnp.float32), 'f_w1': w(ks[3], (2 * NUM_FREQ, C)), 'f_b1': z(C), 'f_w2': w(ks[4], (C, C)), 'f_b2': z(C), 's1_w': w(ks[5], (B, C, D)), 's1_b': z(B, D), 'b1_w': w(ks[6], (B, C, D)), 'b1_b': z(B, D), 'wq': w(ks[7], (B, D, D)), 'bq': z(B, D), 'wk': w(ks[8], (B, D, D)), 'bk': z(B, D), 'wv': w(ks[9], (B, D, D)), 'bv': z(B, D), 'wo': w(ks[10], (B, D, D)), 'bo': z(B, D), 's2_w': w(ks[11], (B, C, D)), 's2_b': z(B, D), 'b2_w': w(ks[12], (B, C, D)), 'b2_b': z(B, D), 'm_w1': w(ks[13], (B, D, D)), 'm_b1': z(B, D), 'm_w2': w(ks[14], (B, D, D)), 'm_b2': z(B, D)}
    _L0_gnn_all = _L0_gnn_setup()
    _L0_gnn_in = {k: v for k, v in _L0_gnn_all.items() if k in ('f_w1', 'f_b1', 'f_w2', 'f_b2', 's1_w', 's1_b', 'b1_w', 'b1_b', 'wq', 'bq', 'wk', 'bk', 'wv', 'bv', 'wo', 'bo', 's2_w', 's2_b', 'b2_w', 'b2_b', 'm_w1', 'm_b1', 'm_w2', 'm_b2')}
    del _L0_gnn_all

    def _L1_gnn_setup():
        import jax, jax.numpy as jnp
        import numpy as np
        N_NODES = 2500
        N_EDGES = 20000
        N_IN = 512
        N_OUT = 512
        key = jax.random.key(seed)
        k1, k2, k3, k4, k5 = jax.random.split(key, 5)
        x = jax.random.normal(k1, (N_NODES, N_IN), dtype=jnp.float32)
        vals = jax.random.uniform(k2, (N_EDGES,), dtype=jnp.float32)
        bound = 1.0 / np.sqrt(N_IN)
        weight = jax.random.uniform(k3, (N_OUT, N_IN), minval=-bound, maxval=bound, dtype=jnp.float32)
        row = jax.random.randint(k4, (N_EDGES,), 0, N_NODES, dtype=jnp.int32)
        col = jax.random.randint(k5, (N_EDGES,), 0, N_NODES, dtype=jnp.int32)
        return {'x': x, 'vals': vals, 'weight': weight, 'row': row, 'col': col}
    _L1_gnn_all = _L1_gnn_setup()
    _L1_gnn_in = {k: v for k, v in _L1_gnn_all.items() if k in ('weight',)}
    del _L1_gnn_all
    return {'x': x, 'src': src, 'dst': dst, 'edge_weight': edge_weight, 'node_vec1': node_vec1, 'L0_gnn_f_w1': _L0_gnn_in['f_w1'], 'L0_gnn_f_b1': _L0_gnn_in['f_b1'], 'L0_gnn_f_w2': _L0_gnn_in['f_w2'], 'L0_gnn_f_b2': _L0_gnn_in['f_b2'], 'L0_gnn_s1_w': _L0_gnn_in['s1_w'], 'L0_gnn_s1_b': _L0_gnn_in['s1_b'], 'L0_gnn_b1_w': _L0_gnn_in['b1_w'], 'L0_gnn_b1_b': _L0_gnn_in['b1_b'], 'L0_gnn_wq': _L0_gnn_in['wq'], 'L0_gnn_bq': _L0_gnn_in['bq'], 'L0_gnn_wk': _L0_gnn_in['wk'], 'L0_gnn_bk': _L0_gnn_in['bk'], 'L0_gnn_wv': _L0_gnn_in['wv'], 'L0_gnn_bv': _L0_gnn_in['bv'], 'L0_gnn_wo': _L0_gnn_in['wo'], 'L0_gnn_bo': _L0_gnn_in['bo'], 'L0_gnn_s2_w': _L0_gnn_in['s2_w'], 'L0_gnn_s2_b': _L0_gnn_in['s2_b'], 'L0_gnn_b2_w': _L0_gnn_in['b2_w'], 'L0_gnn_b2_b': _L0_gnn_in['b2_b'], 'L0_gnn_m_w1': _L0_gnn_in['m_w1'], 'L0_gnn_m_b1': _L0_gnn_in['m_b1'], 'L0_gnn_m_w2': _L0_gnn_in['m_w2'], 'L0_gnn_m_b2': _L0_gnn_in['m_b2'], 'L1_gnn_weight': _L1_gnn_in['weight']}

def reference(x, src, dst, edge_weight, node_vec1, L0_gnn_f_w1, L0_gnn_f_b1, L0_gnn_f_w2, L0_gnn_f_b2, L0_gnn_s1_w, L0_gnn_s1_b, L0_gnn_b1_w, L0_gnn_b1_b, L0_gnn_wq, L0_gnn_bq, L0_gnn_wk, L0_gnn_bk, L0_gnn_wv, L0_gnn_bv, L0_gnn_wo, L0_gnn_bo, L0_gnn_s2_w, L0_gnn_s2_b, L0_gnn_b2_w, L0_gnn_b2_b, L0_gnn_m_w1, L0_gnn_m_b1, L0_gnn_m_w2, L0_gnn_m_b2, L1_gnn_weight):
    import jax
    import jax.numpy as jnp

    def _L0_gnn_ref(latent_mesh_nodes, edge_index, noise_levels, f_w1, f_b1, f_w2, f_b2, s1_w, s1_b, b1_w, b1_b, wq, bq, wk, bk, wv, bv, wo, bo, s2_w, s2_b, b2_w, b2_b, m_w1, m_b1, m_w2, m_b2):
        import jax, jax.numpy as jnp
        import numpy as np
        N_NODES = 40962
        LATENT_DIM = 512
        N_EDGES = 81924
        NUM_BLOCKS = 4
        NUM_HEADS = 4
        NUM_FREQ = 32
        BASE_PERIOD = 16
        NOISE_EMB_DIM = 16
        EPS = 1e-05

        def _cond_layer_norm(x, cond, sw, sb, bw, bb):
            mu = jnp.mean(x, axis=-1, keepdims=True)
            var = jnp.var(x, axis=-1, keepdims=True)
            xn = (x - mu) * jax.lax.rsqrt(var + EPS)
            scale = cond @ sw + sb
            bias = cond @ bw + bb
            return xn * (1.0 + scale) + bias

        def _sparse_attention(x, src, dst, wq, bq, wk, bk, wv, bv, wo, bo):
            N, D = x.shape
            H, Dh = (NUM_HEADS, D // NUM_HEADS)
            q = (x @ wq + bq).reshape(N, H, Dh) * Dh ** (-0.5)
            k = (x @ wk + bk).reshape(N, H, Dh)
            v = (x @ wv + bv).reshape(N, H, Dh)
            scores = jnp.einsum('ehd,ehd->eh', q[src], k[dst])
            smax = jax.ops.segment_max(scores, src, num_segments=N)
            ex = jnp.exp(scores - smax[src])
            denom = jax.ops.segment_sum(ex, src, num_segments=N)
            attn = ex / denom[src]
            out = jax.ops.segment_sum(attn[:, :, None] * v[dst], src, num_segments=N)
            return out.reshape(N, D) @ wo + bo

        def _forward(x, edge_index, noise_levels, f_w1, f_b1, f_w2, f_b2, s1_w, s1_b, b1_w, b1_b, wq, bq, wk, bk, wv, bv, wo, bo, s2_w, s2_b, b2_w, b2_b, m_w1, m_b1, m_w2, m_b2):
            src, dst = (edge_index[0], edge_index[1])
            freqs = jnp.arange(1, NUM_FREQ + 1, dtype=x.dtype) * (2.0 * np.pi / BASE_PERIOD)
            ph = noise_levels * freqs
            emb = jnp.concatenate([jnp.sin(ph), jnp.cos(ph)], axis=-1)
            cond = jax.nn.silu(emb @ f_w1 + f_b1) @ f_w2 + f_b2
            for i in range(NUM_BLOCKS):
                y = _cond_layer_norm(x, cond, s1_w[i], s1_b[i], b1_w[i], b1_b[i])
                y = _sparse_attention(y, src, dst, wq[i], bq[i], wk[i], bk[i], wv[i], bv[i], wo[i], bo[i])
                x = x + y
                y = _cond_layer_norm(x, cond, s2_w[i], s2_b[i], b2_w[i], b2_b[i])
                y = jax.nn.relu(y @ m_w1[i] + m_b1[i]) @ m_w2[i] + m_b2[i]
                x = x + y
            return x
        return _forward(latent_mesh_nodes, edge_index, noise_levels, f_w1, f_b1, f_w2, f_b2, s1_w, s1_b, b1_w, b1_b, wq, bq, wk, bk, wv, bv, wo, bo, s2_w, s2_b, b2_w, b2_b, m_w1, m_b1, m_w2, m_b2)

    def _L1_gnn_ref(x, vals, weight, row, col):
        import jax, jax.numpy as jnp
        import numpy as np
        N_NODES = 2500
        N_EDGES = 20000
        N_IN = 512
        N_OUT = 512
        n = x.shape[0]
        msgs = x[col] * vals[:, None]
        agg = jax.ops.segment_sum(msgs, row, num_segments=n)
        return jnp.einsum('nd,od->no', agg, weight)
    edge_index = jnp.stack([src, dst])
    x = _layernorm(x + _L0_gnn_ref(x, edge_index, node_vec1, L0_gnn_f_w1, L0_gnn_f_b1, L0_gnn_f_w2, L0_gnn_f_b2, L0_gnn_s1_w, L0_gnn_s1_b, L0_gnn_b1_w, L0_gnn_b1_b, L0_gnn_wq, L0_gnn_bq, L0_gnn_wk, L0_gnn_bk, L0_gnn_wv, L0_gnn_bv, L0_gnn_wo, L0_gnn_bo, L0_gnn_s2_w, L0_gnn_s2_b, L0_gnn_b2_w, L0_gnn_b2_b, L0_gnn_m_w1, L0_gnn_m_b1, L0_gnn_m_w2, L0_gnn_m_b2), axis=-1)
    x = _layernorm(x + _L1_gnn_ref(x, edge_weight, L1_gnn_weight, src, dst), axis=-1)
    return x

_drawn_inputs = setup_inputs


def setup_inputs(seed=0):
    import zlib

    import numpy as np

    out = dict(_drawn_inputs(seed))
    spreads = {'L0_gnn_f_b1': (0.0, 0.8),
     'L0_gnn_f_b2': (0.0, 0.8),
     'L0_gnn_s1_b': (0.0, 0.689),
     'L0_gnn_b1_b': (0.0, 0.1),
     'L0_gnn_bq': (0.0, 0.8),
     'L0_gnn_bk': (0.0, 0.8),
     'L0_gnn_bv': (0.0, 0.1),
     'L0_gnn_bo': (0.0, 0.1),
     'L0_gnn_s2_b': (0.0, 0.581),
     'L0_gnn_b2_b': (0.0, 0.276),
     'L0_gnn_m_b1': (0.0, 0.1),
     'L0_gnn_m_b2': (0.0, 0.1)}
    factors = {'node_vec1': 8.0,
     'L0_gnn_f_w1': 8.0,
     'L0_gnn_f_w2': 8.0,
     'L0_gnn_s1_w': 8.0,
     'L0_gnn_b1_w': 8.0,
     'L0_gnn_wq': 6.188,
     'L0_gnn_wk': 5.925,
     'L0_gnn_s2_w': 8.0,
     'L0_gnn_b2_w': 8.0}
    for name, (base, spread) in spreads.items():
        noise = np.random.default_rng([zlib.crc32(name.encode()), seed]).standard_normal(out[name].shape)
        drawn = base * np.exp(spread * noise) if base else spread * noise
        out[name] = jnp.asarray(drawn.astype(out[name].dtype))
    for name, factor in factors.items():
        out[name] = (out[name] * factor).astype(out[name].dtype)
    return out
```

```python
from contextlib import ExitStack

import concourse.bass as bass
from concourse import mybir

ALU = mybir.AluOpType
ACT = mybir.ActivationFunctionType
AX = mybir.AxisListType
F32 = mybir.dt.float32
F32R = mybir.dt.float32r
BF16 = mybir.dt.bfloat16
F16 = mybir.dt.float16
I32 = mybir.dt.int32

P = 128
N = 1250
NT = -(-N // P)
NP = NT * P
LAST = N - (NT - 1) * P
D = 512
KT = D // P
H = 4
DH = D // H
LAYERS = 4
C16 = 16
FREQS = 32
EPS = 1e-5
SCALE = float(DH) ** -0.5
ABSENT = -1e30
E = 21250
GK = 3
GE = GK * P
NG = -(-E // GE)
WIN = 32
CHUNK_G = 7
NCH = NG // CHUNK_G
UNROLL_G = 2 * CHUNK_G
ET = NG * GK
FULL_G = E // GE
TAIL_E = E - FULL_G * GE
GROUPS = NT // 2
PAIR = 2 * P
KINDS = 7
SLOTS = 6
SROWS = C16 + 1
STACK = SLOTS * SROWS
BIAS_ROWS = 3 * LAYERS * KT
BIG = 3.0e38
COND_PART = (0, 0, 0, 1, 1, 2)
WEIGHT_PART = (0, 1, 2, 0, 1, 0)

START = 1

TWO_PI = 6.283185307179586
TURN = (6.28125, 2029.0 / 2 ** 20, TWO_PI - 6.28125 - 2029.0 / 2 ** 20)
MAGIC = 1.5 * 2 ** 23
PI_IN = 3.1415925
WT_ROUNDS = ((0, 4), (4, 8), (8, NT))

ROUNDS = (
    [(0, d) for d in (0, 1, 2, 3)],
    [(0, d) for d in (4, 5, 6, 7)],
    [(0, 8), (0, 9), (1, 8), (1, 9)],
    [(1, d) for d in (0, 1, 2, 3)],
    [(1, d) for d in (4, 5, 6, 7)],
)
assert NT == 10 and NG % UNROLL_G == 0 and UNROLL_G % 2 == 0

PER = dict(
    cond_ready=2 * NT, stats_ready=2 * NT, rstd_ready=2 * NT, y_ready=2 * NT, y_turned=2 * NT,
    y_hi=2 * NT, y_split=2 * NT,
    qk_ready=H * GROUPS, qk_hi=H * GROUPS, qk_split=H * GROUPS,
    v_ready=H * GROUPS, v_hi=H * GROUPS, v_split=H * GROUPS,
    scores_ready=H * NT, masked=H * NT, exped=H * NT, recip_ready=H * NT, probs_ready=H * NT,
    turned=H * GROUPS * 5, pt_hi=H * GROUPS * 5, pt_split=H * GROUPS * 5,
    o_ready=H * GROUPS, o_hi=H * GROUPS, o_split=H * GROUPS,
    wo_ready=H * NT, x_added=H * NT,
    var_eps=2 * NT, h_ready=2 * GROUPS, h_relu=2 * GROUPS, h_hi=2 * GROUPS, h_split=2 * GROUPS,
    m2_ready=NT, x_mlp=NT,
    piece_hi=4 * H + 2 * KT, piece_split=4 * H + 2 * KT, pads_zero=3,
    chain=2 * 2 * NT + H * NT, bias_cur=1,
)


def build(nc, T, out):
    ctx = ExitStack()
    with ctx:
        def sb(name, shape, dt, c=ctx):
            return c.enter_context(nc.sbuf_tensor(name, shape, dt))

        def sem(name):
            return ctx.enter_context(nc.semaphore(name))

        w_dram = nc.dram_tensor("w_table", [NT, P, N], F32).ap()
        stack_dram = nc.dram_tensor("stacks", [STACK, KINDS, LAYERS, D], BF16).ap()

        ident = sb("ident", [P, P], F32)
        cstack = sb("cstack", [STACK, NP], BF16)
        stacks = sb("stacks_sb", [STACK, KINDS, D], BF16)
        bias_all = sb("bias_all", [P, 3, LAYERS, KT], F32)
        bias = sb("bias", [P, 3, KT], F32)
        half = sb("half", [P, 1], F32)
        bn = sb("bn", [P, 2, 6], F32)
        mv = sb("mv", [P, 4, 2], F32)
        rs = sb("rs", [P, 4], F32)
        nmax = sb("nmax", [P, 4], F32)
        rsum = sb("rsum", [P, 4], F32)
        rinv = sb("rinv", [P, 4], F32)
        rnorm = sb("rnorm", [P, 4], F32)
        f_w1 = sb("f_w1", [64, C16], F32)
        f_w2 = sb("f_w2", [33, 33], F32)
        f_b1 = sb("f_b1", [C16, 2], F32)
        fcol = sb("fcol", [64, 3], F32)
        fcol_i = sb("fcol_i", [64, 1], I32)
        bias_rows = sb("bias_rows", [BIAS_ROWS, P], F32)
        oT_hi = sb("oT_hi", [P, PAIR], F32R)
        oT_lo = sb("oT_lo", [P, PAIR], F32R)

        with ExitStack() as prep:
            raw17 = sb("raw17", [33, LAYERS * D], F32, prep)
            part17 = [sb(f"part17_{i}", [33, LAYERS * D], BF16, prep) for i in range(3)]
        with ExitStack() as fin:
            lw_hi = sb("lw_hi", [P, KT, D], F32R, fin)
            lw_lo = sb("lw_lo", [P, KT, D], F32R, fin)
        piece = sb("piece", [P, 2, D], F32)
        wqkv_hi = sb("wqkv_hi", [P, 3, KT, DH], F32R)
        wqkv_lo = sb("wqkv_lo", [P, 3, KT, DH], F32R)
        wo_hi = sb("wo_hi", [P, D], F32R)
        wo_lo = sb("wo_lo", [P, D], F32R)

        with ExitStack() as prep:
            with ExitStack() as late:
                cpart = [sb(f"cpart{i}", [33, NP], BF16, late) for i in range(3)]
            sin_a = sb("sin_a", [64, NP], F32, prep)
            sin_b = sb("sin_b", [64, NP], F32, prep)
            hcond = sb("hcond", [33, NP], F32, prep)
            cpart32 = sb("cpart32", [33, NP], F32, prep)
        x = sb("x", [P, NT, D], F32)

        with ExitStack() as fin:
            z_hi = sb("z_hi", [P, NT, D], F32R, fin)
            z_lo = sb("z_lo", [P, NT, D], F32R, fin)
        with ExitStack() as tables:
            CW = sb("CW", [P, 2, NT, N], F32, tables)
        L = sb("L", [P, NT, N], F32)
        yT_hi = sb("yT_hi", [P, KT, NP], F32R)
        yT_lo = sb("yT_lo", [P, KT, NP], F32R)
        with ExitStack() as mlp:
            hT_hi = sb("hT_hi", [P, 2, KT, PAIR], F32R, mlp)
            hT_lo = sb("hT_lo", [P, 2, KT, PAIR], F32R, mlp)
            h32 = sb("h32", [P, 2, 2, PAIR], F32, mlp)
            y2 = sb("y2", [P, 2, D], F32, mlp)
        with ExitStack() as fin:
            lw_raw = sb("lw_raw", [P, KT, D], F32, fin)
            x0 = sb("x0", [P, 2, D], F32, fin)
            res = sb("res", [P, 2, D], F32, fin)
        q_hi = sb("q_hi", [P, NP], F32R)
        q_lo = sb("q_lo", [P, NP], F32R)
        with ExitStack() as edges:
            eT = sb("eT", [P, 4, GK, NG], F32, edges)
            wres = sb("wres", [P, GK, NG], F32, edges)
            wpart = sb("wpart", [P, 3, NG, GK], BF16, edges)
            iota_h = sb("iota_h", [P, NP], F16, edges)
            grow = sb("grow", [1, 2, NG], F32, edges)
            grow_i = sb("grow_i", [1, NG + 1], I32, edges)
            viol = sb("viol", [1, 1], F32, edges)
            with ExitStack() as load:
                iota_i = sb("iota_i", [P, NP], I32, load)
                src_i = sb("src_i", [NG, GE], I32, load)
                dst_i = sb("dst_i", [NG, GE], I32, load)
                ef = sb("ef", [NG, 4, GE], F32, load)
                gcol = sb("gcol", [NG, 2], F32, load)
            with ExitStack() as full:
                oh_src = sb("oh_src", [P, P], BF16, full)
                oh_dst = sb("oh_dst", [P, 4, N], BF16, full)
            win = sb("win", [P, 2, CHUNK_G * GK, 4, WIN], BF16, edges)
            onehot = sb("onehot", [P, 2, GK, NP], BF16, edges)
        with ExitStack() as tables:
            lnt = sb("lnt", [P, 2, N], F32, tables)
            absent = sb("absent", [P, 2, N], F32, tables)
        k_hi = sb("k_hi", [P, NP], F32R)
        k_lo = sb("k_lo", [P, NP], F32R)
        v_hi = sb("v_hi", [P, NT, DH], F32R)
        v_lo = sb("v_lo", [P, NT, DH], F32R)
        with ExitStack() as mlp:
            mw_hi = sb("mw_hi", [P, 2, KT, D], F32R, mlp)
            mw_lo = sb("mw_lo", [P, 2, KT, D], F32R, mlp)
        with ExitStack() as ln1:
            y1 = sb("y1", [P, 2, D], F32, ln1)
        with ExitStack() as fin:
            WT_hi = sb("WT_hi", [P, 2, NT, P], F32R, fin)
            WT_lo = sb("WT_lo", [P, 2, NT, P], F32R, fin)
        PT_hi = sb("PT_hi", [P, NT, PAIR], F32R)
        PT_lo = sb("PT_lo", [P, NT, PAIR], F32R)
        prob = sb("prob", [P, 3, NP], F32)

        ps = ctx.enter_context(nc.psum_tensor("ps", [P, 8 * 512], F32))

        def bank(b, lo=0, hi=512):
            return ps[:, b * 512 + lo:b * 512 + hi]

        S = {name: sem(name) for name in PER}
        piece_in = [sem(f"piece_in{i}") for i in range(2)]
        stacks_in = sem("stacks_in")

        noise_in, f_in, bias_in, x_in, edge_in = (sem(n) for n in ("noise_in", "f_in", "bias_in", "x_in", "edge_in"))
        pre_set, kind_in, kind_free, kind_parts, kind_out = (sem(n) for n in ("pre_set", "kind_in", "kind_free", "kind_parts", "kind_out"))
        kchain, dchain, sin_ready, emb_ready, hraw, hexp, hsilu = (sem(n) for n in ("kchain", "dchain", "sin_ready", "emb_ready", "hraw", "hexp", "hsilu"))
        cond_raw, cond_hi, cond_parts, cstack_in, iota_set = (sem(n) for n in ("cond_raw", "cond_hi", "cond_parts", "cstack_in", "iota_set"))
        table_zero, edges_ready, edges_turned, eplan = (sem(n) for n in ("table_zero", "edges_ready", "edges_turned", "eplan"))
        e_win, e_parts, e_onehot, e_sum, e_added, e_chain = (sem(n) for n in ("e_win", "e_parts", "e_onehot", "e_sum", "e_added", "e_chain"))
        g_chain, g_onehot, g_sum, g_added = (sem(n) for n in ("g_chain", "g_onehot", "g_sum", "g_added"))
        tables_done, w_stored, mask_in, mask_ln, mask_done = (sem(n) for n in ("tables_done", "w_stored", "mask_in", "mask_ln", "mask_done"))
        x0_in = [sem(f"x0_in{i}") for i in range(2)]
        lw_in, lw_turned, lw_hi_done, lw_split = (sem(n) for n in ("lw_in", "lw_turned", "lw_hi_done", "lw_split"))
        fchain, fstats, frstd, x1_ready, x1_turned, x1_hi, x1_split = (sem(n) for n in ("fchain", "fstats", "frstd", "x1_ready", "x1_turned", "x1_hi", "x1_split"))
        fvar = sem("fvar")
        pool_passed, dve_passed = sem("pool_passed"), sem("dve_passed")
        z_ready, z_hi_done, z_split, pad_zero = (sem(n) for n in ("z_ready", "z_hi_done", "z_split", "pad_zero"))
        wt_in = [sem(f"wt_in{i}") for i in range(3)]
        wt_turned, wt_hi_done, wt_split, agg_ready, agg_added, res_ready = (sem(n) for n in ("wt_turned", "wt_hi_done", "wt_split", "agg_ready", "agg_added", "res_ready"))
        stored = [sem(f"stored{i}") for i in range(2)]

        counted = [*S.values(), e_sum, e_chain, g_chain]

        def nt(t):
            return slice(t * P, (t + 1) * P)

        def pair(c):
            return slice(c * PAIR, (c + 1) * PAIR)

        NCHUNKS = ((0, 512), (512, 1024), (1024, NP))

        def round_view(PT, n, r):
            b = bank(5 + n % 2)
            if r == 2:
                return (PT[:, 8:10, :].rearrange("p d (j c) -> p j d c", j=2),
                        b.rearrange("p (j d c) -> p j d c", j=2, d=2))
            j, d = ROUNDS[r][0]
            return PT[:, d:d + 4, j * P:(j + 1) * P], b.rearrange("p (d c) -> p d c", d=4)

        def store(sp, j):
            n = P if j < NT - 1 else LAST
            sp.wait_ge(res_ready, j + 1)
            sp.dma_start(out[j * P:j * P + n, :], res[0:n, j % 2, :]).then_inc(stored[j % 2], 16)

        block = ctx.enter_context(nc.Block())

        @block.sync
        def _(sp):
            for s in counted:
                sp.sem_inc(s, START)
            sp.wait_ge(pre_set, 1)
            sp.dma_start(sin_a[:, 0:N], T["node_vec1"].rearrange("n o -> o n").broadcast_to([64, N])).then_inc(noise_in, 16)
            sp.dma_start(f_w1[:], T["L0_gnn_f_w1"]).then_inc(f_in, 16)
            sp.dma_start(f_b1[:, 0:1], T["L0_gnn_f_b1"].rearrange("(c o) -> c o", o=1)).then_inc(f_in, 16)
            sp.wait_ge(pre_set, 2)
            sp.dma_start(f_w2[0:C16, 0:C16], T["L0_gnn_f_w2"]).then_inc(f_in, 16)
            sp.dma_start(f_w2[32:33, 0:C16], T["L0_gnn_f_b2"].rearrange("(o c) -> o c", o=1)).then_inc(f_in, 16)
            sp.wait_ge(pre_set, 4)
            rows = FULL_G * GE
            for dst, src in ((src_i[:], T["src"]), (dst_i[:], T["dst"]), (ef[:, 3, :], T["edge_weight"])):
                sp.dma_start(dst[0:FULL_G, :], src[0:rows].rearrange("(g e) -> g e", e=GE)).then_inc(edge_in, 16)
                sp.dma_start(dst[FULL_G:NG, 0:TAIL_E], src[rows:E].rearrange("(o e) -> o e", o=1)).then_inc(edge_in, 16)
            sp.dma_start(dst_i[FULL_G:NG, TAIL_E:GE],
                         T["dst"][E - (GE - TAIL_E):E].rearrange("(o e) -> o e", o=1)).then_inc(edge_in, 16)
            for i, name in enumerate(("L0_gnn_bq", "L0_gnn_bk", "L0_gnn_m_b1")):
                rows = slice(i * LAYERS * KT, (i + 1) * LAYERS * KT)
                sp.dma_start(bias_rows[rows, :], T[name].rearrange("l (t p) -> (l t) p", p=P)).then_inc(bias_in, 16)

            sp.wait_ge(cond_parts, 1)
            for i, part in enumerate(COND_PART):
                sp.dma_start(cstack[i * SROWS:i * SROWS + C16, :], cpart[part][0:C16, :]).then_inc(cstack_in, 16)
                sp.dma_start(cstack[i * SROWS + C16:(i + 1) * SROWS, :], cpart[part][32:33, :]).then_inc(cstack_in, 16)
            sp.wait_ge(pre_set, 5)
            sp.wait_ge(cstack_in, 16 * 2 * SLOTS)
            sp.dma_start(x[:, 0:NT - 1, :], T["x"][0:(NT - 1) * P, :].rearrange("(t p) d -> p t d", p=P)).then_inc(x_in, 16)
            sp.dma_start(x[0:LAST, NT - 1, :], T["x"][(NT - 1) * P:N, :]).then_inc(x_in, 16)

            sp.wait_ge(tables_done, 1)
            sp.dma_start(w_dram.rearrange("t p n -> p t n"), CW[:, 1]).then_inc(w_stored, 16)
            sp.wait_ge(w_stored, 16)
            sp.wait_ge(kind_out, 16 * 2 * SLOTS * KINDS)

            with sp.Fori(0, LAYERS) as l:
                sp.wait_ge(S["m2_ready"], START + l * NT)
                sp.dma_start(stacks[:], stack_dram[:, :, bass.ds(l, 1), :].rearrange("r k o d -> r k (o d)")).then_inc(stacks_in, 16)
                for n in range(PER["piece_split"]):
                    sp.wait_ge(S["piece_split"], START + l * PER["piece_split"] + max(n - 1, 0))
                    if n < 4 * H:
                        h, what = divmod(n, 4)
                        if what < 3:
                            w = T[("L0_gnn_wq", "L0_gnn_wk", "L0_gnn_wv")[what]]
                            src = w[bass.ds(l, 1), :, h * DH:(h + 1) * DH].rearrange("o (t p) n -> p (o t) n", p=P)
                            dst = piece[:, n % 2, :].rearrange("p (t n) -> p t n", t=KT)
                        else:
                            src = T["L0_gnn_wo"][bass.ds(l, 1), h * DH:(h + 1) * DH, :].rearrange("o p n -> p (o n)")
                            dst = piece[:, n % 2, :]
                    else:
                        which, t = divmod(n - 4 * H, KT)
                        src = T[("L0_gnn_m_w1", "L0_gnn_m_w2")[which]][bass.ds(l, 1), t * P:(t + 1) * P, :].rearrange("o p n -> p (o n)")
                        dst = piece[:, n % 2, :]
                    sp.dma_start(dst, src).then_inc(piece_in[n % 2], 16)

            sp.wait_ge(S["m2_ready"], START + LAYERS * NT)
            sp.dma_start(lw_raw[:], T["L1_gnn_weight"].rearrange("(t p) d -> p t d", p=P)).then_inc(lw_in, 16)

            def load_x0(t):
                n = P if t < NT - 1 else LAST
                if t >= 2:
                    sp.wait_ge(fstats, t - 1)
                sp.dma_start(x0[0:n, t % 2, :], T["x"][t * P:t * P + n, :]).then_inc(x0_in[t % 2], 16)

            for t in range(NT):
                load_x0(t)
            sp.wait_ge(pad_zero, 1)
            for j in range(NT):
                if j >= 3:
                    sp.wait_ge(wt_turned, 3 * (j - 2))
                sp.dma_start(prob[:, j % 3, 0:N], w_dram[j]).then_inc(wt_in[j % 3], 16)
                if j >= 3:
                    store(sp, j - 3)
            for j in range(NT - 3, NT):
                store(sp, j)
            for i in range(2):
                sp.wait_ge(stored[i], 16 * NT // 2)

        @block.gpsimd
        def _(pool):
            pool.memset(ident[:], 0.0).then_inc(iota_set, 1)
            pool.wait_ge(iota_set, 1)
            pool.iota(fcol_i[0:32, :], [[0, 1]], base=1, channel_multiplier=1).then_inc(iota_set, 1)
            pool.wait_ge(iota_set, 2)
            pool.iota(fcol_i[32:64, :], [[0, 1]], base=1, channel_multiplier=1).then_inc(iota_set, 1)
            pool.wait_ge(iota_set, 3)
            pool.iota(iota_i[:], [[1, NP]], base=0, channel_multiplier=0).then_inc(iota_set, 1)
            pool.affine_select(out=ident[:], in_=ident[:], pattern=[[-1, P]], compare_op=ALU.not_equal,
                               fill=1.0, base=0, channel_multiplier=1).then_inc(iota_set, 1)
            pool.memset(half[:], -0.5).then_inc(iota_set, 1)
            pool.memset(CW[:], 0.0).then_inc(table_zero, 1)

            pool.wait_ge(table_zero, 1)
            pool.wait_ge(eplan, 2)
            flag = pool.value_load(grow_i[0:1, NG:NG + 1], min_val=0, max_val=1)
            with pool.If(flag < 1):
                with pool.Fori(0, NCH // 2) as i:
                    for c in range(2):
                        pool.wait_ge(e_win, i * 2 + c + 1)
                        pool.wait_ge(bias_in, 48)
                        for part in range(3):
                            oh = win[:, c, :, 0, :].rearrange("p (g b) w -> p g b w", b=GK)
                            o = win[:, c, :, 1 + part, :].rearrange("p (g b) w -> p g b w", b=GK)
                            wp = wpart[:, part, bass.ds(i * UNROLL_G + c * CHUNK_G, CHUNK_G), :]
                            m = pool.tensor_tensor(o, oh, wp.unsqueeze(3).to_broadcast([P, CHUNK_G, GK, WIN]), ALU.mult)
                        m.then_inc(e_parts, 1)
                pool.wait_ge(e_parts, NCH)

            for k in range(KINDS):
                pool.wait_ge(kind_in, 16 * (2 * min(k + 1, 4) + max(k - 3, 0)))
                one = 1.0 if k in (0, 2) else 0.0
                pool.tensor_scalar(raw17[32:33, :], raw17[32:33, :], one, None, ALU.add).then_inc(kchain, 1)
                for i in range(2):
                    pool.wait_ge(kchain, 5 * k + 2 * i + 2)
                    pool.tensor_tensor(raw17[:], raw17[:], part17[i][:], ALU.subtract).then_inc(kchain, 1)
                if k + 1 < KINDS:
                    pool.wait_ge(kind_parts, k + 1)
                    pool.memset(raw17[:], 0.0).then_inc(kind_free, 1)

            pool.wait_ge(tables_done, 1)
            for t in range(NT):
                if t >= 2:
                    pool.wait_ge(mask_done, t - 1)
                pool.tensor_scalar(lnt[:, t % 2, :], CW[:, 0, t, :], 0.5, None, ALU.max).then_inc(mask_in, 1)
                pool.tensor_scalar(absent[:, t % 2, :], CW[:, 0, t, :], 0.0, ABSENT, ALU.is_equal, ALU.mult).then_inc(mask_in, 1)

            with pool.Fori(0, LAYERS) as l:
                def wait(name, n):
                    pool.wait_ge(S[name], START + l * PER[name] + n)

                def settled():
                    pool.sem_inc(pool_passed, 1)

                def rsqrt(n):
                    i = n % 4
                    wait("stats_ready", n + 1)
                    settled()
                    pool.tensor_scalar(rs[:, i:i + 1], mv[:, i, 1:2], EPS, None, ALU.add).then_inc(S["var_eps"], 1)
                    wait("var_eps", n + 1)
                    pool.tensor_tensor(rs[:, i:i + 1], rs[:, i:i + 1], half[:], ALU.pow).then_inc(S["rstd_ready"], 1)

                def split(n, hi, lo, shape=lambda ap: ap):
                    pool.wait_ge(piece_in[n % 2], l * 8 * PER["piece_split"] + 16 * (n // 2 + 1))
                    settled()
                    raw = shape(piece[:, n % 2, :])
                    pool.tensor_copy(hi, raw).then_inc(S["piece_hi"], 1)
                    wait("piece_hi", n + 1)
                    pool.tensor_tensor(lo, raw, hi.bitcast(F32), ALU.subtract).then_inc(S["piece_split"], 1)

                def split_qkv(h, what):
                    if h:
                        wait(("qk_ready", "qk_ready", "v_ready")[what], GROUPS * h)
                    split(4 * h + what, wqkv_hi[:, what], wqkv_lo[:, what],
                          lambda ap: ap.rearrange("p (t n) -> p t n", t=KT))

                def split_wo(h):
                    if h:
                        wait("wo_ready", NT * h)
                    split(4 * h + 3, wo_hi[:], wo_lo[:])

                def split_mlp(which, t):
                    split(4 * H + KT * which + t, mw_hi[:, which, t, :], mw_lo[:, which, t, :])

                def norm(i):
                    wait("recip_ready", i + 1)
                    settled()
                    buf, r = prob[:, i % 3, 0:N], rnorm[:, i % 4:i % 4 + 1]
                    pool.tensor_scalar(buf, buf, r, 1.0, ALU.mult, ALU.mult).then_inc(S["probs_ready"], 1)

                def h_split(c, half_):
                    n = 2 * c + half_
                    wait("h_relu", n + 1)
                    if c >= 2:
                        wait("m2_ready", 2 * (c - 1))
                    settled()
                    hi = hT_hi[:, c % 2, 2 * half_:2 * half_ + 2, :]
                    lo = hT_lo[:, c % 2, 2 * half_:2 * half_ + 2, :]
                    pool.tensor_copy(hi, h32[:, half_]).then_inc(S["h_hi"], 1)
                    wait("h_hi", n + 1)
                    pool.tensor_tensor(lo, h32[:, half_], hi.bitcast(F32), ALU.subtract).then_inc(S["h_split"], 1)

                wait("m2_ready", 0)
                settled()
                pool.tensor_copy(bias[:], bias_all[:, :, bass.ds(l, 1), :].rearrange("p k o t -> p k (o t)")).then_inc(S["bias_cur"], 1)
                rsqrt(0)
                for what in range(2):
                    split_qkv(0, what)
                rsqrt(1)
                split_qkv(0, 2)
                rsqrt(2)
                split_wo(0)
                for t in range(3, NT):
                    rsqrt(t)
                for b in range(3):
                    pool.memset(prob[:, b, N:NP], 0.0).then_inc(S["pads_zero"], 1)
                norm(0)
                norm(1)
                for h in range(H):
                    for g in range(GROUPS):
                        if g < GROUPS - 1:
                            norm(NT * h + 2 * g + 2)
                            norm(NT * h + 2 * g + 3)
                        if g < 3 and h < H - 1:
                            split_qkv(h + 1, g)
                    if h < H - 1:
                        norm(NT * (h + 1))
                        norm(NT * (h + 1) + 1)
                        split_wo(h + 1)
                rsqrt(NT)
                rsqrt(NT + 1)
                wait("o_ready", H * GROUPS)
                for t in range(KT):
                    split_mlp(0, t)
                for c in range(GROUPS):
                    if c < GROUPS - 1:
                        rsqrt(NT + 2 * c + 2)
                        rsqrt(NT + 2 * c + 3)
                    h_split(c, 0)
                    h_split(c, 1)
                    if c == 0:
                        for t in range(KT):
                            split_mlp(1, t)

            pool.wait_ge(S["m2_ready"], START + LAYERS * NT)
            pool.memset(prob[:, :, N:NP], 0.0).then_inc(pad_zero, 1)
            for n in range(2 * NT):
                i = n % 4
                pool.wait_ge(fstats, n + 1)
                pool.tensor_scalar(rs[:, i:i + 1], mv[:, i, 1:2], EPS, None, ALU.add).then_inc(fvar, 1)
                pool.wait_ge(fvar, n + 1)
                pool.tensor_tensor(rs[:, i:i + 1], rs[:, i:i + 1], half[:], ALU.pow).then_inc(frstd, 1)

        @block.scalar
        def _(act):
            names = (("L0_gnn_s1_w", "L0_gnn_s1_b"), ("L0_gnn_b1_w", "L0_gnn_b1_b"),
                     ("L0_gnn_s2_w", "L0_gnn_s2_b"), ("L0_gnn_b2_w", "L0_gnn_b2_b"),
                     (None, "L0_gnn_bv"), (None, "L0_gnn_bo"), (None, "L0_gnn_m_b2"))

            def kind_stack(k):
                w, b = names[k]
                act.wait_ge(kind_free, k + 1)
                if w:
                    act.dma_start(raw17[0:C16, :].rearrange("j (l d) -> j l d", l=LAYERS),
                                  T[w].rearrange("l j d -> j l d")).then_inc(kind_in, 16)
                act.dma_start(raw17[32:33, :], T[b].rearrange("(o l) d -> o (l d)", o=1)).then_inc(kind_in, 16)

            def kind_store(k):
                act.wait_ge(kind_parts, k + 1)
                for i, part in enumerate(WEIGHT_PART):
                    act.dma_start(stack_dram[i * SROWS:i * SROWS + C16, k].rearrange("j l d -> j (l d)"),
                                  part17[part][0:C16, :]).then_inc(kind_out, 16)
                    act.dma_start(stack_dram[i * SROWS + C16:(i + 1) * SROWS, k].rearrange("j l d -> j (l d)"),
                                  part17[part][32:33, :]).then_inc(kind_out, 16)

            def kind_split(k):
                n = 5 * k
                for i in range(3):
                    act.wait_ge(kchain, n + 2 * i + 1)
                    if i == 0 and k:
                        act.wait_ge(kind_out, 16 * 2 * SLOTS * k)
                    act.activation(part17[i][:], raw17[:], ACT.Copy).then_inc(kchain if i < 2 else kind_parts, 1)

            kind_stack(0)
            act.wait_ge(sin_ready, 1)
            act.activation(sin_a[:], sin_a[:], ACT.Sin).then_inc(emb_ready, 1)
            act.wait_ge(hraw, 1)
            act.wait_ge(hsilu, 1)
            act.activation(cpart32[0:C16, :], ps[0:C16, 0:NP], ACT.Exp, bias=f_b1[:, 1:2], scale=-1.0).then_inc(hexp, 1)
            act.wait_ge(cond_raw, 1)
            act.wait_ge(hsilu, 2)
            act.activation(cpart[0][:], ps[0:33, 3 * 512:3 * 512 + NP], ACT.Copy).then_inc(cond_hi, 1)
            for k in range(KINDS):
                kind_split(k)
                kind_store(k)
                if k + 1 < KINDS:
                    kind_stack(k + 1)

            for t in range(NT):
                act.wait_ge(mask_in, 2 * t + 1)
                act.activation(lnt[:, t % 2, :], lnt[:, t % 2, :], ACT.Ln).then_inc(mask_ln, 1)
            act.wait_ge(w_stored, 16)

            with act.Fori(0, LAYERS) as l:
                def wait(name, n):
                    act.wait_ge(S[name], START + l * PER[name] + n)

                def y_hi_(n):
                    t = n % NT
                    wait("y_turned", n + 1)
                    act.activation(yT_hi[:, :, nt(t)], bank(5 + n % 2).rearrange("p (k c) -> p k c", k=KT),
                                   ACT.Copy).then_inc(S["y_hi"], 1)

                def qk_hi_(h, c):
                    wait("qk_ready", GROUPS * h + c + 1)
                    b = 2 + c % 3
                    act.activation(q_hi[:, pair(c)], bank(b, 0, PAIR), ACT.Identity, bias=bias[:, 0, h:h + 1])
                    act.activation(k_hi[:, pair(c)], bank(b, PAIR, 512), ACT.Identity, bias=bias[:, 1, h:h + 1])\
                       .then_inc(S["qk_hi"], 1)

                def v_hi_(h, c):
                    wait("v_ready", GROUPS * h + c + 1)
                    act.activation(v_hi[:, 2 * c:2 * c + 2, :], bank(7, 0, PAIR).rearrange("p (t c) -> p t c", t=2),
                                   ACT.Copy).then_inc(S["v_hi"], 1)

                def exp(i):
                    wait("masked", i + 1)
                    buf = prob[:, i % 3, 0:N]
                    act.activation(buf, buf, ACT.Exp, bias=nmax[:, i % 4:i % 4 + 1], scale=-1.0,
                                   accum_out=rsum[:, i % 4:i % 4 + 1]).then_inc(S["exped"], 1)

                def pt_hi_(h, g, r):
                    n = (GROUPS * h + g) * 5 + r
                    wait("turned", n + 1)
                    if r == 0:
                        wait("o_ready", GROUPS * h + g)
                    o, i = round_view(PT_hi, n, r)
                    act.activation(o, i, ACT.Copy).then_inc(S["pt_hi"], 1)

                def o_hi_(h, g):
                    wait("o_ready", GROUPS * h + g + 1)
                    wait("wo_ready", NT * h + 2 * g)
                    act.activation(oT_hi[:], bank(7, 0, PAIR), ACT.Copy).then_inc(S["o_hi"], 1)

                def relu(c, half_):
                    n = 2 * c + half_
                    wait("h_ready", n + 1)
                    if c:
                        wait("h_split", n - 1)
                    for i in range(2):
                        t = 2 * half_ + i
                        m = act.activation(h32[:, half_, i, :], bank(2 + half_, i * PAIR, (i + 1) * PAIR), ACT.Relu,
                                           bias=bias[:, 2, t:t + 1])
                    m.then_inc(S["h_relu"], 1)

                wait("m2_ready", 0)
                wait("bias_cur", 1)
                for t in range(NT):
                    if t:
                        y_hi_(t - 1)
                    if t % 2 and t >= 3:
                        qk_hi_(0, (t - 3) // 2)
                        v_hi_(0, (t - 3) // 2)
                y_hi_(NT - 1)
                qk_hi_(0, GROUPS - 1)
                v_hi_(0, GROUPS - 1)
                exp(0)
                exp(1)
                for h in range(H):
                    for g in range(GROUPS):
                        last, more = g == GROUPS - 1, h < H - 1
                        i = NT * h + 2 * g + 2
                        if g:
                            o_hi_(h, g - 1)
                        pt_hi_(h, g, 0)
                        if last and more:
                            qk_hi_(h + 1, 0)
                        pt_hi_(h, g, 1)
                        if last and more:
                            qk_hi_(h + 1, 1)
                        pt_hi_(h, g, 2)
                        if not last:
                            exp(i)
                        elif more:
                            qk_hi_(h + 1, 2)
                        pt_hi_(h, g, 3)
                        if last and more:
                            qk_hi_(h + 1, 3)
                        pt_hi_(h, g, 4)
                        if not last:
                            exp(i + 1)
                        elif more:
                            qk_hi_(h + 1, 4)
                    o_hi_(h, GROUPS - 1)
                    if h < H - 1:
                        exp(NT * (h + 1))
                        v_hi_(h + 1, 0)
                        exp(NT * (h + 1) + 1)
                        for c in range(1, GROUPS):
                            v_hi_(h + 1, c)
                wait("v_ready", H * GROUPS)
                y_hi_(NT)
                y_hi_(NT + 1)
                for c in range(GROUPS):
                    relu(c, 0)
                    if c < GROUPS - 1:
                        y_hi_(NT + 2 * c + 2)
                    relu(c, 1)
                    if c < GROUPS - 1:
                        y_hi_(NT + 2 * c + 3)

            for t in range(KT):
                act.wait_ge(lw_turned, t + 1)
                act.activation(lw_hi[:, t, :], bank(5 + t % 2), ACT.Copy).then_inc(lw_hi_done, 1)
            for t in range(NT):
                act.wait_ge(x1_turned, t + 1)
                act.activation(yT_hi[:, :, nt(t)], bank(5 + t % 2).rearrange("p (k c) -> p k c", k=KT), ACT.Copy)\
                   .then_inc(x1_hi, 1)
                if t:
                    act.wait_ge(z_ready, t)
                    act.activation(z_hi[:, t - 1, :], bank(3 + (t - 1) % 2), ACT.Copy).then_inc(z_hi_done, 1)
            act.wait_ge(z_ready, NT)
            act.activation(z_hi[:, NT - 1, :], bank(3 + (NT - 1) % 2), ACT.Copy).then_inc(z_hi_done, 1)
            for j in range(NT):
                for r, (lo, hi) in enumerate(WT_ROUNDS):
                    n = 3 * j + r
                    act.wait_ge(wt_turned, n + 1)
                    if j >= 2:
                        act.wait_ge(agg_ready, j - 1)
                    act.activation(WT_hi[:, j % 2, lo:hi, :], bank(5 + n % 2, 0, (hi - lo) * P).rearrange("p (k c) -> p k c", c=P),
                                   ACT.Copy).then_inc(wt_hi_done, 1)

        @block.vector
        def _(dve):
            dve.memset(sin_a[:, N:NP], 0.0).then_inc(pre_set, 1)
            dve.memset(f_w2[:], 0.0).then_inc(dchain, 1)
            dve.memset(raw17[:], 0.0).then_inc(kind_free, 1)
            dve.wait_ge(dchain, 1)
            dve.memset(f_w2[32:33, 32:33], 1.0).then_inc(pre_set, 1)
            dve.memset(src_i[:], -1).then_inc(pre_set, 1)
            dve.memset(ef[:, 3, :], 0.0).then_inc(pre_set, 1)
            link_n = [1]

            def link(m):
                link_n[0] += 1
                m.then_inc(dchain, 1)
                dve.wait_ge(dchain, link_n[0])

            dve.memset(hcond[:], 0.0)
            link(dve.memset(fcol[0:32, 1:3], 0.0))
            dve.memset(hcond[32:33, :], 1.0)
            dve.memset(fcol[32:64, 1:2], 0.25)
            link(dve.memset(fcol[32:64, 2:3], TWO_PI / 4))
            dve.wait_ge(iota_set, 3)
            link(dve.tensor_scalar(fcol[:, 0:1], fcol_i[:], TWO_PI / 16.0, None, ALU.mult))
            dve.wait_ge(noise_in, 16)
            link(dve.tensor_scalar(sin_a[:], sin_a[:], fcol[:, 0:1], None, ALU.mult))
            link(dve.tensor_scalar(sin_b[:], sin_a[:], 1.0 / TWO_PI, None, ALU.mult))
            link(dve.tensor_scalar(sin_b[:], sin_b[:], fcol[:, 1:2], None, ALU.add))
            link(dve.tensor_scalar(sin_b[:], sin_b[:], MAGIC, None, ALU.add))
            link(dve.tensor_scalar(sin_b[:], sin_b[:], -MAGIC, None, ALU.add))
            for c in TURN:
                link(dve.scalar_tensor_tensor(out=sin_a[:], in0=sin_b[:], scalar=-c, in1=sin_a[:], op0=ALU.mult, op1=ALU.add))
            link(dve.tensor_scalar(sin_a[:], sin_a[:], fcol[:, 2:3], PI_IN, ALU.add, ALU.min))
            dve.tensor_scalar(sin_a[:], sin_a[:], -PI_IN, None, ALU.max).then_inc(sin_ready, 1)

            dve.wait_ge(edge_in, 16 * 7)
            dve.tensor_copy(ef[:, 0, :], src_i[:])
            link(dve.tensor_copy(ef[:, 2, :], dst_i[:]))
            link(dve.tensor_reduce(gcol[:, 0:1], ef[:, 2, :], AX.X, ALU.min))
            link(dve.tensor_scalar(gcol[:, 0:1], gcol[:, 0:1], float(N - WIN), None, ALU.min))
            link(dve.tensor_scalar(ef[:, 1, :], ef[:, 2, :], gcol[:, 0:1], None, ALU.subtract))
            dve.tensor_reduce(gcol[:, 1:2], ef[:, 1, :], AX.X, ALU.max).then_inc(edges_ready, 1)

            dve.wait_ge(f_in, 16 * 4)
            dve.tensor_scalar(f_b1[:, 1:2], f_b1[:, 0:1], -1.0, None, ALU.mult).then_inc(hsilu, 1)
            dve.wait_ge(hexp, 1)
            dve.tensor_scalar(sin_b[0:C16, :], ps[0:C16, 0:NP], f_b1[:, 0:1], None, ALU.add)
            link(dve.tensor_scalar(cpart32[0:C16, :], cpart32[0:C16, :], 1.0, None, ALU.add))
            link(dve.reciprocal(cpart32[0:C16, :], cpart32[0:C16, :]))
            dve.tensor_tensor(hcond[0:C16, :], sin_b[0:C16, :], cpart32[0:C16, :], ALU.mult).then_inc(hsilu, 1)
            dve.wait_ge(cond_hi, 1)
            link(dve.tensor_tensor(cpart32[:], ps[0:33, 3 * 512:3 * 512 + NP], cpart[0][:], ALU.subtract))
            link(dve.tensor_copy(cpart[1][:], cpart32[:]))
            link(dve.tensor_tensor(cpart32[:], cpart32[:], cpart[1][:], ALU.subtract))
            dve.tensor_copy(cpart[2][:], cpart32[:]).then_inc(cond_parts, 1)

            dve.wait_ge(cond_parts, 1)
            dve.memset(x[:, NT - 1, :], 0.0).then_inc(pre_set, 1)

            dve.wait_ge(iota_set, 4)
            link(dve.tensor_copy(iota_h[:], iota_i[:]))
            dve.wait_ge(edges_turned, 1)
            cols = GK * NG
            dve.tensor_copy(eT[:, 0:2].rearrange("p k b g -> p (k b g)"), bank(6, 0, 2 * cols))
            dve.tensor_copy(bias_all[:].rearrange("p k l t -> p (k l t)"), bank(7, 2 * cols, 2 * cols + BIAS_ROWS))
            dve.tensor_copy(grow[:].rearrange("o k g -> o (k g)"), ps[0:1, 6 * 512 + 2 * cols:6 * 512 + 2 * cols + 2 * NG])
            link(dve.tensor_copy(eT[:, 2:4].rearrange("p k b g -> p (k b g)"), bank(7, 0, 2 * cols)))
            weight = eT[:, 3]
            parts = [wpart[:, i].rearrange("p g b -> p b g") for i in range(3)]
            link(dve.tensor_copy(parts[0], weight))
            link(dve.tensor_tensor(wres[:], weight, parts[0], ALU.subtract))
            link(dve.tensor_copy(parts[1], wres[:]))
            link(dve.tensor_tensor(wres[:], wres[:], parts[1], ALU.subtract))
            dve.tensor_copy(parts[2], wres[:]).then_inc(eplan, 1)
            link(dve.tensor_reduce(viol[:], grow[:, 1, :], AX.X, ALU.max))
            link(dve.tensor_copy(grow_i[:, 0:NG], grow[:, 0, :]))
            dve.tensor_scalar(grow_i[:, NG:NG + 1], viol[:], float(WIN), None, ALU.is_ge).then_inc(eplan, 1)
            dve.wait_ge(eplan, 2)
            dve.wait_ge(table_zero, 1)

            flag = dve.value_load(grow_i[0:1, NG:NG + 1], min_val=0, max_val=1)
            with dve.If(flag < 1):
                with dve.Fori(0, NG // UNROLL_G) as i:
                    def window(c):
                        dve.wait_ge(e_sum, START + i * UNROLL_G)
                        off = eT[:, 1, :, bass.ds(i * UNROLL_G + c * CHUNK_G, CHUNK_G)].rearrange("p b g -> p g b")
                        dve.tensor_tensor(win[:, c, :, 0, :].rearrange("p (g b) w -> p g b w", b=GK),
                                          iota_h[:, 0:WIN].unsqueeze(1).unsqueeze(1).to_broadcast([P, CHUNK_G, GK, WIN]),
                                          off.unsqueeze(3).to_broadcast([P, CHUNK_G, GK, WIN]), ALU.is_equal)\
                           .then_inc(e_win, 1)

                    def sources(j):
                        if j >= 2:
                            dve.wait_ge(e_sum, START + i * UNROLL_G + j - 1)
                        for b in range(GK):
                            m = dve.tensor_scalar(onehot[:, j % 2, b, :], iota_h[:], eT[:, 0, b, bass.ds(i * UNROLL_G + j, 1)],
                                                  None, ALU.is_equal)
                        m.then_inc(e_onehot, 1)

                    def accumulate(j):
                        dve.wait_ge(e_sum, START + i * UNROLL_G + j + 1)
                        base = dve.value_load(grow_i[0:1, bass.ds(i * UNROLL_G + j, 1)], min_val=0, max_val=N - WIN)
                        sums = ps[:, (j % 2) * 3 * 512:(j % 2) * 3 * 512 + NT * 4 * WIN].rearrange("p (t k w) -> p k t w", k=4, w=WIN)
                        both = CW[:, :, :, bass.ds(base, WIN)]
                        only = CW[:, 1, :, bass.ds(base, WIN)]
                        at = i * 3 * UNROLL_G + 3 * j
                        dve.wait_ge(e_chain, START + at)
                        dve.tensor_tensor(both, both, sums[:, 0:2], ALU.add).then_inc(e_chain, 1)
                        dve.wait_ge(e_chain, START + at + 1)
                        dve.tensor_tensor(only, only, sums[:, 2], ALU.add).then_inc(e_chain, 1)
                        dve.wait_ge(e_chain, START + at + 2)
                        dve.tensor_tensor(only, only, sums[:, 3], ALU.add).then_inc(e_chain, 1)

                    window(0)
                    sources(0)
                    for j in range(UNROLL_G):
                        if j == CHUNK_G - 3:
                            window(1)
                        if j + 1 < UNROLL_G:
                            sources(j + 1)
                        accumulate(j)
                dve.wait_ge(e_chain, START + 3 * NG)
            with dve.Else():
                with dve.Fori(0, NT) as s:
                    with dve.Fori(0, NG) as g:
                        for b in range(GK):
                            step = s * NG * GK + g * GK + b
                            dve.wait_ge(g_chain, START + 3 * step)
                            dve.tensor_scalar(oh_src[:], iota_h[:, bass.ds(s * P, P)], eT[:, 0, b, bass.ds(g, 1)],
                                              None, ALU.is_equal)
                            dve.tensor_scalar(oh_dst[:, 0, :], iota_h[:, 0:N], eT[:, 2, b, bass.ds(g, 1)],
                                              None, ALU.is_equal).then_inc(g_chain, 1)
                            dve.wait_ge(g_chain, START + 3 * step + 1)
                            for part in range(3):
                                m = dve.tensor_tensor(oh_dst[:, 1 + part, :], oh_dst[:, 0, :],
                                                      wpart[:, part, bass.ds(g, 1), b].to_broadcast([P, N]), ALU.mult)
                            m.then_inc(g_onehot, 1)
                            dve.wait_ge(g_sum, step + 1)
                            for k in range(2):
                                dst = CW[:, k, bass.ds(s, 1), :].rearrange("p o n -> p (o n)")
                                dve.tensor_tensor(dst, dst, ps[:, k * 1536:k * 1536 + N], ALU.add).then_inc(g_chain, 1)
                dve.wait_ge(g_chain, START + 3 * NT * ET)
            dve.memset(viol[:], 0.0).then_inc(tables_done, 1)

            for t in range(NT):
                dve.wait_ge(mask_in, 2 * t + 2)
                dve.wait_ge(mask_ln, t + 1)
                dve.scalar_tensor_tensor(out=L[:, t, :], in0=lnt[:, t % 2, :], scalar=1.0 / SCALE,
                                         in1=absent[:, t % 2, :], op0=ALU.mult, op1=ALU.add).then_inc(mask_done, 1)
            dve.wait_ge(mask_done, NT)
            dve.wait_ge(x_in, 32)

            with dve.Fori(0, LAYERS) as l:
                chain = [0]

                def wait(name, n):
                    dve.wait_ge(S[name], START + l * PER[name] + n)

                def settled():
                    dve.sem_inc(dve_passed, 1)

                def link(m):
                    chain[0] += 1
                    m.then_inc(S["chain"], 1)
                    wait("chain", chain[0])

                def stats(n):
                    if n >= NT:
                        wait("x_added", (H - 1) * NT + n % NT + 1)
                    dve.bn_stats(bn[:, n % 2, :], x[:, n % NT, :]).then_inc(S["chain"], 1)
                    chain[0] += 1
                    wait("chain", chain[0])
                    settled()
                    dve.bn_aggr(mv[:, n % 4, :], bn[:, n % 2, :]).then_inc(S["stats_ready"], 1)

                def norm(n):
                    y = (y1 if n < NT else y2)[:, n % 2, :]
                    wait("cond_ready", n + 1)
                    if n % NT >= 2:
                        wait("y_turned", n - 1)
                    link(dve.scalar_tensor_tensor(out=y, in0=x[:, n % NT, :], scalar=mv[:, n % 4, 0:1], in1=bank(0),
                                                  op0=ALU.subtract, op1=ALU.mult))
                    wait("rstd_ready", n + 1)
                    dve.scalar_tensor_tensor(out=y, in0=y, scalar=rs[:, n % 4:n % 4 + 1], in1=bank(1),
                                             op0=ALU.mult, op1=ALU.add).then_inc(S["y_ready"], 1)

                def y_lo_(n):
                    wait("y_hi", n + 1)
                    dve.tensor_tensor(yT_lo[:, :, nt(n % NT)], bank(5 + n % 2).rearrange("p (k c) -> p k c", k=KT),
                                      yT_hi[:, :, nt(n % NT)].bitcast(F32), ALU.subtract).then_inc(S["y_split"], 1)

                def qk_lo_(h, c):
                    wait("qk_hi", GROUPS * h + c + 1)
                    b = 2 + c % 3
                    for i, (hi, lo) in enumerate(((q_hi, q_lo), (k_hi, k_lo))):
                        m = dve.scalar_tensor_tensor(out=lo[:, pair(c)], in0=bank(b, i * PAIR, (i + 1) * PAIR),
                                                     scalar=bias[:, i, h:h + 1], in1=hi[:, pair(c)].bitcast(F32),
                                                     op0=ALU.add, op1=ALU.subtract)
                    m.then_inc(S["qk_split"], 1)

                def v_lo_(h, c):
                    wait("v_hi", GROUPS * h + c + 1)
                    dve.tensor_tensor(v_lo[:, 2 * c:2 * c + 2, :], bank(7, 0, PAIR).rearrange("p (t c) -> p t c", t=2),
                                      v_hi[:, 2 * c:2 * c + 2, :].bitcast(F32), ALU.subtract).then_inc(S["v_split"], 1)

                def mask(i):
                    wait("scores_ready", i + 1)
                    if i >= 3:
                        g, j = divmod(i - 3, 2)
                        wait("turned", 5 * g + (5 if j else 3))
                    settled()
                    off = (i % 2) * N
                    dve.tensor_tensor_reduce(prob[:, i % 3, 0:N], ps[:, off:off + N], L[:, i % NT, :], -SCALE, BIG,
                                             ALU.add, ALU.min, nmax[:, i % 4:i % 4 + 1]).then_inc(S["masked"], 1)

                def recip(i):
                    r = slice(i % 4, i % 4 + 1)
                    wait("exped", i + 1)
                    link(dve.reciprocal(rinv[:, r], rsum[:, r]))
                    dve.scalar_tensor_tensor(out=rnorm[:, r], in0=nmax[:, r], scalar=-ABSENT * SCALE * 0.1, in1=rinv[:, r],
                                             op0=ALU.is_lt, op1=ALU.mult).then_inc(S["recip_ready"], 1)

                def pt_lo_(h, g, r):
                    n = (GROUPS * h + g) * 5 + r
                    wait("pt_hi", n + 1)
                    hi, i = round_view(PT_hi, n, r)
                    lo, _ = round_view(PT_lo, n, r)
                    dve.tensor_tensor(lo, i, hi.bitcast(F32), ALU.subtract).then_inc(S["pt_split"], 1)

                def o_lo_(h, g):
                    wait("o_hi", GROUPS * h + g + 1)
                    dve.tensor_tensor(oT_lo[:], bank(7, 0, PAIR), oT_hi[:].bitcast(F32), ALU.subtract).then_inc(S["o_split"], 1)

                def add_wo(h, t):
                    i = NT * h + t
                    wait("wo_ready", i + 1)
                    if h:
                        wait("x_added", i - NT + 1)
                    dve.tensor_tensor(x[:, t, :], bank(7), x[:, t, :], ALU.add).then_inc(S["x_added"], 1)

                def add_mlp(t):
                    wait("m2_ready", t + 1)
                    dve.tensor_tensor(x[:, t, :], bank(4 + 3 * (t % 2)), x[:, t, :], ALU.add).then_inc(S["x_mlp"], 1)

                wait("x_mlp", 0)
                wait("m2_ready", 0)
                stats(0)
                stats(1)
                wait("bias_cur", 1)
                for t in range(NT):
                    norm(t)
                    if t + 2 < NT:
                        stats(t + 2)
                    if t:
                        y_lo_(t - 1)
                    if t % 2 and t >= 3:
                        qk_lo_(0, (t - 3) // 2)
                        v_lo_(0, (t - 3) // 2)
                y_lo_(NT - 1)
                qk_lo_(0, GROUPS - 1)
                v_lo_(0, GROUPS - 1)
                mask(0)
                mask(1)
                recip(0)
                recip(1)
                for h in range(H):
                    for g in range(GROUPS):
                        last, more = g == GROUPS - 1, h < H - 1
                        i = NT * h + 2 * g + 2
                        if g:
                            o_lo_(h, g - 1)
                        pt_lo_(h, g, 0)
                        if last and more:
                            qk_lo_(h + 1, 0)
                        pt_lo_(h, g, 1)
                        if not last:
                            mask(i)
                        elif more:
                            qk_lo_(h + 1, 1)
                        if g:
                            add_wo(h, 2 * g - 2)
                        pt_lo_(h, g, 2)
                        if not last:
                            recip(i)
                        elif more:
                            qk_lo_(h + 1, 2)
                        pt_lo_(h, g, 3)
                        if not last:
                            mask(i + 1)
                        elif more:
                            qk_lo_(h + 1, 3)
                        if g:
                            add_wo(h, 2 * g - 1)
                        pt_lo_(h, g, 4)
                        if not last:
                            recip(i + 1)
                        elif more:
                            qk_lo_(h + 1, 4)
                    o_lo_(h, GROUPS - 1)
                    if h < H - 1:
                        mask(NT * (h + 1))
                    add_wo(h, NT - 2)
                    if h < H - 1:
                        v_lo_(h + 1, 0)
                        recip(NT * (h + 1))
                        mask(NT * (h + 1) + 1)
                    add_wo(h, NT - 1)
                    if h < H - 1:
                        for c in range(1, GROUPS):
                            v_lo_(h + 1, c)
                            if c == 1:
                                recip(NT * (h + 1) + 1)
                stats(NT)
                stats(NT + 1)
                norm(NT)
                stats(NT + 2)
                norm(NT + 1)
                stats(NT + 3)
                y_lo_(NT)
                y_lo_(NT + 1)
                for c in range(GROUPS):
                    if c < GROUPS - 1:
                        for n in (NT + 2 * c + 2, NT + 2 * c + 3):
                            norm(n)
                            if n + 2 < 2 * NT:
                                stats(n + 2)
                            y_lo_(n)
                    if c:
                        add_mlp(2 * c - 2)
                        add_mlp(2 * c - 1)
                add_mlp(NT - 2)
                add_mlp(NT - 1)

            fn = [0]

            def flink(m):
                fn[0] += 1
                m.then_inc(fchain, 1)
                dve.wait_ge(fchain, fn[0])

            def fstat(n):
                flink(dve.bn_stats(bn[:, n % 2, :], x[:, n % NT, :]))
                dve.bn_aggr(mv[:, n % 4, :], bn[:, n % 2, :]).then_inc(fstats, 1)

            def residual(t):
                dve.wait_ge(x0_in[t % 2], 16 * (t // 2 + 1))
                flink(dve.tensor_tensor(x[:, t, :], x[:, t, :], x0[:, t % 2, :], ALU.add))
                fstat(t)

            def norm_x1(t):
                dve.wait_ge(frstd, t + 1)
                dve.tensor_scalar(x[:, t, :], x[:, t, :], mv[:, t % 4, 0:1], rs[:, t % 4:t % 4 + 1], ALU.subtract, ALU.mult)\
                   .then_inc(x1_ready, 1)

            def z_lo_(t):
                dve.wait_ge(z_hi_done, t + 1)
                dve.tensor_tensor(z_lo[:, t, :], bank(3 + t % 2), z_hi[:, t, :].bitcast(F32), ALU.subtract).then_inc(z_split, 1)

            dve.wait_ge(S["x_mlp"], START + LAYERS * NT)
            for t in range(KT):
                dve.wait_ge(lw_hi_done, t + 1)
                dve.tensor_tensor(lw_lo[:, t, :], bank(5 + t % 2), lw_hi[:, t, :].bitcast(F32), ALU.subtract).then_inc(lw_split, 1)
            residual(0)
            residual(1)
            norm_x1(0)
            for t in range(NT):
                if t + 1 < NT:
                    norm_x1(t + 1)
                if t + 2 < NT:
                    residual(t + 2)
                dve.wait_ge(x1_hi, t + 1)
                dve.tensor_tensor(yT_lo[:, :, nt(t)], bank(5 + t % 2).rearrange("p (k c) -> p k c", k=KT),
                                  yT_hi[:, :, nt(t)].bitcast(F32), ALU.subtract).then_inc(x1_split, 1)
                if t:
                    z_lo_(t - 1)
            z_lo_(NT - 1)

            def result(j):
                dve.wait_ge(frstd, NT + j + 1)
                if j >= 2:
                    dve.wait_ge(stored[j % 2], 16 * (j // 2))
                n = NT + j
                dve.tensor_scalar(res[:, j % 2, :], x[:, j, :], mv[:, n % 4, 0:1], rs[:, n % 4:n % 4 + 1],
                                  ALU.subtract, ALU.mult).then_inc(res_ready, 1)

            def aggregated(j):
                dve.wait_ge(agg_ready, j + 1)
                m = dve.tensor_tensor(x[:, j, :], bank(j % 2), x[:, j, :], ALU.add)
                m.then_inc(agg_added, 1)
                dve.wait_ge(agg_added, j + 1)
                fstat(NT + j)

            for j in range(NT):
                for r, (lo, hi) in enumerate(WT_ROUNDS):
                    n = 3 * j + r
                    dve.wait_ge(wt_hi_done, n + 1)
                    dve.tensor_tensor(WT_lo[:, j % 2, lo:hi, :], bank(5 + n % 2, 0, (hi - lo) * P).rearrange("p (k c) -> p k c", c=P),
                                      WT_hi[:, j % 2, lo:hi, :].bitcast(F32), ALU.subtract).then_inc(wt_split, 1)
                if j:
                    aggregated(j - 1)
                    result(j - 1)
            aggregated(NT - 1)
            result(NT - 1)

        @block.tensor
        def _(pe):
            def mm(o, a, b, start, stop):
                return pe.matmul(o, a, b, start=start, stop=stop)

            def mm3(o, a_hi, a_lo, b_hi, b_lo, start, stop):
                mm(o, a_hi, b_hi, start, False)
                mm(o, a_hi, b_lo, False, False)
                return mm(o, a_lo, b_hi, False, stop)

            pe.wait_ge(f_in, 16 * 4)
            pe.wait_ge(emb_ready, 1)
            for lo, hi in NCHUNKS:
                m = mm(ps[0:C16, lo:hi], f_w1[:], sin_a[:, lo:hi], True, True)
            m.then_inc(hraw, 1)
            pe.wait_ge(edges_ready, 1)
            pe.wait_ge(iota_set, 6)
            cols = GK * NG
            for kind in range(4):
                for b in range(GK):
                    at = (6 + kind // 2) * 512 + (kind % 2) * cols + b * NG
                    pe.transpose(ps[:, at:at + NG], ef[:, kind, b * P:(b + 1) * P], ident[0:NG, 0:NG])
            pe.wait_ge(bias_in, 48)
            pe.transpose(bank(7, 2 * cols, 2 * cols + BIAS_ROWS), bias_rows[:], ident[0:BIAS_ROWS, 0:BIAS_ROWS])
            for i in range(2):
                at = 6 * 512 + 2 * cols + i * NG
                m = pe.transpose(ps[0:1, at:at + NG], gcol[:, i:i + 1], ident[0:NG, 0:NG])
            m.then_inc(edges_turned, 1)
            pe.wait_ge(hsilu, 2)
            for lo, hi in NCHUNKS:
                m = mm(ps[0:33, 3 * 512 + lo:3 * 512 + hi], f_w2[:], hcond[:, lo:hi], True, True)
            m.then_inc(cond_raw, 1)

            pe.wait_ge(eplan, 2)
            pe.wait_ge(cond_parts, 1)
            flag = pe.value_load(grow_i[0:1, NG:NG + 1], min_val=0, max_val=1)
            with pe.If(flag < 1):
                with pe.Fori(0, NG // UNROLL_G) as i:
                    for j in range(UNROLL_G):
                        c, gl = divmod(j, CHUNK_G)
                        if gl == 0:
                            pe.wait_ge(e_parts, i * 2 + c + 1)
                        pe.wait_ge(e_onehot, i * UNROLL_G + j + 1)
                        pe.wait_ge(e_chain, START + i * 3 * UNROLL_G + 3 * max(j - 1, 0))
                        for s in range(NT):
                            for b in range(GK):
                                at = (j % 2) * 3 * 512 + s * 4 * WIN
                                m = mm(ps[:, at:at + 4 * WIN], onehot[:, j % 2, b, nt(s)],
                                       win[:, c, gl * GK + b].rearrange("p k w -> p (k w)"), b == 0, b == GK - 1)
                        m.then_inc(e_sum, 1)
            with pe.Else():
                with pe.Fori(0, NT) as s:
                    with pe.Fori(0, NG) as g:
                        for b in range(GK):
                            step = s * NG * GK + g * GK + b
                            pe.wait_ge(g_onehot, step + 1)
                            pe.wait_ge(g_chain, START + 3 * step)
                            for lo, hi in ((0, 512), (512, 1024), (1024, N)):
                                mm(ps[:, lo:hi], oh_src[:], oh_dst[:, 0, lo:hi], True, True)
                                for part in range(3):
                                    m = mm(ps[:, 1536 + lo:1536 + hi], oh_src[:], oh_dst[:, 1 + part, lo:hi],
                                           part == 0, part == 2)
                            m.then_inc(g_sum, 1)
            pe.wait_ge(cstack_in, 16 * 2 * SLOTS)
            pe.wait_ge(tables_done, 1)

            with pe.Fori(0, LAYERS) as l:
                m_last = [("x_mlp", 0)]

                def wait(name, n):
                    pe.wait_ge(S[name], START + l * PER[name] + n)

                def take_m(name, n):
                    wait(*m_last[0])
                    m_last[0] = (name, n)

                def cond(n):
                    if n % NT:
                        wait("y_ready", n)
                    for i in range(2):
                        m = mm(bank(i), cstack[:, nt(n % NT)], stacks[:, 2 * (n // NT) + i, :], True, True)
                    m.then_inc(S["cond_ready"], 1)

                def turn_y(n):
                    wait("y_ready", n + 1)
                    if n % NT < NT - 1:
                        cond(n + 1)
                    if n in (NT, NT + 1):
                        wait("pt_split", PER["pt_split"] - 1 + n - NT)
                    else:
                        wait("y_split", max(n - 1, 0))
                    y = y1 if n < NT else y2
                    for k in range(KT):
                        m = pe.transpose(bank(5 + n % 2, k * P, (k + 1) * P), y[:, n % 2, k * P:(k + 1) * P], ident[:])
                    m.then_inc(S["y_turned"], 1)

                def qk(h, c):
                    if c >= 3:
                        wait("qk_split", GROUPS * h + c - 2)
                    elif h:
                        wait("masked", NT * h)
                    else:
                        wait("h_relu", 0)
                        wait("x_mlp", 0)
                    if h == 0:
                        wait("y_split", 2 * c + 2)
                    wait("piece_split", 4 * h + 2)
                    for i in range(2):
                        o = bank(2 + c % 3, i * PAIR, (i + 1) * PAIR)
                        for k in range(KT):
                            m = mm3(o, wqkv_hi[:, i, k, :], wqkv_lo[:, i, k, :], yT_hi[:, k, pair(c)], yT_lo[:, k, pair(c)],
                                    k == 0, k == KT - 1)
                    m.then_inc(S["qk_ready"], 1)

                def values(h, c):
                    take_m("v_split", GROUPS * h + c + 1)
                    wait("piece_split", 4 * h + 3)
                    for j in range(2):
                        t = 2 * c + j
                        o = bank(7, j * P, (j + 1) * P)
                        mm(o, cstack[:, nt(t)], stacks[:, 4, h * DH:(h + 1) * DH], True, False)
                        for k in range(KT):
                            m = mm3(o, yT_hi[:, k, nt(t)], yT_lo[:, k, nt(t)], wqkv_hi[:, 2, k, :], wqkv_lo[:, 2, k, :],
                                    False, k == KT - 1)
                    m.then_inc(S["v_ready"], 1)

                def scores(i, chunks):
                    for b in chunks:
                        wait("masked", i if b == 2 else max(i - 1, 0))
                        lo, hi = max(b * 512, (i % 2) * N), min((b + 1) * 512, (i % 2 + 1) * N)
                        off = (i % 2) * N
                        m = mm3(ps[:, lo:hi], q_hi[:, nt(i % NT)], q_lo[:, nt(i % NT)], k_hi[:, lo - off:hi - off],
                                k_lo[:, lo - off:hi - off], True, True)
                    return m

                def scores_a(h, t, part):
                    i = NT * h + t
                    if part == 0:
                        scores(i, (0, 1) if t % 2 == 0 else (3, 4))
                    else:
                        scores(i, (2,)).then_inc(S["scores_ready"], 1)

                def turn(h, g, r):
                    n = (GROUPS * h + g) * 5 + r
                    if r in (0, 2):
                        wait("probs_ready", NT * h + 2 * g + (1 if r == 0 else 2))
                    if n < 2:
                        wait("y_split", NT - 1 + n)
                    else:
                        wait("pt_split", n - 1)
                    for at, (j, d) in enumerate(ROUNDS[r]):
                        m = pe.transpose(bank(5 + n % 2, at * P, (at + 1) * P), prob[:, (NT * h + 2 * g + j) % 3, d * P:(d + 1) * P],
                                         ident[:])
                    m.then_inc(S["turned"], 1)

                def out_heads(h, g):
                    take_m("o_split", GROUPS * h + g + 1)
                    wait("pt_split", (GROUPS * h + g + 1) * 5)
                    if g == 0:
                        wait("v_split", GROUPS * (h + 1))
                    for d in range(NT):
                        m = mm3(bank(7, 0, PAIR), v_hi[:, d, :], v_lo[:, d, :], PT_hi[:, d, :], PT_lo[:, d, :], d == 0, d == NT - 1)
                    m.then_inc(S["o_ready"], 1)

                def project(h, g, j):
                    t = 2 * g + j
                    take_m("x_added", NT * h + t + 1)
                    wait("o_split", GROUPS * h + g + 1)
                    wait("piece_split", 4 * h + 4)
                    cols = slice(j * P, (j + 1) * P)
                    if h == 0:
                        mm(bank(7), cstack[:, nt(t)], stacks[:, 5, :], True, False)
                    mm3(bank(7), oT_hi[:, cols], oT_lo[:, cols], wo_hi[:], wo_lo[:], h > 0, True).then_inc(S["wo_ready"], 1)

                def hidden(c, half_):
                    n = 2 * c + half_
                    if c:
                        wait("h_relu", n - 1)
                    wait("y_split", NT + 2 * c + 2)
                    wait("piece_split", 4 * H + KT)
                    for i in range(2):
                        t = 2 * half_ + i
                        for k in range(KT):
                            m = mm3(bank(2 + half_, i * PAIR, (i + 1) * PAIR), mw_hi[:, 0, k, nt(t)], mw_lo[:, 0, k, nt(t)],
                                    yT_hi[:, k, pair(c)], yT_lo[:, k, pair(c)], k == 0, k == KT - 1)
                    m.then_inc(S["h_ready"], 1)

                def mlp_out(t):
                    c, j = divmod(t, 2)
                    if j:
                        take_m("x_mlp", t + 1)
                    elif t:
                        wait("x_mlp", t - 1)
                    wait("h_split", 2 * c + 2)
                    wait("piece_split", 4 * H + 2 * KT)
                    o = bank(4 + 3 * j)
                    mm(o, cstack[:, nt(t)], stacks[:, 6, :], True, False)
                    for k in range(KT):
                        m = mm3(o, hT_hi[:, c % 2, k, nt(j)], hT_lo[:, c % 2, k, nt(j)], mw_hi[:, 1, k, :], mw_lo[:, 1, k, :],
                                False, k == KT - 1)
                    m.then_inc(S["m2_ready"], 1)

                pe.wait_ge(stacks_in, l * 16 + 16)
                cond(0)
                for t in range(NT):
                    turn_y(t)
                    if t % 2 and t >= 3:
                        qk(0, (t - 3) // 2)
                        values(0, (t - 3) // 2)
                qk(0, GROUPS - 1)
                values(0, GROUPS - 1)
                wait("qk_split", GROUPS)
                wait("pads_zero", 3)
                for t in range(2):
                    scores_a(0, t, 0)
                    scores_a(0, t, 1)
                for h in range(H):
                    for g in range(GROUPS):
                        last, more = g == GROUPS - 1, h < H - 1
                        t = 2 * g + 2
                        if g:
                            out_heads(h, g - 1)
                        turn(h, g, 0)
                        if not last:
                            scores_a(h, t, 0)
                        elif more:
                            qk(h + 1, 0)
                        turn(h, g, 1)
                        if not last:
                            scores_a(h, t, 1)
                        elif more:
                            qk(h + 1, 1)
                        if g:
                            project(h, g - 1, 0)
                        turn(h, g, 2)
                        if not last:
                            scores_a(h, t + 1, 0)
                        elif more:
                            qk(h + 1, 2)
                        turn(h, g, 3)
                        if not last:
                            scores_a(h, t + 1, 1)
                        elif more:
                            qk(h + 1, 3)
                        if g:
                            project(h, g - 1, 1)
                        turn(h, g, 4)
                        if last and more:
                            qk(h + 1, 4)
                    out_heads(h, GROUPS - 1)
                    if h < H - 1:
                        wait("qk_split", GROUPS * (h + 2))
                        scores_a(h + 1, 0, 0)
                        scores_a(h + 1, 0, 1)
                    project(h, GROUPS - 1, 0)
                    if h < H - 1:
                        values(h + 1, 0)
                        scores_a(h + 1, 1, 0)
                        scores_a(h + 1, 1, 1)
                    project(h, GROUPS - 1, 1)
                    if h < H - 1:
                        for c in range(1, GROUPS):
                            values(h + 1, c)
                wait("masked", H * NT)
                cond(NT)
                turn_y(NT)
                turn_y(NT + 1)
                for c in range(GROUPS):
                    hidden(c, 0)
                    if c < GROUPS - 1:
                        turn_y(NT + 2 * c + 2)
                    hidden(c, 1)
                    if c < GROUPS - 1:
                        turn_y(NT + 2 * c + 3)
                    if c:
                        mlp_out(2 * c - 2)
                        mlp_out(2 * c - 1)
                mlp_out(NT - 2)
                mlp_out(NT - 1)

            pe.wait_ge(lw_in, 16)
            pe.wait_ge(S["y_split"], START + LAYERS * PER["y_split"])
            for t in range(KT):
                if t >= 2:
                    pe.wait_ge(lw_split, t - 1)
                for o in range(KT):
                    m = pe.transpose(bank(5 + t % 2, o * P, (o + 1) * P), lw_raw[:, o, t * P:(t + 1) * P], ident[:])
                m.then_inc(lw_turned, 1)

            def turn_x1(t):
                pe.wait_ge(x1_ready, t + 1)
                if t < 2:
                    pe.wait_ge(lw_split, KT - 1 + t)
                else:
                    pe.wait_ge(x1_split, t - 1)
                for k in range(KT):
                    m = pe.transpose(bank(5 + t % 2, k * P, (k + 1) * P), x[:, t, k * P:(k + 1) * P], ident[:])
                m.then_inc(x1_turned, 1)

            turn_x1(0)
            for t in range(NT):
                if t + 1 < NT:
                    turn_x1(t + 1)
                pe.wait_ge(x1_split, t + 1)
                if t >= 2:
                    pe.wait_ge(z_split, t - 1)
                for k in range(KT):
                    m = mm3(bank(3 + t % 2), yT_hi[:, k, nt(t)], yT_lo[:, k, nt(t)], lw_hi[:, k, :], lw_lo[:, k, :], k == 0, k == KT - 1)
                m.then_inc(z_ready, 1)

            def turn_w(j):
                pe.wait_ge(wt_in[j % 3], 16 * (j // 3 + 1))
                for r, (lo, hi) in enumerate(WT_ROUNDS):
                    n = 3 * j + r
                    if n < 2:
                        pe.wait_ge(x1_split, NT - 1 + n)
                    else:
                        pe.wait_ge(wt_split, n - 1)
                    for d in range(lo, hi):
                        m = pe.transpose(bank(5 + n % 2, (d - lo) * P, (d - lo + 1) * P), prob[:, j % 3, d * P:(d + 1) * P], ident[:])
                    m.then_inc(wt_turned, 1)

            pe.wait_ge(pad_zero, 1)
            turn_w(0)
            for j in range(NT):
                if j + 1 < NT:
                    turn_w(j + 1)
                pe.wait_ge(wt_split, 3 * j + 3)
                if j == 0:
                    pe.wait_ge(z_split, NT)
                if j >= 2:
                    pe.wait_ge(agg_added, j - 1)
                for d in range(NT):
                    m = mm3(bank(j % 2), WT_hi[:, j % 2, d, :], WT_lo[:, j % 2, d, :], z_hi[:, d, :], z_lo[:, d, :], d == 0, d == NT - 1)
                m.then_inc(agg_ready, 1)


_INS = ["x", "src", "dst", "edge_weight", "node_vec1"] + ["L0_gnn_" + n for n in (
    "f_w1", "f_b1", "f_w2", "f_b2", "s1_w", "s1_b", "b1_w", "b1_b", "wq", "bq", "wk", "bk", "wv", "bv", "wo", "bo",
    "s2_w", "s2_b", "b2_w", "b2_b", "m_w1", "m_b1", "m_w2", "m_b2")] + ["L1_gnn_weight"]


def kernel(**inputs):
    import numpy as _np
    import concourse.bacc as _bacc
    from concourse import mybir as _mybir
    from concourse.bass_utils import run_bass_kernel_spmd as _run

    nc = _bacc.Bacc("TRN2", target_bir_lowering=False, num_devices=1)
    arrays = {name: _np.ascontiguousarray(inputs[name]) for name in _INS}
    T = {name: nc.dram_tensor(f"in_{name}_dram", a.shape, _mybir.dt.from_np(a.dtype), kind="ExternalInput").ap()
         for name, a in arrays.items()}
    out = nc.dram_tensor("out_0_dram", (N, D), F32, kind="ExternalOutput").ap()
    build(nc, T, out)
    r = _run(nc, [{f"in_{name}_dram": a for name, a in arrays.items()}], core_ids=[0])
    return r.results[0]["out_0_dram"]
```

```python
from contextlib import ExitStack

import concourse.bass as bass
from concourse import mybir

ALU = mybir.AluOpType
ACT = mybir.ActivationFunctionType
AX = mybir.AxisListType
F32 = mybir.dt.float32
F32R = mybir.dt.float32r
BF16 = mybir.dt.bfloat16
F16 = mybir.dt.float16
I32 = mybir.dt.int32

P = 128
N = 1250
NT = -(-N // P)
NP = NT * P
LAST = N - (NT - 1) * P
D = 512
KT = D // P
H = 4
DH = D // H
LAYERS = 4
C16 = 16
FREQS = 32
EPS = 1e-5
SCALE = float(DH) ** -0.5
ABSENT = -1e30
E = 21250
GK = 3
GE = GK * P
NG = -(-E // GE)
WIN = 32
CHUNK_G = 7
NCH = NG // CHUNK_G
UNROLL_G = 2 * CHUNK_G
ET = NG * GK
FULL_G = E // GE
TAIL_E = E - FULL_G * GE
GROUPS = NT // 2
PAIR = 2 * P
SLOTS = 6
STACK = SLOTS * C16 + 3
S1, S2, B1, B2, BV, BO, MB2 = range(7)
KINDS, CKINDS = 7, 4
BIAS_ROWS = 3 * LAYERS * KT
BIG = 3.0e38
COND_PART = (0, 0, 0, 1, 1, 2)
WEIGHT_PART = (0, 1, 2, 0, 1, 0)

START = NT

TWO_PI = 6.283185307179586
TURN = (6.28125, 2029.0 / 2 ** 20, TWO_PI - 6.28125 - 2029.0 / 2 ** 20)
MAGIC = 1.5 * 2 ** 23
PI_IN = 3.1415925
WT_ROUNDS = ((0, 4), (4, 8), (8, NT))

ROUNDS = (
    [(0, d) for d in (0, 1, 2, 3)],
    [(0, d) for d in (4, 5, 6, 7)],
    [(0, 8), (0, 9), (1, 8), (1, 9)],
    [(1, d) for d in (0, 1, 2, 3)],
    [(1, d) for d in (4, 5, 6, 7)],
)
assert NT == 10 and NG % UNROLL_G == 0 and UNROLL_G % 2 == 0

PER = dict(
    cond_ready=2 * NT, stats_ready=2 * NT, rstd_ready=2 * NT, y_ready=2 * NT, y_turned=2 * NT,
    y_hi=2 * NT, y_split=2 * NT,
    qk_ready=H * GROUPS, qk_hi=H * GROUPS, qk_split=H * GROUPS,
    v_ready=H * GROUPS, v_hi=H * GROUPS, v_split=H * GROUPS,
    scores_ready=H * NT, masked=H * NT, exped=H * NT, recip_ready=H * NT, probs_ready=H * NT,
    turned=H * GROUPS * 5, pt_hi=H * GROUPS * 5, pt_split=H * GROUPS * 5,
    o_ready=H * GROUPS, o_hi=H * GROUPS, o_split=H * GROUPS,
    wo_ready=H * NT, x_added=H * NT,
    bn_done=2 * NT, centered=2 * NT, inverted=H * NT, var_eps=2 * NT, h_ready=2 * GROUPS, h_relu=2 * GROUPS, h_split=2 * GROUPS,
    m2_ready=NT, x_mlp=NT,
    piece_hi=4 * H + 2 * KT, piece_split=4 * H + 2 * KT, pads_zero=3,
    bias_cur=1,
)


def build(nc, T, out):
    ctx = ExitStack()
    with ctx:
        def sb(name, shape, dt, c=ctx):
            return c.enter_context(nc.sbuf_tensor(name, shape, dt))

        def sem(name):
            return ctx.enter_context(nc.semaphore(name))

        w_dram = nc.dram_tensor("w_table", [NT, P, N], F32).ap()
        w_stack = nc.dram_tensor("w_stack", [SLOTS, C16, CKINDS, LAYERS, D], BF16).ap()
        b_stack = nc.dram_tensor("b_stack", [3, KINDS, LAYERS, D], BF16).ap()

        ident = sb("ident", [P, P], F32)
        cstack = sb("cstack", [STACK, NP], BF16)
        stacks = sb("stacks_sb", [STACK, KINDS, D], BF16)
        bias_all = sb("bias_all", [P, 3, LAYERS, KT], F32)
        bias = sb("bias", [P, 3, KT], F32)
        half = sb("half", [P, 1], F32)
        bn = sb("bn", [P, 2, 6], F32)
        mv = sb("mv", [P, 2 * NT, 2], F32)
        rs = sb("rs", [P, 2 * NT], F32)
        tiny = sb("tiny", [P, 1], F32)
        nmax = sb("nmax", [P, 4], F32)
        rsum = sb("rsum", [P, 4], F32)
        rinv = sb("rinv", [P, 4], F32)
        rnorm = sb("rnorm", [P, 4], F32)
        f_w1 = sb("f_w1", [64, C16], F32)
        f_w2 = sb("f_w2", [33, C16], F32)
        f_b1 = sb("f_b1", [C16, 2], F32)
        fcol = sb("fcol", [64, 3], F32)
        fcol_i = sb("fcol_i", [64, 1], I32)
        oT_hi = sb("oT_hi", [P, PAIR], F32R)
        oT_lo = sb("oT_lo", [P, PAIR], F32R)

        with ExitStack() as prep:
            row_raw = sb("row_raw", [KINDS + CKINDS * C16, LAYERS * D], F32, prep)
            row_part = [sb(f"row_part{i}", [KINDS + CKINDS * C16, LAYERS * D], BF16, prep) for i in range(3)]
        with ExitStack() as fin:
            lw_hi = sb("lw_hi", [P, KT, D], F32R, fin)
            lw_lo = sb("lw_lo", [P, KT, D], F32R, fin)
        piece = sb("piece", [P, 2, D], F32)
        wqkv_hi = sb("wqkv_hi", [P, 3, KT, DH], F32R)
        wqkv_lo = sb("wqkv_lo", [P, 3, KT, DH], F32R)
        wo_hi = sb("wo_hi", [P, D], F32R)
        wo_lo = sb("wo_lo", [P, D], F32R)

        with ExitStack() as prep:
            with ExitStack() as late:
                cpart = [sb(f"cpart{i}", [C16, NP], BF16, late) for i in range(3)]
            sin_a = sb("sin_a", [64, NP], F32, prep)
            sin_b = sb("sin_b", [64, NP], F32, prep)
            hcond = sb("hcond", [33, NP], F32, prep)
            cpart32 = sb("cpart32", [C16, NP], F32, prep)
        x = sb("x", [P, NT, D], F32)

        with ExitStack() as fin:
            z_hi = sb("z_hi", [P, NT, D], F32R, fin)
            z_lo = sb("z_lo", [P, NT, D], F32R, fin)
        with ExitStack() as tables:
            CW = sb("CW", [P, 2, NT, N], F32, tables)
        L = sb("L", [P, NT, N], F32)
        yT_hi = sb("yT_hi", [P, KT, NP], F32R)
        yT_lo = sb("yT_lo", [P, KT, NP], F32R)
        with ExitStack() as mlp:
            y2 = sb("y2", [P, 2, D], F32, mlp)
            mw_hi = [sb("mw1_hi", [P, KT, D], F32R, mlp)]
            mw_lo = [sb("mw1_lo", [P, KT, D], F32R, mlp)]
        with ExitStack() as fin:
            lw_raw = sb("lw_raw", [P, KT, D], F32, fin)
            x0 = sb("x0", [P, 2, D], F32, fin)
            res = sb("res", [P, 2, D], F32, fin)
        q_hi = sb("q_hi", [P, NP], F32R)
        q_lo = sb("q_lo", [P, NP], F32R)
        with ExitStack() as edges:
            eT = sb("eT", [P, 4, GK, NG], F32, edges)
            wres = sb("wres", [P, GK, NG], F32, edges)
            wpart = sb("wpart", [P, 3, NG, GK], BF16, edges)
            iota_h = sb("iota_h", [P, NP], F16, edges)
            grow = sb("grow", [1, 2, NG], F32, edges)
            grow_i = sb("grow_i", [1, NG + 1], I32, edges)
            viol = sb("viol", [1, 1], F32, edges)
            with ExitStack() as load:
                iota_i = sb("iota_i", [P, NP], I32, load)
                bias_rows = sb("bias_rows", [BIAS_ROWS, P], F32, load)
                src_i = sb("src_i", [NG, GE], I32, load)
                dst_i = sb("dst_i", [NG, GE], I32, load)
                ef = sb("ef", [NG, 4, GE], F32, load)
                gcol = sb("gcol", [NG, 2], F32, load)
            with ExitStack() as full:
                oh_src = sb("oh_src", [P, P], BF16, full)
                oh_dst = sb("oh_dst", [P, 4, N], BF16, full)
            win = sb("win", [P, 2, CHUNK_G * GK, 4, WIN], BF16, edges)
            onehot = sb("onehot", [P, 3, GK, NP], BF16, edges)
        with ExitStack() as tables:
            lnt = sb("lnt", [P, 2, N], F32, tables)
            absent = sb("absent", [P, 2, N], F32, tables)
        k_hi = sb("k_hi", [P, NP], F32R)
        k_lo = sb("k_lo", [P, NP], F32R)
        with ExitStack() as mlp:
            hT_hi = sb("hT_hi", [P, 2, KT, PAIR], F32R, mlp)
            hT_lo = sb("hT_lo", [P, 2, KT, PAIR], F32R, mlp)
            h32 = sb("h32", [P, 2, 2, PAIR], F32, mlp)
            mw_hi.append(sb("mw2_hi", [P, KT, D], F32R, mlp))
            mw_lo.append(sb("mw2_lo", [P, KT, D], F32R, mlp))
            y1 = sb("y1", [P, 3, D], F32, mlp)
        v_hi = sb("v_hi", [P, NT, DH], F32R)
        v_lo = sb("v_lo", [P, NT, DH], F32R)
        with ExitStack() as fin:
            WT_hi = sb("WT_hi", [P, 2, NT, P], F32R, fin)
            WT_lo = sb("WT_lo", [P, 2, NT, P], F32R, fin)
        PT_hi = sb("PT_hi", [P, NT, PAIR], F32R)
        PT_lo = sb("PT_lo", [P, NT, PAIR], F32R)
        prob = sb("prob", [P, 3, NP], F32)

        ps = ctx.enter_context(nc.psum_tensor("ps", [P, 8 * 512], F32))

        def bank(b, lo=0, hi=512):
            return ps[:, b * 512 + lo:b * 512 + hi]

        S = {name: sem(name) for name in PER}
        piece_in = [sem(f"piece_in{i}") for i in range(2)]
        stacks1_in, stacks2_in = sem("stacks1_in"), sem("stacks2_in")

        noise_in, f_in, bias_in, x_in, edge_in = (sem(n) for n in ("noise_in", "f_in", "bias_in", "x_in", "edge_in"))
        pre_set, rows_in, row_parts, stack_out, stack_zero = (sem(n) for n in ("pre_set", "rows_in", "row_parts", "stack_out", "stack_zero"))
        rchain, dchain, sin_ready, emb_ready, hraw, hexp, hsilu = (sem(n) for n in ("rchain", "dchain", "sin_ready", "emb_ready", "hraw", "hexp", "hsilu"))
        cond_raw, cond_hi, cond_parts, cstack_in, iota_set = (sem(n) for n in ("cond_raw", "cond_hi", "cond_parts", "cstack_in", "iota_set"))
        table_zero, edges_ready, edges_turned, eplan = (sem(n) for n in ("table_zero", "edges_ready", "edges_turned", "eplan"))
        e_win, e_parts, e_onehot, e_sum, e_added, e_chain = (sem(n) for n in ("e_win", "e_parts", "e_onehot", "e_sum", "e_added", "e_chain"))
        g_chain, g_onehot, g_sum, g_added = (sem(n) for n in ("g_chain", "g_onehot", "g_sum", "g_added"))
        tables_done, w_stored, mask_in, mask_ln, mask_done = (sem(n) for n in ("tables_done", "w_stored", "mask_in", "mask_ln", "mask_done"))
        x0_in = [sem(f"x0_in{i}") for i in range(2)]
        lw_in, lw_turned, lw_hi_done, lw_split = (sem(n) for n in ("lw_in", "lw_turned", "lw_hi_done", "lw_split"))
        fchain, fstats, frstd, x1_ready, x1_turned, x1_hi, x1_split = (sem(n) for n in ("fchain", "fstats", "frstd", "x1_ready", "x1_turned", "x1_hi", "x1_split"))
        fvar, x0_bn = sem("fvar"), sem("x0_bn")
        pool_passed, dve_passed = sem("pool_passed"), sem("dve_passed")
        z_ready, z_hi_done, z_split, pad_zero = (sem(n) for n in ("z_ready", "z_hi_done", "z_split", "pad_zero"))
        wt_in = [sem(f"wt_in{i}") for i in range(3)]
        wt_turned, wt_hi_done, wt_split, agg_ready, agg_added, res_ready = (sem(n) for n in ("wt_turned", "wt_hi_done", "wt_split", "agg_ready", "agg_added", "res_ready"))
        stored = [sem(f"stored{i}") for i in range(2)]

        counted = [*S.values(), e_sum, e_chain, g_chain]

        def t_bank(n):
            return 5 + n % 2

        def v_bank(h, c):
            return 7 if c else t_bank(PER["turned"] // H * h + 1)

        def nt(t):
            return slice(t * P, (t + 1) * P)

        def pair(c):
            return slice(c * PAIR, (c + 1) * PAIR)

        NCHUNKS = ((0, 512), (512, 1024), (1024, NP))

        def round_view(PT, n, r):
            b = bank(5 + n % 2)
            if r == 2:
                return (PT[:, 8:10, :].rearrange("p d (j c) -> p j d c", j=2),
                        b.rearrange("p (j d c) -> p j d c", j=2, d=2))
            j, d = ROUNDS[r][0]
            return PT[:, d:d + 4, j * P:(j + 1) * P], b.rearrange("p (d c) -> p d c", d=4)

        PIECES = [[[4 * h + 3] if g == 0 and h else [4 * (h + 1) + g - 1] if 0 < g < 4 and h < H - 1 else [] for g in range(GROUPS)]
                  for h in range(H)]
        PIECES[H - 1][GROUPS - 1] = [4 * H + t for t in range(KT)]

        def piece_parts(n):
            raw = piece[:, n % 2, :]
            if n >= 4 * H:
                which, t = divmod(n - 4 * H, KT)
                return raw, mw_hi[which][:, t, :], mw_lo[which][:, t, :]
            if n % 4 == 3:
                return raw, wo_hi[:], wo_lo[:]
            return raw.rearrange("p (t n) -> p t n", t=KT), wqkv_hi[:, n % 4], wqkv_lo[:, n % 4]

        def store(sp, j):
            n = P if j < NT - 1 else LAST
            sp.wait_ge(res_ready, j + 1)
            sp.dma_start(out[j * P:j * P + n, :], res[0:n, j % 2, :]).then_inc(stored[j % 2], 16)

        block = ctx.enter_context(nc.Block())

        @block.sync
        def _(sp):
            for s in counted:
                sp.sem_inc(s, START)
            sp.wait_ge(pre_set, 1)
            sp.dma_start(sin_a[:, 0:N], T["node_vec1"].rearrange("n o -> o n").broadcast_to([64, N])).then_inc(noise_in, 16)
            sp.dma_start(f_w1[:], T["L0_gnn_f_w1"]).then_inc(f_in, 16)
            sp.dma_start(f_b1[:, 0:1], T["L0_gnn_f_b1"].rearrange("(c o) -> c o", o=1)).then_inc(f_in, 16)
            sp.wait_ge(pre_set, 2)
            sp.dma_start(f_w2[0:C16, :], T["L0_gnn_f_w2"]).then_inc(f_in, 16)
            sp.dma_start(f_w2[32:33, :], T["L0_gnn_f_b2"].rearrange("(o c) -> o c", o=1)).then_inc(f_in, 16)
            sp.wait_ge(pre_set, 4)
            rows = FULL_G * GE
            for dst, src in ((src_i[:], T["src"]), (dst_i[:], T["dst"]), (ef[:, 3, :], T["edge_weight"])):
                sp.dma_start(dst[0:FULL_G, :], src[0:rows].rearrange("(g e) -> g e", e=GE)).then_inc(edge_in, 16)
                sp.dma_start(dst[FULL_G:NG, 0:TAIL_E], src[rows:E].rearrange("(o e) -> o e", o=1)).then_inc(edge_in, 16)
            sp.dma_start(dst_i[FULL_G:NG, TAIL_E:GE],
                         T["dst"][E - (GE - TAIL_E):E].rearrange("(o e) -> o e", o=1)).then_inc(edge_in, 16)
            for i, name in enumerate(("L0_gnn_bq", "L0_gnn_bk", "L0_gnn_m_b1")):
                rows = slice(i * LAYERS * KT, (i + 1) * LAYERS * KT)
                sp.dma_start(bias_rows[rows, :], T[name].rearrange("l (t p) -> (l t) p", p=P)).then_inc(bias_in, 16)
            for k, name in enumerate(("s1_b", "s2_b", "b1_b", "b2_b", "bv", "bo", "m_b2")):
                sp.dma_start(row_raw[k:k + 1, :], T["L0_gnn_" + name].rearrange("(o l) d -> o (l d)", o=1)).then_inc(rows_in, 16)
            for k, name in enumerate(("s1_w", "s2_w", "b1_w", "b2_w")):
                rows = slice(KINDS + k * C16, KINDS + (k + 1) * C16)
                sp.dma_start(row_raw[rows, :].rearrange("j (l d) -> j l d", l=LAYERS),
                             T["L0_gnn_" + name].rearrange("l j d -> j l d")).then_inc(rows_in, 16)

            sp.wait_ge(cond_parts, 1)
            for i, part in enumerate(COND_PART):
                sp.dma_start(cstack[i * C16:(i + 1) * C16, :], cpart[part][:]).then_inc(cstack_in, 16)
            sp.wait_ge(pre_set, 5)
            sp.wait_ge(cstack_in, 16 * SLOTS)
            sp.dma_start(x[:, 0:NT - 1, :], T["x"][0:(NT - 1) * P, :].rearrange("(t p) d -> p t d", p=P)).then_inc(x_in, 16)
            sp.dma_start(x[0:LAST, NT - 1, :], T["x"][(NT - 1) * P:N, :]).then_inc(x_in, 16)

            sp.wait_ge(row_parts, 3)
            for i, part in enumerate(WEIGHT_PART):
                for k in range(CKINDS):
                    sp.dma_start(w_stack[i, :, k].rearrange("j l d -> j (l d)"),
                                 row_part[part][KINDS + k * C16:KINDS + (k + 1) * C16, :]).then_inc(stack_out, 16)
            for part in range(3):
                sp.dma_start(b_stack[part].rearrange("k l d -> k (l d)"), row_part[part][0:KINDS, :]).then_inc(stack_out, 16)

            sp.wait_ge(tables_done, 1)
            sp.dma_start(w_dram.rearrange("t p n -> p t n"), CW[:, 1]).then_inc(w_stored, 16)
            sp.wait_ge(w_stored, 16)
            sp.wait_ge(stack_zero, 1)
            sp.wait_ge(stack_out, 16 * (SLOTS * CKINDS + 3))

            with sp.Fori(0, LAYERS) as l:
                def load_stacks(w, b, loaded):
                    sp.dma_start(stacks[0:SLOTS * C16, w, :],
                                 w_stack[:, :, w, bass.ds(l, 1), :].rearrange("i j k o d -> (i j) k (o d)")).then_inc(loaded, 16)
                    sp.dma_start(stacks[SLOTS * C16:STACK, b, :],
                                 b_stack[:, b, bass.ds(l, 1), :].rearrange("i k o d -> i k (o d)")).then_inc(loaded, 16)

                def load_piece(n):
                    sp.wait_ge(S["piece_split"], START + l * PER["piece_split"] + max(n - 1, 0))
                    if n < 4 * H:
                        h, what = divmod(n, 4)
                        if what < 3:
                            w = T[("L0_gnn_wq", "L0_gnn_wk", "L0_gnn_wv")[what]]
                            src = w[bass.ds(l, 1), :, h * DH:(h + 1) * DH].rearrange("o (t p) n -> p (o t) n", p=P)
                            dst = piece[:, n % 2, :].rearrange("p (t n) -> p t n", t=KT)
                        else:
                            src = T["L0_gnn_wo"][bass.ds(l, 1), h * DH:(h + 1) * DH, :].rearrange("o p n -> p (o n)")
                            dst = piece[:, n % 2, :]
                    else:
                        which, t = divmod(n - 4 * H, KT)
                        src = T[("L0_gnn_m_w1", "L0_gnn_m_w2")[which]][bass.ds(l, 1), t * P:(t + 1) * P, :].rearrange("o p n -> p (o n)")
                        dst = piece[:, n % 2, :]
                    sp.dma_start(dst, src).then_inc(piece_in[n % 2], 16)

                sp.wait_ge(S["v_ready"], START + l * PER["v_ready"])
                load_stacks(slice(S1, CKINDS, 2), slice(S1, BV + 1, 2), stacks1_in)
                for n in range(4):
                    load_piece(n)
                sp.wait_ge(S["m2_ready"], START + l * NT)
                load_stacks(slice(S2, CKINDS, 2), slice(S2, BO + 1, 2), stacks2_in)
                sp.dma_start(stacks[SLOTS * C16:STACK, MB2:KINDS, :],
                             b_stack[:, MB2:KINDS, bass.ds(l, 1), :].rearrange("i k o d -> i k (o d)")).then_inc(stacks2_in, 16)
                for n in range(4, PER["piece_split"]):
                    load_piece(n)

            sp.wait_ge(S["m2_ready"], START + LAYERS * NT)
            sp.dma_start(lw_raw[:], T["L1_gnn_weight"].rearrange("(t p) d -> p t d", p=P)).then_inc(lw_in, 16)

            def load_x0(t):
                n = P if t < NT - 1 else LAST
                if t >= 2:
                    sp.wait_ge(fstats, t - 1)
                sp.dma_start(x0[0:n, t % 2, :], T["x"][t * P:t * P + n, :]).then_inc(x0_in[t % 2], 16)

            for t in range(NT):
                load_x0(t)
            sp.wait_ge(pad_zero, 1)
            for j in range(NT):
                if j >= 3:
                    sp.wait_ge(wt_turned, 3 * (j - 2))
                sp.dma_start(prob[:, j % 3, 0:N], w_dram[j]).then_inc(wt_in[j % 3], 16)
                if j >= 3:
                    store(sp, j - 3)
            for j in range(NT - 3, NT):
                store(sp, j)
            for i in range(2):
                sp.wait_ge(stored[i], 16 * NT // 2)

        @block.gpsimd
        def _(pool):
            pool.memset(ident[:], 0.0).then_inc(iota_set, 1)
            pool.wait_ge(iota_set, 1)
            pool.iota(fcol_i[0:32, :], [[0, 1]], base=1, channel_multiplier=1).then_inc(iota_set, 1)
            pool.wait_ge(iota_set, 2)
            pool.iota(fcol_i[32:64, :], [[0, 1]], base=1, channel_multiplier=1).then_inc(iota_set, 1)
            pool.wait_ge(iota_set, 3)
            pool.iota(iota_i[:], [[1, NP]], base=0, channel_multiplier=0).then_inc(iota_set, 1)
            pool.affine_select(out=ident[:], in_=ident[:], pattern=[[-1, P]], compare_op=ALU.not_equal,
                               fill=1.0, base=0, channel_multiplier=1).then_inc(iota_set, 1)
            pool.memset(half[:], -0.5).then_inc(iota_set, 1)
            pool.memset(tiny[:], 2.0 ** -60).then_inc(iota_set, 1)
            pool.memset(stacks[0:SLOTS * C16, CKINDS:KINDS, :], 0.0).then_inc(stack_zero, 1)
            pool.wait_ge(stack_zero, 1)
            pool.memset(CW[:], 0.0).then_inc(table_zero, 1)

            for i in range(2):
                pool.wait_ge(row_parts, i + 1)
                pool.tensor_tensor(row_raw[:], row_raw[:], row_part[i][:], ALU.subtract).then_inc(rchain, 1)
            pool.wait_ge(rchain, 3)

            pool.wait_ge(table_zero, 1)
            pool.wait_ge(eplan, 2)
            flag = pool.value_load(grow_i[0:1, NG:NG + 1], min_val=0, max_val=1)
            with pool.If(flag < 1):
                with pool.Fori(0, NCH // 2) as i:
                    for c in range(2):
                        pool.wait_ge(e_win, i * 2 + c + 1)
                        pool.wait_ge(bias_in, 48)
                        for part in range(3):
                            oh = win[:, c, :, 0, :].rearrange("p (g b) w -> p g b w", b=GK)
                            o = win[:, c, :, 1 + part, :].rearrange("p (g b) w -> p g b w", b=GK)
                            wp = wpart[:, part, bass.ds(i * UNROLL_G + c * CHUNK_G, CHUNK_G), :]
                            m = pool.tensor_tensor(o, oh, wp.unsqueeze(3).to_broadcast([P, CHUNK_G, GK, WIN]), ALU.mult)
                        m.then_inc(e_parts, 1)
                pool.wait_ge(e_parts, NCH)

            for t in range(NT):
                pool.wait_ge(S["stats_ready"], START + t + 1)
                pool.tensor_scalar(rs[:, t:t + 1], mv[:, t, 1:2], EPS, None, ALU.add).then_inc(S["var_eps"], 1)
                pool.wait_ge(S["var_eps"], START + t + 1)
                pool.tensor_tensor(rs[:, t:t + 1], rs[:, t:t + 1], half[:], ALU.pow).then_inc(S["rstd_ready"], 1)

            with pool.Fori(0, LAYERS) as l:
                def wait(name, n):
                    pool.wait_ge(S[name], START + l * PER[name] + n)

                def settled():
                    pool.sem_inc(pool_passed, 1)

                def rsqrt(n):
                    i = n % (2 * NT)
                    wait("stats_ready", n + 1)
                    settled()
                    pool.tensor_scalar(rs[:, i:i + 1], mv[:, i, 1:2], EPS, None, ALU.add).then_inc(S["var_eps"], 1)
                    wait("var_eps", n + 1)
                    pool.tensor_tensor(rs[:, i:i + 1], rs[:, i:i + 1], half[:], ALU.pow).then_inc(S["rstd_ready"], 1)

                def rest(n):
                    wait("piece_hi", n + 1)
                    raw, hi, lo = piece_parts(n)
                    pool.tensor_tensor(lo, raw, hi.bitcast(F32), ALU.subtract).then_inc(S["piece_split"], 1)

                def norm(i):
                    wait("recip_ready", i + 1)
                    settled()
                    buf, r = prob[:, i % 3, 0:N], rnorm[:, i % 4:i % 4 + 1]
                    pool.tensor_scalar(buf, buf, r, 1.0, ALU.mult, ALU.mult).then_inc(S["probs_ready"], 1)

                def h_rest(c, half_):
                    wait("h_relu", 2 * c + half_ + 1)
                    pool.tensor_tensor(hT_lo[:, c % 2, 2 * half_:2 * half_ + 2, :], h32[:, half_],
                                       hT_hi[:, c % 2, 2 * half_:2 * half_ + 2, :].bitcast(F32), ALU.subtract)\
                        .then_inc(S["h_split"], 1)

                wait("h_relu", 0)
                settled()
                pool.tensor_copy(bias[:], bias_all[:, :, bass.ds(l, 1), :].rearrange("p k o t -> p k (o t)")).then_inc(S["bias_cur"], 1)
                for n in range(4):
                    rest(n)
                wait("y_turned", NT)
                settled()
                for b in range(3):
                    pool.memset(prob[:, b, N:NP], 0.0).then_inc(S["pads_zero"], 1)
                norm(0)
                norm(1)
                for h in range(H):
                    for g in range(GROUPS):
                        if h == H - 1 and g:
                            rsqrt(NT + 2 * g - 2)
                        if g < GROUPS - 1:
                            norm(NT * h + 2 * g + 2)
                        if h == H - 1 and g:
                            rsqrt(NT + 2 * g - 1)
                        for n in PIECES[h][g]:
                            rest(n)
                        if g < GROUPS - 1:
                            norm(NT * h + 2 * g + 3)
                    if h < H - 1:
                        norm(NT * (h + 1))
                        norm(NT * (h + 1) + 1)
                rsqrt(2 * NT - 2)
                rsqrt(2 * NT - 1)
                for c in range(GROUPS):
                    h_rest(c, 0)
                    h_rest(c, 1)
                    if c == 0:
                        for t in range(KT):
                            rest(4 * H + KT + t)
                    if c:
                        for t in (2 * c - 2, 2 * c - 1):
                            rsqrt(2 * NT + t)
                for t in range(NT - 2, NT):
                    rsqrt(2 * NT + t)

            pool.wait_ge(S["m2_ready"], START + LAYERS * NT)
            pool.memset(prob[:, :, N:NP], 0.0).then_inc(pad_zero, 1)
            for n in range(2 * NT):
                i = n % 4
                pool.wait_ge(fstats, n + 1)
                pool.tensor_scalar(rs[:, i:i + 1], mv[:, i, 1:2], EPS, None, ALU.add).then_inc(fvar, 1)
                pool.wait_ge(fvar, n + 1)
                pool.tensor_tensor(rs[:, i:i + 1], rs[:, i:i + 1], half[:], ALU.pow).then_inc(frstd, 1)

        @block.scalar
        def _(act):
            act.wait_ge(sin_ready, 1)
            act.activation(sin_a[:], sin_a[:], ACT.Sin).then_inc(emb_ready, 1)
            act.wait_ge(hraw, 1)
            act.wait_ge(hsilu, 1)
            act.activation(cpart32[:], ps[0:C16, 0:NP], ACT.Exp, bias=f_b1[:, 1:2], scale=-1.0).then_inc(hexp, 1)
            act.wait_ge(cond_raw, 1)
            act.wait_ge(hsilu, 2)
            act.activation(cpart[0][:], ps[0:C16, 3 * 512:3 * 512 + NP], ACT.Copy).then_inc(cond_hi, 1)
            for i in range(3):
                act.wait_ge(rchain, i + 1)
                act.activation(row_part[i][:], row_raw[:], ACT.Copy).then_inc(row_parts, 1)

            for t in range(NT):
                if t == 0:
                    act.wait_ge(tables_done, 1)
                    act.wait_ge(iota_set, 7)
                if t >= 2:
                    act.wait_ge(mask_done, t - 1)
                act.activation(lnt[:, t % 2, :], CW[:, 0, t, :], ACT.Ln, bias=tiny[:]).then_inc(mask_ln, 1)
            act.wait_ge(w_stored, 16)

            with act.Fori(0, LAYERS) as l:
                def wait(name, n):
                    act.wait_ge(S[name], START + l * PER[name] + n)

                def y_hi_(n):
                    t = n % NT
                    wait("y_turned", n + 1)
                    act.activation(yT_hi[:, :, nt(t)], bank(5 + n % 2).rearrange("p (k c) -> p k c", k=KT),
                                   ACT.Copy).then_inc(S["y_hi"], 1)

                def qk_hi_(h, c):
                    wait("qk_ready", GROUPS * h + c + 1)
                    b = 2 + c % 3 if h else 2
                    act.activation(q_hi[:, pair(c)], bank(b, 0, PAIR), ACT.Identity, bias=bias[:, 0, h:h + 1])
                    act.activation(k_hi[:, pair(c)], bank(b, PAIR, 512), ACT.Identity, bias=bias[:, 1, h:h + 1])\
                       .then_inc(S["qk_hi"], 1)

                def v_hi_(h, c):
                    wait("v_ready", GROUPS * h + c + 1)
                    act.activation(v_hi[:, 2 * c:2 * c + 2, :], bank(v_bank(h, c), 0, PAIR).rearrange("p (t c) -> p t c", t=2),
                                   ACT.Copy).then_inc(S["v_hi"], 1)

                def exp(i):
                    wait("masked", i + 1)
                    buf = prob[:, i % 3, 0:N]
                    act.activation(buf, buf, ACT.Exp, bias=nmax[:, i % 4:i % 4 + 1], scale=-1.0,
                                   accum_out=rsum[:, i % 4:i % 4 + 1]).then_inc(S["exped"], 1)

                def pt_hi_(h, g, r):
                    n = (GROUPS * h + g) * 5 + r
                    wait("turned", n + 1)
                    if r == 0:
                        wait("o_ready", GROUPS * h + g)
                    o, i = round_view(PT_hi, n, r)
                    act.activation(o, i, ACT.Copy).then_inc(S["pt_hi"], 1)

                def o_hi_(h, g):
                    wait("o_ready", GROUPS * h + g + 1)
                    wait("wo_ready", NT * h + 2 * g)
                    act.activation(oT_hi[:], bank(7, 0, PAIR), ACT.Copy).then_inc(S["o_hi"], 1)

                def relu(c, half_):
                    n = 2 * c + half_
                    wait("h_ready", n + 1)
                    if c:
                        wait("h_split", n - 1)
                    if c >= 2:
                        wait("m2_ready", 2 * (c - 1))
                    for i in range(2):
                        t = 2 * half_ + i
                        for o in (h32[:, half_, i, :], hT_hi[:, c % 2, t, :]):
                            m = act.activation(o, bank(2 + half_, i * PAIR, (i + 1) * PAIR), ACT.Relu, bias=bias[:, 2, t:t + 1])
                    m.then_inc(S["h_relu"], 1)

                def piece_hi(n):
                    if n >= 4 * H:
                        if n < 4 * H + KT:
                            wait("masked", H * NT)
                        else:
                            wait("o_ready", H * GROUPS)
                    elif n % 4 < 3:
                        wait(("qk_ready", "qk_ready", "v_ready")[n % 4], GROUPS * (n // 4))
                    else:
                        wait("wo_ready", NT * (n // 4))
                    act.wait_ge(piece_in[n % 2], l * 8 * PER["piece_split"] + 16 * (n // 2 + 1))
                    raw, hi, _ = piece_parts(n)
                    act.activation(hi, raw, ACT.Copy).then_inc(S["piece_hi"], 1)

                for n in range(4):
                    piece_hi(n)
                wait("m2_ready", 0)
                wait("bias_cur", 1)
                for t in range(NT):
                    y_hi_(t)
                    if t % 2 and t >= 3:
                        qk_hi_(0, (t - 3) // 2)
                qk_hi_(0, GROUPS - 1)
                exp(0)
                exp(1)
                v_hi_(0, 0)
                for h in range(H):
                    for g in range(GROUPS):
                        last, more = g == GROUPS - 1, h < H - 1
                        i = NT * h + 2 * g + 2
                        if g:
                            o_hi_(h, g - 1)
                        for r in range(5):
                            pt_hi_(h, g, r)
                            if last and more:
                                qk_hi_(h + 1, r)
                            if g == 0 and r < 4:
                                v_hi_(h, r + 1)
                            if r == 2 and not last:
                                exp(i)
                        if not last:
                            exp(i + 1)
                        for n in PIECES[h][g]:
                            piece_hi(n)
                    o_hi_(h, GROUPS - 1)
                    if h < H - 1:
                        exp(NT * (h + 1))
                        exp(NT * (h + 1) + 1)
                        v_hi_(h + 1, 0)
                wait("v_ready", H * GROUPS)
                y_hi_(NT)
                y_hi_(NT + 1)
                for c in range(GROUPS):
                    relu(c, 0)
                    if c < GROUPS - 1:
                        y_hi_(NT + 2 * c + 2)
                    relu(c, 1)
                    if c < GROUPS - 1:
                        y_hi_(NT + 2 * c + 3)
                    if c == 0:
                        for t in range(KT):
                            piece_hi(4 * H + KT + t)

            for t in range(KT):
                act.wait_ge(lw_turned, t + 1)
                act.activation(lw_hi[:, t, :], bank(5 + t % 2), ACT.Copy).then_inc(lw_hi_done, 1)
            for t in range(NT):
                act.wait_ge(x1_turned, t + 1)
                act.activation(yT_hi[:, :, nt(t)], bank(5 + t % 2).rearrange("p (k c) -> p k c", k=KT), ACT.Copy)\
                   .then_inc(x1_hi, 1)
                if t:
                    act.wait_ge(z_ready, t)
                    act.activation(z_hi[:, t - 1, :], bank(3 + (t - 1) % 2), ACT.Copy).then_inc(z_hi_done, 1)
            act.wait_ge(z_ready, NT)
            act.activation(z_hi[:, NT - 1, :], bank(3 + (NT - 1) % 2), ACT.Copy).then_inc(z_hi_done, 1)
            for j in range(NT):
                for r, (lo, hi) in enumerate(WT_ROUNDS):
                    n = 3 * j + r
                    act.wait_ge(wt_turned, n + 1)
                    if j >= 2:
                        act.wait_ge(agg_ready, j - 1)
                    act.activation(WT_hi[:, j % 2, lo:hi, :], bank(5 + n % 2, 0, (hi - lo) * P).rearrange("p (k c) -> p k c", c=P),
                                   ACT.Copy).then_inc(wt_hi_done, 1)

        @block.vector
        def _(dve):
            dve.memset(sin_a[:, N:NP], 0.0).then_inc(pre_set, 1)
            dve.memset(f_w2[:], 0.0).then_inc(pre_set, 1)
            dve.memset(cstack[SLOTS * C16:STACK, :], 1.0).then_inc(dchain, 1)
            dve.memset(src_i[:], -1).then_inc(pre_set, 1)
            dve.memset(ef[:, 3, :], 0.0).then_inc(pre_set, 1)
            link_n = [1]

            def link(m):
                link_n[0] += 1
                m.then_inc(dchain, 1)
                dve.wait_ge(dchain, link_n[0])

            dve.memset(hcond[:], 0.0)
            link(dve.memset(fcol[0:32, 1:3], 0.0))
            dve.memset(hcond[32:33, :], 1.0)
            dve.memset(fcol[32:64, 1:2], 0.25)
            link(dve.memset(fcol[32:64, 2:3], TWO_PI / 4))
            dve.wait_ge(iota_set, 3)
            link(dve.tensor_scalar(fcol[:, 0:1], fcol_i[:], TWO_PI / 16.0, None, ALU.mult))
            dve.wait_ge(noise_in, 16)
            link(dve.tensor_scalar(sin_a[:], sin_a[:], fcol[:, 0:1], None, ALU.mult))
            link(dve.tensor_scalar(sin_b[:], sin_a[:], 1.0 / TWO_PI, None, ALU.mult))
            link(dve.tensor_scalar(sin_b[:], sin_b[:], fcol[:, 1:2], None, ALU.add))
            link(dve.tensor_scalar(sin_b[:], sin_b[:], MAGIC, None, ALU.add))
            link(dve.tensor_scalar(sin_b[:], sin_b[:], -MAGIC, None, ALU.add))
            for c in TURN:
                link(dve.scalar_tensor_tensor(out=sin_a[:], in0=sin_b[:], scalar=-c, in1=sin_a[:], op0=ALU.mult, op1=ALU.add))
            link(dve.tensor_scalar(sin_a[:], sin_a[:], fcol[:, 2:3], PI_IN, ALU.add, ALU.min))
            dve.tensor_scalar(sin_a[:], sin_a[:], -PI_IN, None, ALU.max).then_inc(sin_ready, 1)

            dve.wait_ge(edge_in, 16 * 7)
            dve.tensor_copy(ef[:, 0, :], src_i[:])
            link(dve.tensor_copy(ef[:, 2, :], dst_i[:]))
            link(dve.tensor_reduce(gcol[:, 0:1], ef[:, 2, :], AX.X, ALU.min))
            link(dve.tensor_scalar(gcol[:, 0:1], gcol[:, 0:1], float(N - WIN), None, ALU.min))
            link(dve.tensor_scalar(ef[:, 1, :], ef[:, 2, :], gcol[:, 0:1], None, ALU.subtract))
            dve.tensor_reduce(gcol[:, 1:2], ef[:, 1, :], AX.X, ALU.max).then_inc(edges_ready, 1)

            dve.wait_ge(rows_in, 16 * (KINDS + CKINDS))
            dve.tensor_scalar(row_raw[0:2, :], row_raw[0:2, :], 1.0, None, ALU.add).then_inc(rchain, 1)
            dve.wait_ge(f_in, 16 * 4)
            dve.tensor_scalar(f_b1[:, 1:2], f_b1[:, 0:1], -1.0, None, ALU.mult).then_inc(hsilu, 1)
            dve.wait_ge(hexp, 1)
            dve.tensor_scalar(sin_b[0:C16, :], ps[0:C16, 0:NP], f_b1[:, 0:1], None, ALU.add)
            link(dve.tensor_scalar(cpart32[:], cpart32[:], 1.0, None, ALU.add))
            link(dve.reciprocal(cpart32[:], cpart32[:]))
            dve.tensor_tensor(hcond[0:C16, :], sin_b[0:C16, :], cpart32[:], ALU.mult).then_inc(hsilu, 1)
            dve.wait_ge(cond_hi, 1)
            link(dve.tensor_tensor(cpart32[:], ps[0:C16, 3 * 512:3 * 512 + NP], cpart[0][:], ALU.subtract))
            link(dve.tensor_copy(cpart[1][:], cpart32[:]))
            link(dve.tensor_tensor(cpart32[:], cpart32[:], cpart[1][:], ALU.subtract))
            dve.tensor_copy(cpart[2][:], cpart32[:]).then_inc(cond_parts, 1)

            dve.wait_ge(cond_parts, 1)
            dve.memset(x[:, NT - 1, :], 0.0).then_inc(pre_set, 1)

            dve.wait_ge(iota_set, 4)
            link(dve.tensor_copy(iota_h[:], iota_i[:]))
            dve.wait_ge(edges_turned, 1)
            cols = GK * NG
            dve.tensor_copy(eT[:, 0:2].rearrange("p k b g -> p (k b g)"), bank(6, 0, 2 * cols))
            dve.tensor_copy(bias_all[:].rearrange("p k l t -> p (k l t)"), bank(7, 2 * cols, 2 * cols + BIAS_ROWS))
            dve.tensor_copy(grow[:].rearrange("o k g -> o (k g)"), ps[0:1, 6 * 512 + 2 * cols:6 * 512 + 2 * cols + 2 * NG])
            link(dve.tensor_copy(eT[:, 2:4].rearrange("p k b g -> p (k b g)"), bank(7, 0, 2 * cols)))
            weight = eT[:, 3]
            parts = [wpart[:, i].rearrange("p g b -> p b g") for i in range(3)]
            link(dve.tensor_copy(parts[0], weight))
            link(dve.tensor_tensor(wres[:], weight, parts[0], ALU.subtract))
            link(dve.tensor_copy(parts[1], wres[:]))
            link(dve.tensor_tensor(wres[:], wres[:], parts[1], ALU.subtract))
            dve.tensor_copy(parts[2], wres[:]).then_inc(eplan, 1)
            link(dve.tensor_reduce(viol[:], grow[:, 1, :], AX.X, ALU.max))
            link(dve.tensor_copy(grow_i[:, 0:NG], grow[:, 0, :]))
            dve.tensor_scalar(grow_i[:, NG:NG + 1], viol[:], float(WIN), None, ALU.is_ge).then_inc(eplan, 1)
            dve.wait_ge(eplan, 2)
            dve.wait_ge(table_zero, 1)

            flag = dve.value_load(grow_i[0:1, NG:NG + 1], min_val=0, max_val=1)
            with dve.If(flag < 1):
                with dve.Fori(0, NG // UNROLL_G) as i:
                    def window(c):
                        dve.wait_ge(e_sum, START + i * UNROLL_G)
                        off = eT[:, 1, :, bass.ds(i * UNROLL_G + c * CHUNK_G, CHUNK_G)].rearrange("p b g -> p g b")
                        dve.tensor_tensor(win[:, c, :, 0, :].rearrange("p (g b) w -> p g b w", b=GK),
                                          iota_h[:, 0:WIN].unsqueeze(1).unsqueeze(1).to_broadcast([P, CHUNK_G, GK, WIN]),
                                          off.unsqueeze(3).to_broadcast([P, CHUNK_G, GK, WIN]), ALU.is_equal)\
                           .then_inc(e_win, 1)

                    def sources(j):
                        if j >= 3:
                            dve.wait_ge(e_sum, START + i * UNROLL_G + j - 2)
                        for b in range(GK):
                            m = dve.tensor_scalar(onehot[:, j % 3, b, :], iota_h[:], eT[:, 0, b, bass.ds(i * UNROLL_G + j, 1)],
                                                  None, ALU.is_equal)
                        m.then_inc(e_onehot, 1)

                    def accumulate(j):
                        dve.wait_ge(e_sum, START + i * UNROLL_G + j + 1)
                        base = dve.value_load(grow_i[0:1, bass.ds(i * UNROLL_G + j, 1)], min_val=0, max_val=N - WIN)
                        sums = ps[:, (j % 2) * 3 * 512:(j % 2) * 3 * 512 + NT * 4 * WIN].rearrange("p (t k w) -> p k t w", k=4, w=WIN)
                        both = CW[:, :, :, bass.ds(base, WIN)]
                        only = CW[:, 1, :, bass.ds(base, WIN)]
                        at = i * 3 * UNROLL_G + 3 * j
                        dve.wait_ge(e_chain, START + at)
                        dve.tensor_tensor(both, both, sums[:, 0:2], ALU.add).then_inc(e_chain, 1)
                        dve.wait_ge(e_chain, START + at + 1)
                        dve.tensor_tensor(only, only, sums[:, 2], ALU.add).then_inc(e_chain, 1)
                        dve.wait_ge(e_chain, START + at + 2)
                        dve.tensor_tensor(only, only, sums[:, 3], ALU.add).then_inc(e_chain, 1)

                    window(0)
                    sources(0)
                    sources(1)
                    for j in range(UNROLL_G):
                        if j == CHUNK_G - 3:
                            window(1)
                        if j + 2 < UNROLL_G:
                            sources(j + 2)
                        accumulate(j)
                dve.wait_ge(e_chain, START + 3 * NG)
            with dve.Else():
                with dve.Fori(0, NT) as s:
                    with dve.Fori(0, NG) as g:
                        for b in range(GK):
                            step = s * NG * GK + g * GK + b
                            dve.wait_ge(g_chain, START + 3 * step)
                            dve.tensor_scalar(oh_src[:], iota_h[:, bass.ds(s * P, P)], eT[:, 0, b, bass.ds(g, 1)],
                                              None, ALU.is_equal)
                            dve.tensor_scalar(oh_dst[:, 0, :], iota_h[:, 0:N], eT[:, 2, b, bass.ds(g, 1)],
                                              None, ALU.is_equal).then_inc(g_chain, 1)
                            dve.wait_ge(g_chain, START + 3 * step + 1)
                            for part in range(3):
                                m = dve.tensor_tensor(oh_dst[:, 1 + part, :], oh_dst[:, 0, :],
                                                      wpart[:, part, bass.ds(g, 1), b].to_broadcast([P, N]), ALU.mult)
                            m.then_inc(g_onehot, 1)
                            dve.wait_ge(g_sum, step + 1)
                            for k in range(2):
                                dst = CW[:, k, bass.ds(s, 1), :].rearrange("p o n -> p (o n)")
                                dve.tensor_tensor(dst, dst, ps[:, k * 1536:k * 1536 + N], ALU.add).then_inc(g_chain, 1)
                dve.wait_ge(g_chain, START + 3 * NT * ET)
            dve.memset(viol[:], 0.0).then_inc(tables_done, 1)

            for t in range(NT):
                if t >= 2:
                    dve.wait_ge(mask_done, t - 1)
                dve.tensor_scalar(absent[:, t % 2, :], CW[:, 0, t, :], 0.0, ABSENT, ALU.is_equal, ALU.mult).then_inc(mask_in, 1)
                dve.wait_ge(mask_in, t + 1)
                dve.wait_ge(mask_ln, t + 1)
                dve.scalar_tensor_tensor(out=L[:, t, :], in0=lnt[:, t % 2, :], scalar=1.0 / SCALE,
                                         in1=absent[:, t % 2, :], op0=ALU.mult, op1=ALU.add).then_inc(mask_done, 1)
            dve.wait_ge(mask_done, NT)
            dve.wait_ge(x_in, 32)
            for t in range(NT):
                dve.bn_stats(bn[:, t % 2, :], x[:, t, :]).then_inc(S["bn_done"], 1)
                dve.wait_ge(S["bn_done"], START + t + 1)
                dve.bn_aggr(mv[:, t, :], bn[:, t % 2, :]).then_inc(S["stats_ready"], 1)

            with dve.Fori(0, LAYERS) as l:
                def wait(name, n):
                    dve.wait_ge(S[name], START + l * PER[name] + n)

                def settled():
                    dve.sem_inc(dve_passed, 1)

                def stats(n):
                    if n < 2 * NT:
                        wait("x_added", (H - 1) * NT + n % NT + 1)
                    else:
                        wait("x_mlp", n % NT + 1)
                    dve.bn_stats(bn[:, n % 2, :], x[:, n % NT, :]).then_inc(S["bn_done"], 1)
                    wait("bn_done", n + 1)
                    settled()
                    dve.bn_aggr(mv[:, n % (2 * NT), :], bn[:, n % 2, :]).then_inc(S["stats_ready"], 1)

                def rows_of(n):
                    if n < NT:
                        return y1[:, n % 3, :], 3 * (n % 2)
                    return y2[:, n % 2, :], 0

                def center(n):
                    y, b = rows_of(n)
                    wait("cond_ready", n + 1)
                    if n < NT and n >= 3:
                        wait("y_turned", n - 2)
                    elif n >= NT + 2:
                        wait("y_turned", n - 1)
                    dve.scalar_tensor_tensor(out=y, in0=x[:, n % NT, :], scalar=mv[:, n, 0:1], in1=bank(b),
                                             op0=ALU.subtract, op1=ALU.mult).then_inc(S["centered"], 1)

                def norm(n):
                    y, b = rows_of(n)
                    wait("centered", n + 1)
                    wait("rstd_ready", n + 1)
                    dve.scalar_tensor_tensor(out=y, in0=y, scalar=rs[:, n:n + 1], in1=bank(b + 1),
                                             op0=ALU.mult, op1=ALU.add).then_inc(S["y_ready"], 1)

                def y_lo_(n):
                    wait("y_hi", n + 1)
                    dve.tensor_tensor(yT_lo[:, :, nt(n % NT)], bank(5 + n % 2).rearrange("p (k c) -> p k c", k=KT),
                                      yT_hi[:, :, nt(n % NT)].bitcast(F32), ALU.subtract).then_inc(S["y_split"], 1)

                def qk_lo_(h, c):
                    wait("qk_hi", GROUPS * h + c + 1)
                    b = 2 + c % 3 if h else 2
                    for i, (hi, lo) in enumerate(((q_hi, q_lo), (k_hi, k_lo))):
                        m = dve.scalar_tensor_tensor(out=lo[:, pair(c)], in0=bank(b, i * PAIR, (i + 1) * PAIR),
                                                     scalar=bias[:, i, h:h + 1], in1=hi[:, pair(c)].bitcast(F32),
                                                     op0=ALU.add, op1=ALU.subtract)
                    m.then_inc(S["qk_split"], 1)

                def v_lo_(h, c):
                    wait("v_hi", GROUPS * h + c + 1)
                    dve.tensor_tensor(v_lo[:, 2 * c:2 * c + 2, :], bank(v_bank(h, c), 0, PAIR).rearrange("p (t c) -> p t c", t=2),
                                      v_hi[:, 2 * c:2 * c + 2, :].bitcast(F32), ALU.subtract).then_inc(S["v_split"], 1)

                def mask(i):
                    wait("scores_ready", i + 1)
                    if i >= 3:
                        g, j = divmod(i - 3, 2)
                        wait("turned", 5 * g + (5 if j else 3))
                    settled()
                    off = (i % 2) * N
                    dve.tensor_tensor_reduce(prob[:, i % 3, 0:N], ps[:, off:off + N], L[:, i % NT, :], -SCALE, BIG,
                                             ALU.add, ALU.min, nmax[:, i % 4:i % 4 + 1]).then_inc(S["masked"], 1)

                def recip(i):
                    r = slice(i % 4, i % 4 + 1)
                    wait("exped", i + 1)
                    dve.reciprocal(rinv[:, r], rsum[:, r]).then_inc(S["inverted"], 1)
                    wait("inverted", i + 1)
                    dve.scalar_tensor_tensor(out=rnorm[:, r], in0=nmax[:, r], scalar=-ABSENT * SCALE * 0.1, in1=rinv[:, r],
                                             op0=ALU.is_lt, op1=ALU.mult).then_inc(S["recip_ready"], 1)

                def pt_lo_(h, g, r):
                    n = (GROUPS * h + g) * 5 + r
                    wait("pt_hi", n + 1)
                    hi, i = round_view(PT_hi, n, r)
                    lo, _ = round_view(PT_lo, n, r)
                    dve.tensor_tensor(lo, i, hi.bitcast(F32), ALU.subtract).then_inc(S["pt_split"], 1)

                def o_lo_(h, g):
                    wait("o_hi", GROUPS * h + g + 1)
                    dve.tensor_tensor(oT_lo[:], bank(7, 0, PAIR), oT_hi[:].bitcast(F32), ALU.subtract).then_inc(S["o_split"], 1)

                def add_wo(h, t):
                    i = NT * h + t
                    wait("wo_ready", i + 1)
                    if h:
                        wait("x_added", i - NT + 1)
                    dve.tensor_tensor(x[:, t, :], bank(7), x[:, t, :], ALU.add).then_inc(S["x_added"], 1)

                def add_mlp(t):
                    wait("m2_ready", t + 1)
                    dve.tensor_tensor(x[:, t, :], bank(4 + 3 * (t % 2)), x[:, t, :], ALU.add).then_inc(S["x_mlp"], 1)

                wait("x_mlp", 0)
                wait("bias_cur", 1)
                for t in range(2):
                    center(t)
                    norm(t)
                for t in range(NT):
                    if t + 2 < NT:
                        center(t + 2)
                    y_lo_(t)
                    if t + 2 < NT:
                        norm(t + 2)
                    if t % 2 and t >= 3:
                        qk_lo_(0, (t - 3) // 2)
                qk_lo_(0, GROUPS - 1)
                mask(0)
                mask(1)
                recip(0)
                recip(1)
                v_lo_(0, 0)
                for h in range(H):
                    for g in range(GROUPS):
                        last, more = g == GROUPS - 1, h < H - 1
                        i = NT * h + 2 * g + 2
                        if g:
                            o_lo_(h, g - 1)
                        for r in range(5):
                            pt_lo_(h, g, r)
                            if last and more:
                                qk_lo_(h + 1, r)
                            if g == 0 and r < 4:
                                v_lo_(h, r + 1)
                            if r == 1 and not last:
                                mask(i)
                            if r == 1 and last and not more:
                                center(NT)
                            if r == 2:
                                if g:
                                    add_wo(h, 2 * g - 2)
                                    if not more:
                                        stats(NT + 2 * g - 2)
                                if not last:
                                    recip(i)
                                elif not more:
                                    norm(NT)
                            if r == 3 and g:
                                add_wo(h, 2 * g - 1)
                        if not last:
                            mask(i + 1)
                        if g and not more:
                            stats(NT + 2 * g - 1)
                        if not last:
                            recip(i + 1)
                    if h == H - 1:
                        center(NT + 1)
                        norm(NT + 1)
                    o_lo_(h, GROUPS - 1)
                    if h < H - 1:
                        mask(NT * (h + 1))
                        add_wo(h, NT - 2)
                        recip(NT * (h + 1))
                        mask(NT * (h + 1) + 1)
                        v_lo_(h + 1, 0)
                        add_wo(h, NT - 1)
                        recip(NT * (h + 1) + 1)
                y_lo_(NT)
                center(NT + 2)
                y_lo_(NT + 1)
                norm(NT + 2)
                for t in (NT - 2, NT - 1):
                    add_wo(H - 1, t)
                    stats(NT + t)
                for c in range(GROUPS):
                    if c < GROUPS - 1:
                        for n in (NT + 2 * c + 2, NT + 2 * c + 3):
                            if n + 1 < 2 * NT:
                                center(n + 1)
                            y_lo_(n)
                            if n + 1 < 2 * NT:
                                norm(n + 1)
                    if c:
                        for t in (2 * c - 2, 2 * c - 1):
                            add_mlp(t)
                            stats(2 * NT + t)
                for t in range(NT - 2, NT):
                    add_mlp(t)
                    stats(2 * NT + t)

            fn = [0]

            def flink(m):
                fn[0] += 1
                m.then_inc(fchain, 1)
                dve.wait_ge(fchain, fn[0])

            def fstat(n):
                flink(dve.bn_stats(bn[:, n % 2, :], x[:, n % NT, :]))
                dve.bn_aggr(mv[:, n % 4, :], bn[:, n % 2, :]).then_inc(fstats, 1)

            def residual(t):
                dve.wait_ge(x0_in[t % 2], 16 * (t // 2 + 1))
                flink(dve.tensor_tensor(x[:, t, :], x[:, t, :], x0[:, t % 2, :], ALU.add))
                fstat(t)

            def norm_x1(t):
                dve.wait_ge(frstd, t + 1)
                dve.tensor_scalar(x[:, t, :], x[:, t, :], mv[:, t % 4, 0:1], rs[:, t % 4:t % 4 + 1], ALU.subtract, ALU.mult)\
                   .then_inc(x1_ready, 1)

            def z_lo_(t):
                dve.wait_ge(z_hi_done, t + 1)
                dve.tensor_tensor(z_lo[:, t, :], bank(3 + t % 2), z_hi[:, t, :].bitcast(F32), ALU.subtract).then_inc(z_split, 1)

            dve.wait_ge(S["x_mlp"], START + LAYERS * NT)
            for t in range(KT):
                dve.wait_ge(lw_hi_done, t + 1)
                dve.tensor_tensor(lw_lo[:, t, :], bank(5 + t % 2), lw_hi[:, t, :].bitcast(F32), ALU.subtract).then_inc(lw_split, 1)
            residual(0)
            residual(1)
            norm_x1(0)
            for t in range(NT):
                if t + 1 < NT:
                    norm_x1(t + 1)
                if t + 2 < NT:
                    residual(t + 2)
                dve.wait_ge(x1_hi, t + 1)
                dve.tensor_tensor(yT_lo[:, :, nt(t)], bank(5 + t % 2).rearrange("p (k c) -> p k c", k=KT),
                                  yT_hi[:, :, nt(t)].bitcast(F32), ALU.subtract).then_inc(x1_split, 1)
                if t:
                    z_lo_(t - 1)
            z_lo_(NT - 1)

            def result(j):
                dve.wait_ge(frstd, NT + j + 1)
                if j >= 2:
                    dve.wait_ge(stored[j % 2], 16 * (j // 2))
                n = NT + j
                dve.tensor_scalar(res[:, j % 2, :], x[:, j, :], mv[:, n % 4, 0:1], rs[:, n % 4:n % 4 + 1],
                                  ALU.subtract, ALU.mult).then_inc(res_ready, 1)

            def aggregated(j):
                dve.wait_ge(agg_ready, j + 1)
                m = dve.tensor_tensor(x[:, j, :], bank(j % 2), x[:, j, :], ALU.add)
                m.then_inc(agg_added, 1)
                dve.wait_ge(agg_added, j + 1)
                fstat(NT + j)

            for j in range(NT):
                for r, (lo, hi) in enumerate(WT_ROUNDS):
                    n = 3 * j + r
                    dve.wait_ge(wt_hi_done, n + 1)
                    dve.tensor_tensor(WT_lo[:, j % 2, lo:hi, :], bank(5 + n % 2, 0, (hi - lo) * P).rearrange("p (k c) -> p k c", c=P),
                                      WT_hi[:, j % 2, lo:hi, :].bitcast(F32), ALU.subtract).then_inc(wt_split, 1)
                if j:
                    aggregated(j - 1)
                    result(j - 1)
            aggregated(NT - 1)
            result(NT - 1)

        @block.tensor
        def _(pe):
            def mm(o, a, b, start, stop):
                return pe.matmul(o, a, b, start=start, stop=stop)

            def mm3(o, a_hi, a_lo, b_hi, b_lo, start, stop):
                mm(o, a_hi, b_hi, start, False)
                mm(o, a_hi, b_lo, False, False)
                return mm(o, a_lo, b_hi, False, stop)

            pe.wait_ge(f_in, 16 * 4)
            pe.wait_ge(emb_ready, 1)
            for lo, hi in NCHUNKS:
                m = mm(ps[0:C16, lo:hi], f_w1[:], sin_a[:, lo:hi], True, True)
            m.then_inc(hraw, 1)
            pe.wait_ge(edges_ready, 1)
            pe.wait_ge(iota_set, 6)
            cols = GK * NG
            for kind in range(4):
                for b in range(GK):
                    at = (6 + kind // 2) * 512 + (kind % 2) * cols + b * NG
                    pe.transpose(ps[:, at:at + NG], ef[:, kind, b * P:(b + 1) * P], ident[0:NG, 0:NG])
            pe.wait_ge(bias_in, 48)
            pe.transpose(bank(7, 2 * cols, 2 * cols + BIAS_ROWS), bias_rows[:], ident[0:BIAS_ROWS, 0:BIAS_ROWS])
            for i in range(2):
                at = 6 * 512 + 2 * cols + i * NG
                m = pe.transpose(ps[0:1, at:at + NG], gcol[:, i:i + 1], ident[0:NG, 0:NG])
            m.then_inc(edges_turned, 1)
            pe.wait_ge(hsilu, 2)
            for lo, hi in NCHUNKS:
                m = mm(ps[0:C16, 3 * 512 + lo:3 * 512 + hi], f_w2[:], hcond[:, lo:hi], True, True)
            m.then_inc(cond_raw, 1)

            pe.wait_ge(eplan, 2)
            pe.wait_ge(cond_parts, 1)
            flag = pe.value_load(grow_i[0:1, NG:NG + 1], min_val=0, max_val=1)
            with pe.If(flag < 1):
                with pe.Fori(0, NG // UNROLL_G) as i:
                    for j in range(UNROLL_G):
                        c, gl = divmod(j, CHUNK_G)
                        if gl == 0:
                            pe.wait_ge(e_parts, i * 2 + c + 1)
                        pe.wait_ge(e_onehot, i * UNROLL_G + j + 1)
                        pe.wait_ge(e_chain, START + i * 3 * UNROLL_G + 3 * max(j - 1, 0))
                        for s in range(NT):
                            for b in range(GK):
                                at = (j % 2) * 3 * 512 + s * 4 * WIN
                                m = mm(ps[:, at:at + 4 * WIN], onehot[:, j % 3, b, nt(s)],
                                       win[:, c, gl * GK + b].rearrange("p k w -> p (k w)"), b == 0, b == GK - 1)
                        m.then_inc(e_sum, 1)
            with pe.Else():
                with pe.Fori(0, NT) as s:
                    with pe.Fori(0, NG) as g:
                        for b in range(GK):
                            step = s * NG * GK + g * GK + b
                            pe.wait_ge(g_onehot, step + 1)
                            pe.wait_ge(g_chain, START + 3 * step)
                            for lo, hi in ((0, 512), (512, 1024), (1024, N)):
                                mm(ps[:, lo:hi], oh_src[:], oh_dst[:, 0, lo:hi], True, True)
                                for part in range(3):
                                    m = mm(ps[:, 1536 + lo:1536 + hi], oh_src[:], oh_dst[:, 1 + part, lo:hi],
                                           part == 0, part == 2)
                            m.then_inc(g_sum, 1)
            pe.wait_ge(cstack_in, 16 * SLOTS)
            pe.wait_ge(tables_done, 1)

            with pe.Fori(0, LAYERS) as l:
                m_last = [("x_mlp", 0)]

                def wait(name, n):
                    pe.wait_ge(S[name], START + l * PER[name] + n)

                def take_m(name, n):
                    wait(*m_last[0])
                    m_last[0] = (name, n)

                def cond(n):
                    b = 3 * (n % 2) if n < NT else 0
                    if n == 0:
                        wait("y_ready", 0)
                    elif n == 1:
                        wait("h_relu", 0)
                        wait("x_mlp", -1)
                    elif n < NT:
                        wait("y_ready", n - 1)
                    elif n == NT:
                        wait("masked", H * NT)
                    else:
                        wait("y_ready", n)
                    for i, kind in enumerate((S1, B1) if n < NT else (S2, B2)):
                        m = mm(bank(b + i), cstack[:, nt(n % NT)], stacks[:, kind, :], True, True)
                    m.then_inc(S["cond_ready"], 1)

                def turn_y(n):
                    wait("y_ready", n + 1)
                    if n < NT - 2:
                        cond(n + 2)
                    elif NT < n < 2 * NT - 1:
                        cond(n + 1)
                    if n in (NT, NT + 1):
                        wait("pt_split", PER["pt_split"] - 1 + n - NT)
                    else:
                        wait("y_split", max(n - 1, 0))
                    y = y1[:, n % 3, :] if n < NT else y2[:, n % 2, :]
                    for k in range(KT):
                        m = pe.transpose(bank(5 + n % 2, k * P, (k + 1) * P), y[:, k * P:(k + 1) * P], ident[:])
                    m.then_inc(S["y_turned"], 1)

                def qk(h, c):
                    if h == 0:
                        wait("y_split", 2 * c + 2)
                        wait("h_relu", 0)
                        wait("qk_split", c)
                    elif c < 3:
                        wait("masked", NT * h)
                    else:
                        wait("qk_split", GROUPS * h + c - 2)
                    wait("piece_split", 4 * h + 2)
                    for i in range(2):
                        o = bank(2 + c % 3 if h else 2, i * PAIR, (i + 1) * PAIR)
                        for k in range(KT):
                            m = mm3(o, wqkv_hi[:, i, k, :], wqkv_lo[:, i, k, :], yT_hi[:, k, pair(c)], yT_lo[:, k, pair(c)],
                                    k == 0, k == KT - 1)
                    m.then_inc(S["qk_ready"], 1)

                def values(h, c):
                    if c:
                        take_m("v_split", GROUPS * h + c + 1)
                    elif h == 0:
                        wait("y_split", NT)
                    else:
                        wait("pt_split", PER["pt_split"] // H * h)
                    wait("piece_split", 4 * h + 3)
                    for j in range(2):
                        t = 2 * c + j
                        o = bank(v_bank(h, c), j * P, (j + 1) * P)
                        mm(o, cstack[:, nt(t)], stacks[:, BV, h * DH:(h + 1) * DH], True, False)
                        for k in range(KT):
                            m = mm3(o, yT_hi[:, k, nt(t)], yT_lo[:, k, nt(t)], wqkv_hi[:, 2, k, :], wqkv_lo[:, 2, k, :],
                                    False, k == KT - 1)
                    m.then_inc(S["v_ready"], 1)

                def scores(i, chunks):
                    for b in chunks:
                        wait("masked", i if b == 2 else max(i - 1, 0))
                        lo, hi = max(b * 512, (i % 2) * N), min((b + 1) * 512, (i % 2 + 1) * N)
                        off = (i % 2) * N
                        m = mm3(ps[:, lo:hi], q_hi[:, nt(i % NT)], q_lo[:, nt(i % NT)], k_hi[:, lo - off:hi - off],
                                k_lo[:, lo - off:hi - off], True, True)
                    return m

                def scores_a(h, t, part):
                    i = NT * h + t
                    if part == 0:
                        scores(i, (0, 1) if t % 2 == 0 else (3, 4))
                    else:
                        scores(i, (2,)).then_inc(S["scores_ready"], 1)

                def turn(h, g, r):
                    n = (GROUPS * h + g) * 5 + r
                    if r in (0, 2):
                        wait("probs_ready", NT * h + 2 * g + (1 if r == 0 else 2))
                    if n < 2:
                        wait("y_split", NT - 1 + n)
                    else:
                        wait("pt_split", n - 1)
                    if g == 0 and r == 1:
                        wait("v_split", GROUPS * h + 1)
                    for at, (j, d) in enumerate(ROUNDS[r]):
                        m = pe.transpose(bank(5 + n % 2, at * P, (at + 1) * P), prob[:, (NT * h + 2 * g + j) % 3, d * P:(d + 1) * P],
                                         ident[:])
                    m.then_inc(S["turned"], 1)

                def out_heads(h, g):
                    take_m("o_split", GROUPS * h + g + 1)
                    if g == 0:
                        wait("v_split", GROUPS * (h + 1))
                    order = (8, 9, 0, 1, 2, 3, 4, 5, 6, 7)
                    for d in order:
                        if d in (8, 0, 4):
                            wait("pt_split", (GROUPS * h + g) * 5 + {8: 3, 0: 4, 4: 5}[d])
                        m = mm3(bank(7, 0, PAIR), v_hi[:, d, :], v_lo[:, d, :], PT_hi[:, d, :], PT_lo[:, d, :],
                                d == order[0], d == order[-1])
                    m.then_inc(S["o_ready"], 1)

                def project(h, g, j):
                    t = 2 * g + j
                    take_m("x_added", NT * h + t + 1)
                    wait("o_split", GROUPS * h + g + 1)
                    wait("piece_split", 4 * h + 4)
                    cols = slice(j * P, (j + 1) * P)
                    if h == 0:
                        mm(bank(7), cstack[:, nt(t)], stacks[:, BO, :], True, False)
                    mm3(bank(7), oT_hi[:, cols], oT_lo[:, cols], wo_hi[:], wo_lo[:], h > 0, True).then_inc(S["wo_ready"], 1)

                def hidden(c, half_):
                    n = 2 * c + half_
                    if c:
                        wait("h_relu", n - 1)
                    wait("y_split", NT + 2 * c + 2)
                    wait("piece_split", 4 * H + KT)
                    for i in range(2):
                        t = 2 * half_ + i
                        for k in range(KT):
                            m = mm3(bank(2 + half_, i * PAIR, (i + 1) * PAIR), mw_hi[0][:, k, nt(t)], mw_lo[0][:, k, nt(t)],
                                    yT_hi[:, k, pair(c)], yT_lo[:, k, pair(c)], k == 0, k == KT - 1)
                    m.then_inc(S["h_ready"], 1)

                def mlp_out(t):
                    c, j = divmod(t, 2)
                    if j:
                        take_m("x_mlp", t + 1)
                    elif t:
                        wait("x_mlp", t - 1)
                    wait("h_split", 2 * c + 2)
                    wait("piece_split", 4 * H + 2 * KT)
                    o = bank(4 + 3 * j)
                    mm(o, cstack[:, nt(t)], stacks[:, MB2, :], True, False)
                    for k in range(KT):
                        m = mm3(o, hT_hi[:, c % 2, k, nt(j)], hT_lo[:, c % 2, k, nt(j)], mw_hi[1][:, k, :], mw_lo[1][:, k, :],
                                False, k == KT - 1)
                    m.then_inc(S["m2_ready"], 1)

                pe.wait_ge(stacks1_in, l * 16 * 2 + 16 * 2)
                cond(0)
                cond(1)
                for t in range(NT):
                    turn_y(t)
                    if t % 2 and t >= 3:
                        qk(0, (t - 3) // 2)
                qk(0, GROUPS - 1)
                pe.wait_ge(stacks2_in, l * 16 * 3 + 16 * 3)
                wait("qk_split", GROUPS)
                wait("pads_zero", 3)
                for t in range(2):
                    scores_a(0, t, 0)
                    scores_a(0, t, 1)
                values(0, 0)
                for h in range(H):
                    for g in range(GROUPS):
                        last, more = g == GROUPS - 1, h < H - 1
                        t = 2 * g + 2
                        if g:
                            out_heads(h, g - 1)
                        for r in range(5):
                            turn(h, g, r)
                            if last and more:
                                qk(h + 1, r)
                            elif last:
                                if r == 0:
                                    cond(NT)
                                if r == 3:
                                    cond(NT + 1)
                            elif r < 4:
                                scores_a(h, t + r // 2, r % 2)
                            if g == 0 and r < 4:
                                values(h, r + 1)
                            if g and r in (1, 3):
                                project(h, g - 1, r // 2)
                    out_heads(h, GROUPS - 1)
                    if more:
                        wait("qk_split", GROUPS * (h + 2))
                        scores_a(h + 1, 0, 0)
                        scores_a(h + 1, 0, 1)
                        project(h, GROUPS - 1, 0)
                        scores_a(h + 1, 1, 0)
                        scores_a(h + 1, 1, 1)
                        values(h + 1, 0)
                        project(h, GROUPS - 1, 1)
                turn_y(NT)
                turn_y(NT + 1)
                project(H - 1, GROUPS - 1, 0)
                project(H - 1, GROUPS - 1, 1)
                for c in range(GROUPS):
                    hidden(c, 0)
                    if c < GROUPS - 1:
                        turn_y(NT + 2 * c + 2)
                    hidden(c, 1)
                    if c < GROUPS - 1:
                        turn_y(NT + 2 * c + 3)
                    if c:
                        mlp_out(2 * c - 2)
                        mlp_out(2 * c - 1)
                mlp_out(NT - 2)
                mlp_out(NT - 1)

            pe.wait_ge(lw_in, 16)
            pe.wait_ge(S["y_split"], START + LAYERS * PER["y_split"])
            for t in range(KT):
                if t >= 2:
                    pe.wait_ge(lw_split, t - 1)
                for o in range(KT):
                    m = pe.transpose(bank(5 + t % 2, o * P, (o + 1) * P), lw_raw[:, o, t * P:(t + 1) * P], ident[:])
                m.then_inc(lw_turned, 1)

            def turn_x1(t):
                pe.wait_ge(x1_ready, t + 1)
                if t < 2:
                    pe.wait_ge(lw_split, KT - 1 + t)
                else:
                    pe.wait_ge(x1_split, t - 1)
                for k in range(KT):
                    m = pe.transpose(bank(5 + t % 2, k * P, (k + 1) * P), x[:, t, k * P:(k + 1) * P], ident[:])
                m.then_inc(x1_turned, 1)

            turn_x1(0)
            for t in range(NT):
                if t + 1 < NT:
                    turn_x1(t + 1)
                pe.wait_ge(x1_split, t + 1)
                if t >= 2:
                    pe.wait_ge(z_split, t - 1)
                for k in range(KT):
                    m = mm3(bank(3 + t % 2), yT_hi[:, k, nt(t)], yT_lo[:, k, nt(t)], lw_hi[:, k, :], lw_lo[:, k, :], k == 0, k == KT - 1)
                m.then_inc(z_ready, 1)

            def turn_w(j):
                pe.wait_ge(wt_in[j % 3], 16 * (j // 3 + 1))
                for r, (lo, hi) in enumerate(WT_ROUNDS):
                    n = 3 * j + r
                    if n < 2:
                        pe.wait_ge(x1_split, NT - 1 + n)
                    else:
                        pe.wait_ge(wt_split, n - 1)
                    for d in range(lo, hi):
                        m = pe.transpose(bank(5 + n % 2, (d - lo) * P, (d - lo + 1) * P), prob[:, j % 3, d * P:(d + 1) * P], ident[:])
                    m.then_inc(wt_turned, 1)

            pe.wait_ge(pad_zero, 1)
            turn_w(0)
            for j in range(NT):
                if j + 1 < NT:
                    turn_w(j + 1)
                pe.wait_ge(wt_split, 3 * j + 3)
                if j == 0:
                    pe.wait_ge(z_split, NT)
                if j >= 2:
                    pe.wait_ge(agg_added, j - 1)
                for d in range(NT):
                    m = mm3(bank(j % 2), WT_hi[:, j % 2, d, :], WT_lo[:, j % 2, d, :], z_hi[:, d, :], z_lo[:, d, :], d == 0, d == NT - 1)
                m.then_inc(agg_ready, 1)


_INS = ["x", "src", "dst", "edge_weight", "node_vec1"] + ["L0_gnn_" + n for n in (
    "f_w1", "f_b1", "f_w2", "f_b2", "s1_w", "s1_b", "b1_w", "b1_b", "wq", "bq", "wk", "bk", "wv", "bv", "wo", "bo",
    "s2_w", "s2_b", "b2_w", "b2_b", "m_w1", "m_b1", "m_w2", "m_b2")] + ["L1_gnn_weight"]


def kernel(**inputs):
    import numpy as _np
    import concourse.bacc as _bacc
    from concourse import mybir as _mybir
    from concourse.bass_utils import run_bass_kernel_spmd as _run

    nc = _bacc.Bacc("TRN2", target_bir_lowering=False, num_devices=1)
    arrays = {name: _np.ascontiguousarray(inputs[name]) for name in _INS}
    T = {name: nc.dram_tensor(f"in_{name}_dram", a.shape, _mybir.dt.from_np(a.dtype), kind="ExternalInput").ap()
         for name, a in arrays.items()}
    out = nc.dram_tensor("out_0_dram", (N, D), F32, kind="ExternalOutput").ap()
    build(nc, T, out)
    r = _run(nc, [{f"in_{name}_dram": a for name, a in arrays.items()}], core_ids=[0])
    return r.results[0]["out_0_dram"]
```

```python
from contextlib import ExitStack

import concourse.bass as bass
from concourse import mybir

ALU = mybir.AluOpType
ACT = mybir.ActivationFunctionType
AX = mybir.AxisListType
F32 = mybir.dt.float32
F32R = mybir.dt.float32r
BF16 = mybir.dt.bfloat16
F16 = mybir.dt.float16
I32 = mybir.dt.int32

P = 128
N = 1250
NT = -(-N // P)
NP = NT * P
LAST = N - (NT - 1) * P
D = 512
KT = D // P
H = 4
DH = D // H
LAYERS = 4
C16 = 16
FREQS = 32
EPS = 1e-5
SCALE = float(DH) ** -0.5
ABSENT = -1e30
E = 21250
GK = 3
GE = GK * P
NG = -(-E // GE)
WIN = 32
CHUNK_G = 4
NCH = NG // CHUNK_G
SBUFS = 4
AHEAD = SBUFS - 1
UNROLL_G = 2 * CHUNK_G
ET = NG * GK
FULL_G = E // GE
TAIL_E = E - FULL_G * GE
GROUPS = NT // 2
PAIR = 2 * P
SLOTS = 6
STACK = SLOTS * C16 + 3
S1, S2, B1, B2, BV, BO, MB2 = range(7)
KINDS, CKINDS = 7, 4
BIAS_ROWS = 3 * LAYERS * KT
BIG = 3.0e38
COND_PART = (0, 0, 0, 1, 1, 2)
WEIGHT_PART = (0, 1, 2, 0, 1, 0)

START = NT

TWO_PI = 6.283185307179586
TURN = (6.28125, 2029.0 / 2 ** 20, TWO_PI - 6.28125 - 2029.0 / 2 ** 20)
MAGIC = 1.5 * 2 ** 23
PI_IN = 3.1415925
WT_ROUNDS = ((0, 4), (4, 8), (8, NT))

ROUNDS = (
    [(0, d) for d in (0, 1, 2, 3)],
    [(0, d) for d in (4, 5, 6, 7)],
    [(0, 8), (0, 9), (1, 8), (1, 9)],
    [(1, d) for d in (0, 1, 2, 3)],
    [(1, d) for d in (4, 5, 6, 7)],
)
assert NT == 10 and NG % UNROLL_G == 0 and UNROLL_G % SBUFS == 0

PER = dict(
    cond_ready=2 * NT, stats_ready=2 * NT, rstd_ready=2 * NT, y_ready=2 * NT, y_turned=2 * NT,
    y_hi=2 * NT, y_split=2 * NT,
    qk_ready=H * GROUPS, qk_hi=H * GROUPS, qk_split=H * GROUPS,
    v_ready=H * GROUPS, v_hi=H * GROUPS, v_split=H * GROUPS,
    scores_ready=H * NT, masked=H * NT, exped=H * NT, recip_ready=H * NT, probs_ready=H * NT,
    turned=H * GROUPS * 5, pt_hi=H * GROUPS * 5, pt_split=H * GROUPS * 5,
    o_ready=H * GROUPS, o_hi=H * GROUPS, o_split=H * GROUPS,
    wo_ready=H * NT, x_added=H * NT,
    bn_done=2 * NT, centered=2 * NT, inverted=H * NT, var_eps=2 * NT, h_ready=2 * GROUPS, h_relu=2 * GROUPS, h_split=2 * GROUPS,
    m2_ready=NT, x_mlp=NT,
    piece_hi=4 * H + 2 * KT, piece_split=4 * H + 2 * KT, pads_zero=3,
    bias_cur=1,
)


def build(nc, T, out):
    ctx = ExitStack()
    with ctx:
        def sb(name, shape, dt, c=ctx):
            return c.enter_context(nc.sbuf_tensor(name, shape, dt))

        def sem(name):
            return ctx.enter_context(nc.semaphore(name))

        w_dram = nc.dram_tensor("w_table", [NT, P, N], F32).ap()
        w_stack = nc.dram_tensor("w_stack", [SLOTS, C16, CKINDS, LAYERS, D], BF16).ap()
        b_stack = nc.dram_tensor("b_stack", [3, KINDS, LAYERS, D], BF16).ap()

        ident = sb("ident", [P, P], F32)
        cstack = sb("cstack", [STACK, NP], BF16)
        stacks = sb("stacks_sb", [STACK, KINDS, D], BF16)
        bias_all = sb("bias_all", [P, 3, LAYERS, KT], F32)
        bias = sb("bias", [P, 3, KT], F32)
        half = sb("half", [P, 1], F32)
        bn = sb("bn", [P, 2, 6], F32)
        mv = sb("mv", [P, 2 * NT, 2], F32)
        rs = sb("rs", [P, 2 * NT], F32)
        tiny = sb("tiny", [P, 1], F32)
        nmax = sb("nmax", [P, 4], F32)
        rsum = sb("rsum", [P, 4], F32)
        rinv = sb("rinv", [P, 4], F32)
        rnorm = sb("rnorm", [P, 4], F32)
        f_w1 = sb("f_w1", [64, C16], F32)
        f_w2 = sb("f_w2", [33, C16], F32)
        f_b1 = sb("f_b1", [C16, 2], F32)
        fcol = sb("fcol", [64, 3], F32)
        fcol_i = sb("fcol_i", [64, 1], I32)
        oT_hi = sb("oT_hi", [P, PAIR], F32R)
        oT_lo = sb("oT_lo", [P, PAIR], F32R)

        with ExitStack() as prep:
            row_raw = sb("row_raw", [KINDS + CKINDS * C16, LAYERS * D], F32, prep)
            row_part = [sb(f"row_part{i}", [KINDS + CKINDS * C16, LAYERS * D], BF16, prep) for i in range(3)]
        with ExitStack() as fin:
            lw_hi = sb("lw_hi", [P, KT, D], F32R, fin)
            lw_lo = sb("lw_lo", [P, KT, D], F32R, fin)
        piece = sb("piece", [P, 2, D], F32)
        wqkv_hi = sb("wqkv_hi", [P, 3, KT, DH], F32R)
        wqkv_lo = sb("wqkv_lo", [P, 3, KT, DH], F32R)
        wo_hi = sb("wo_hi", [P, D], F32R)
        wo_lo = sb("wo_lo", [P, D], F32R)

        with ExitStack() as prep:
            with ExitStack() as late:
                cpart = [sb(f"cpart{i}", [C16, NP], BF16, late) for i in range(3)]
            sin_a = sb("sin_a", [64, NP], F32, prep)
            sin_b = sb("sin_b", [64, NP], F32, prep)
            hcond = sb("hcond", [33, NP], F32, prep)
            cpart32 = sb("cpart32", [C16, NP], F32, prep)
        x = sb("x", [P, NT, D], F32)

        with ExitStack() as fin:
            z_hi = sb("z_hi", [P, NT, D], F32R, fin)
            with ExitStack() as early:
                x0 = sb("x0", [P, NT, D], F32, early)
            z_lo = sb("z_lo", [P, NT, D], F32R, fin)
            lw_raw = sb("lw_raw", [P, KT, D], F32, fin)
        with ExitStack() as tables:
            CW = sb("CW", [P, 2, NT, N], F32, tables)
        L = sb("L", [P, NT, N], F32)
        yT_hi = sb("yT_hi", [P, KT, NP], F32R)
        yT_lo = sb("yT_lo", [P, KT, NP], F32R)
        with ExitStack() as mlp:
            y2 = sb("y2", [P, 2, D], F32, mlp)
            mw_hi = [sb("mw1_hi", [P, KT, D], F32R, mlp)]
            mw_lo = [sb("mw1_lo", [P, KT, D], F32R, mlp)]
        with ExitStack() as fin:
            res = sb("res", [P, 2, D], F32, fin)
        q_hi = sb("q_hi", [P, NP], F32R)
        q_lo = sb("q_lo", [P, NP], F32R)
        with ExitStack() as edges:
            eT = sb("eT", [P, 4, GK, NG + UNROLL_G], F32, edges)
            wres = sb("wres", [P, GK, NG], F32, edges)
            wpart = sb("wpart", [P, 3, NG, GK], BF16, edges)
            iota_h = sb("iota_h", [P, NP], F16, edges)
            grow = sb("grow", [1, 2, NG], F32, edges)
            grow_i = sb("grow_i", [1, NG + 1], I32, edges)
            viol = sb("viol", [1, 1], F32, edges)
            with ExitStack() as load:
                iota_i = sb("iota_i", [P, NP], I32, load)
                bias_rows = sb("bias_rows", [BIAS_ROWS, P], F32, load)
                src_i = sb("src_i", [NG, GE], I32, load)
                dst_i = sb("dst_i", [NG, GE], I32, load)
                ef = sb("ef", [NG, 4, GE], F32, load)
                gcol = sb("gcol", [NG, 2], F32, load)
            with ExitStack() as full:
                oh_src = sb("oh_src", [P, P], BF16, full)
                oh_dst = sb("oh_dst", [P, 4, N], BF16, full)
            win = sb("win", [P, 2, CHUNK_G * GK, 4, WIN], BF16, edges)
            onehot = sb("onehot", [P, SBUFS, GK, NP], BF16, edges)
            dist = sb("dist", [P, 2, NP], F16, edges)
        with ExitStack() as tables:
            lnt = sb("lnt", [P, 2, N], F32, tables)
            absent = sb("absent", [P, 2, N], F32, tables)
        k_hi = sb("k_hi", [P, NP], F32R)
        k_lo = sb("k_lo", [P, NP], F32R)
        with ExitStack() as mlp:
            hT_hi = sb("hT_hi", [P, 2, KT, PAIR], F32R, mlp)
            hT_lo = sb("hT_lo", [P, 2, KT, PAIR], F32R, mlp)
            h32 = sb("h32", [P, 2, 2, PAIR], F32, mlp)
            mw_hi.append(sb("mw2_hi", [P, KT, D], F32R, mlp))
            mw_lo.append(sb("mw2_lo", [P, KT, D], F32R, mlp))
            y1 = sb("y1", [P, 3, D], F32, mlp)
        v_hi = sb("v_hi", [P, NT, DH], F32R)
        v_lo = sb("v_lo", [P, NT, DH], F32R)
        with ExitStack() as fin:
            WT_hi = sb("WT_hi", [P, 2, NT, P], F32R, fin)
            WT_lo = sb("WT_lo", [P, 2, NT, P], F32R, fin)
        PT_hi = sb("PT_hi", [P, NT, PAIR], F32R)
        PT_lo = sb("PT_lo", [P, NT, PAIR], F32R)
        prob = sb("prob", [P, 3, NP], F32)

        ps = ctx.enter_context(nc.psum_tensor("ps", [P, 8 * 512], F32))

        def bank(b, lo=0, hi=512):
            return ps[:, b * 512 + lo:b * 512 + hi]

        S = {name: sem(name) for name in PER}
        piece_in = [sem(f"piece_in{i}") for i in range(2)]
        stacks1_in, stacks2_in = sem("stacks1_in"), sem("stacks2_in")

        noise_in, f_in, bias_in, x_in, edge_in = (sem(n) for n in ("noise_in", "f_in", "bias_in", "x_in", "edge_in"))
        pre_set, rows_in, row_parts, stack_out, stack_zero = (sem(n) for n in ("pre_set", "rows_in", "row_parts", "stack_out", "stack_zero"))
        rchain, dchain, sin_ready, emb_ready, hraw, hexp, hsilu = (sem(n) for n in ("rchain", "dchain", "sin_ready", "emb_ready", "hraw", "hexp", "hsilu"))
        cond_raw, cond_hi, cond_parts, cstack_in, iota_set = (sem(n) for n in ("cond_raw", "cond_hi", "cond_parts", "cstack_in", "iota_set"))
        table_zero, edges_ready, edges_turned, eplan = (sem(n) for n in ("table_zero", "edges_ready", "edges_turned", "eplan"))
        flag_read = sem("flag_read")
        a_dist, a_onehot = sem("a_dist"), sem("a_onehot")
        e_win, e_parts, e_onehot, e_sum, e_added, e_chain = (sem(n) for n in ("e_win", "e_parts", "e_onehot", "e_sum", "e_added", "e_chain"))
        g_chain, g_onehot, g_sum, g_added = (sem(n) for n in ("g_chain", "g_onehot", "g_sum", "g_added"))
        tables_done, w_stored, mask_in, mask_ln, mask_done = (sem(n) for n in ("tables_done", "w_stored", "mask_in", "mask_ln", "mask_done"))
        x0_in = sem("x0_in")
        lw_in, lw_turned, lw_hi_done, lw_split = (sem(n) for n in ("lw_in", "lw_turned", "lw_hi_done", "lw_split"))
        fchain, fstats, frstd, x1_ready, x1_turned, x1_hi, x1_split = (sem(n) for n in ("fchain", "fstats", "frstd", "x1_ready", "x1_turned", "x1_hi", "x1_split"))
        fvar, x0_bn = sem("fvar"), sem("x0_bn")
        pool_passed, dve_passed, act_passed = sem("pool_passed"), sem("dve_passed"), sem("act_passed")
        z_ready, z_hi_done, z_split, pad_zero = (sem(n) for n in ("z_ready", "z_hi_done", "z_split", "pad_zero"))
        wt_in = [sem(f"wt_in{i}") for i in range(3)]
        wt_turned, wt_hi_done, wt_split, agg_ready, agg_added, res_ready = (sem(n) for n in ("wt_turned", "wt_hi_done", "wt_split", "agg_ready", "agg_added", "res_ready"))
        stored = [sem(f"stored{i}") for i in range(2)]

        counted = [*S.values(), e_sum, e_chain, g_chain, a_dist, a_onehot]

        def t_bank(n):
            return 5 + n % 2

        def v_bank(h, c):
            return 7 if c else t_bank(PER["turned"] // H * h + 1)

        def qk_bank(h, c):
            return 2 + c % 3 if h else (2, 7)[c % 2]

        def v_slot(h, g, r):
            c = r + (1 if h else 2)
            return c if g == 0 and c < GROUPS else None

        def nt(t):
            return slice(t * P, (t + 1) * P)

        def pair(c):
            return slice(c * PAIR, (c + 1) * PAIR)

        NCHUNKS = ((0, 512), (512, 1024), (1024, NP))

        def round_view(PT, n, r):
            b = bank(5 + n % 2)
            if r == 2:
                return (PT[:, 8:10, :].rearrange("p d (j c) -> p j d c", j=2),
                        b.rearrange("p (j d c) -> p j d c", j=2, d=2))
            j, d = ROUNDS[r][0]
            return PT[:, d:d + 4, j * P:(j + 1) * P], b.rearrange("p (d c) -> p d c", d=4)

        def pieces(h, g, r):
            if h == H - 1 and g == GROUPS - 1:
                return {0: [4 * H], 1: [4 * H + 1], 3: [4 * H + 2], 4: [4 * H + 3]}.get(r, [])
            if r == 1 and g == 0 and h:
                return [4 * h + 3]
            if r == 1 and 0 < g < 4 and h < H - 1:
                return [4 * (h + 1) + g - 1]
            return []

        def piece_parts(n):
            raw = piece[:, n % 2, :]
            if n >= 4 * H:
                which, t = divmod(n - 4 * H, KT)
                return raw, mw_hi[which][:, t, :], mw_lo[which][:, t, :]
            if n % 4 == 3:
                return raw, wo_hi[:], wo_lo[:]
            return raw.rearrange("p (t n) -> p t n", t=KT), wqkv_hi[:, n % 4], wqkv_lo[:, n % 4]

        def store(sp, j):
            n = P if j < NT - 1 else LAST
            sp.wait_ge(res_ready, j + 1)
            sp.dma_start(out[j * P:j * P + n, :], res[0:n, j % 2, :]).then_inc(stored[j % 2], 16)

        block = ctx.enter_context(nc.Block())

        @block.sync
        def _(sp):
            for s in counted:
                sp.sem_inc(s, START)
            sp.wait_ge(pre_set, 1)
            sp.dma_start(sin_a[:, 0:N], T["node_vec1"].rearrange("n o -> o n").broadcast_to([64, N])).then_inc(noise_in, 16)
            sp.dma_start(f_w1[:], T["L0_gnn_f_w1"]).then_inc(f_in, 16)
            sp.dma_start(f_b1[:, 0:1], T["L0_gnn_f_b1"].rearrange("(c o) -> c o", o=1)).then_inc(f_in, 16)
            sp.wait_ge(pre_set, 2)
            sp.dma_start(f_w2[0:C16, :], T["L0_gnn_f_w2"]).then_inc(f_in, 16)
            sp.dma_start(f_w2[32:33, :], T["L0_gnn_f_b2"].rearrange("(o c) -> o c", o=1)).then_inc(f_in, 16)
            sp.wait_ge(pre_set, 4)
            rows = FULL_G * GE
            for dst, src in ((src_i[:], T["src"]), (dst_i[:], T["dst"]), (ef[:, 3, :], T["edge_weight"])):
                sp.dma_start(dst[0:FULL_G, :], src[0:rows].rearrange("(g e) -> g e", e=GE)).then_inc(edge_in, 16)
                sp.dma_start(dst[FULL_G:NG, 0:TAIL_E], src[rows:E].rearrange("(o e) -> o e", o=1)).then_inc(edge_in, 16)
            sp.dma_start(dst_i[FULL_G:NG, TAIL_E:GE],
                         T["dst"][E - (GE - TAIL_E):E].rearrange("(o e) -> o e", o=1)).then_inc(edge_in, 16)
            for i, name in enumerate(("L0_gnn_bq", "L0_gnn_bk", "L0_gnn_m_b1")):
                rows = slice(i * LAYERS * KT, (i + 1) * LAYERS * KT)
                sp.dma_start(bias_rows[rows, :], T[name].rearrange("l (t p) -> (l t) p", p=P)).then_inc(bias_in, 16)
            for k, name in enumerate(("s1_b", "s2_b", "b1_b", "b2_b", "bv", "bo", "m_b2")):
                sp.dma_start(row_raw[k:k + 1, :], T["L0_gnn_" + name].rearrange("(o l) d -> o (l d)", o=1)).then_inc(rows_in, 16)
            for k, name in enumerate(("s1_w", "s2_w", "b1_w", "b2_w")):
                rows = slice(KINDS + k * C16, KINDS + (k + 1) * C16)
                sp.dma_start(row_raw[rows, :].rearrange("j (l d) -> j l d", l=LAYERS),
                             T["L0_gnn_" + name].rearrange("l j d -> j l d")).then_inc(rows_in, 16)

            sp.wait_ge(cond_parts, 1)
            for i, part in enumerate(COND_PART):
                sp.dma_start(cstack[i * C16:(i + 1) * C16, :], cpart[part][:]).then_inc(cstack_in, 16)
            sp.wait_ge(pre_set, 5)
            sp.wait_ge(cstack_in, 16 * SLOTS)
            sp.dma_start(x[:, 0:NT - 1, :], T["x"][0:(NT - 1) * P, :].rearrange("(t p) d -> p t d", p=P)).then_inc(x_in, 16)
            sp.dma_start(x[0:LAST, NT - 1, :], T["x"][(NT - 1) * P:N, :]).then_inc(x_in, 16)

            sp.wait_ge(row_parts, 3)
            for i, part in enumerate(WEIGHT_PART):
                for k in range(CKINDS):
                    sp.dma_start(w_stack[i, :, k].rearrange("j l d -> j (l d)"),
                                 row_part[part][KINDS + k * C16:KINDS + (k + 1) * C16, :]).then_inc(stack_out, 16)
            for part in range(3):
                sp.dma_start(b_stack[part].rearrange("k l d -> k (l d)"), row_part[part][0:KINDS, :]).then_inc(stack_out, 16)

            sp.wait_ge(tables_done, 1)
            sp.dma_start(w_dram.rearrange("t p n -> p t n"), CW[:, 1]).then_inc(w_stored, 16)
            sp.wait_ge(w_stored, 16)
            sp.wait_ge(stack_zero, 1)
            sp.wait_ge(stack_out, 16 * (SLOTS * CKINDS + 3))

            with sp.Fori(0, LAYERS) as l:
                def load_stacks(w, b, loaded):
                    sp.dma_start(stacks[0:SLOTS * C16, w, :],
                                 w_stack[:, :, w, bass.ds(l, 1), :].rearrange("i j k o d -> (i j) k (o d)")).then_inc(loaded, 16)
                    sp.dma_start(stacks[SLOTS * C16:STACK, b, :],
                                 b_stack[:, b, bass.ds(l, 1), :].rearrange("i k o d -> i k (o d)")).then_inc(loaded, 16)

                def load_piece(n):
                    sp.wait_ge(S["piece_split"], START + l * PER["piece_split"] + max(n - 1, 0))
                    if n < 4 * H:
                        h, what = divmod(n, 4)
                        if what < 3:
                            w = T[("L0_gnn_wq", "L0_gnn_wk", "L0_gnn_wv")[what]]
                            src = w[bass.ds(l, 1), :, h * DH:(h + 1) * DH].rearrange("o (t p) n -> p (o t) n", p=P)
                            dst = piece[:, n % 2, :].rearrange("p (t n) -> p t n", t=KT)
                        else:
                            src = T["L0_gnn_wo"][bass.ds(l, 1), h * DH:(h + 1) * DH, :].rearrange("o p n -> p (o n)")
                            dst = piece[:, n % 2, :]
                    else:
                        which, t = divmod(n - 4 * H, KT)
                        src = T[("L0_gnn_m_w1", "L0_gnn_m_w2")[which]][bass.ds(l, 1), t * P:(t + 1) * P, :].rearrange("o p n -> p (o n)")
                        dst = piece[:, n % 2, :]
                    sp.dma_start(dst, src).then_inc(piece_in[n % 2], 16)

                sp.wait_ge(S["v_ready"], START + l * PER["v_ready"])
                load_stacks(slice(S1, CKINDS, 2), slice(S1, BV + 1, 2), stacks1_in)
                for n in range(4):
                    load_piece(n)
                sp.wait_ge(S["m2_ready"], START + l * NT)
                load_stacks(slice(S2, CKINDS, 2), slice(S2, BO + 1, 2), stacks2_in)
                sp.dma_start(stacks[SLOTS * C16:STACK, MB2:KINDS, :],
                             b_stack[:, MB2:KINDS, bass.ds(l, 1), :].rearrange("i k o d -> i k (o d)")).then_inc(stacks2_in, 16)
                for n in range(4, PER["piece_split"]):
                    load_piece(n)

            sp.wait_ge(S["masked"], START + LAYERS * PER["masked"])
            sp.dma_start(lw_raw[:], T["L1_gnn_weight"].rearrange("(t p) d -> p t d", p=P)).then_inc(lw_in, 16)
            sp.dma_start(x0[:, 0:NT - 1, :], T["x"][0:(NT - 1) * P, :].rearrange("(t p) d -> p t d", p=P)).then_inc(x0_in, 16)
            sp.dma_start(x0[0:LAST, NT - 1, :], T["x"][(NT - 1) * P:N, :]).then_inc(x0_in, 16)
            sp.wait_ge(pad_zero, 1)
            for j in range(NT):
                if j >= 3:
                    sp.wait_ge(wt_turned, 3 * (j - 2))
                sp.dma_start(prob[:, j % 3, 0:N], w_dram[j]).then_inc(wt_in[j % 3], 16)
                if j >= 3:
                    store(sp, j - 3)
            for j in range(NT - 3, NT):
                store(sp, j)
            for i in range(2):
                sp.wait_ge(stored[i], 16 * NT // 2)

        @block.gpsimd
        def _(pool):
            pool.memset(ident[:], 0.0).then_inc(iota_set, 1)
            pool.wait_ge(iota_set, 1)
            pool.iota(fcol_i[0:32, :], [[0, 1]], base=1, channel_multiplier=1).then_inc(iota_set, 1)
            pool.wait_ge(iota_set, 2)
            pool.iota(fcol_i[32:64, :], [[0, 1]], base=1, channel_multiplier=1).then_inc(iota_set, 1)
            pool.wait_ge(iota_set, 3)
            pool.iota(iota_i[:], [[1, NP]], base=0, channel_multiplier=0).then_inc(iota_set, 1)
            pool.affine_select(out=ident[:], in_=ident[:], pattern=[[-1, P]], compare_op=ALU.not_equal,
                               fill=1.0, base=0, channel_multiplier=1).then_inc(iota_set, 1)
            pool.memset(half[:], -0.5).then_inc(iota_set, 1)
            pool.memset(tiny[:], 2.0 ** -60).then_inc(iota_set, 1)
            pool.memset(stacks[0:SLOTS * C16, CKINDS:KINDS, :], 0.0).then_inc(stack_zero, 1)
            pool.wait_ge(stack_zero, 1)
            pool.memset(CW[:, 0], 0.0).then_inc(table_zero, 1)

            pool.wait_ge(table_zero, 1)
            for i in range(2):
                pool.wait_ge(row_parts, i + 1)
                pool.tensor_tensor(row_raw[:], row_raw[:], row_part[i][:], ALU.subtract).then_inc(rchain, 1)
            pool.wait_ge(rchain, 3)

            pool.memset(CW[:, 1], 0.0).then_inc(table_zero, 1)

            pool.wait_ge(table_zero, 2)
            pool.wait_ge(eplan, 2)
            flag = pool.value_load(grow_i[0:1, NG:NG + 1], min_val=0, max_val=1)
            pool.sem_inc(flag_read, 1)
            with pool.If(flag < 1):
                with pool.Fori(0, NCH // 2) as i:
                    for c in range(2):
                        pool.wait_ge(e_win, i * 2 + c + 1)
                        pool.wait_ge(bias_in, 48)
                        for part in range(3):
                            oh = win[:, c, :, 0, :].rearrange("p (g b) w -> p g b w", b=GK)
                            o = win[:, c, :, 1 + part, :].rearrange("p (g b) w -> p g b w", b=GK)
                            wp = wpart[:, part, bass.ds(i * UNROLL_G + c * CHUNK_G, CHUNK_G), :]
                            m = pool.tensor_tensor(o, oh, wp.unsqueeze(3).to_broadcast([P, CHUNK_G, GK, WIN]), ALU.mult)
                        m.then_inc(e_parts, 1)
                pool.wait_ge(e_parts, NCH)

            for t in range(NT - 1):
                pool.wait_ge(S["stats_ready"], START + t + 1)
                pool.tensor_scalar(rs[:, t:t + 1], mv[:, t, 1:2], EPS, None, ALU.add).then_inc(S["var_eps"], 1)
                pool.wait_ge(S["var_eps"], START + t + 1)
                pool.tensor_tensor(rs[:, t:t + 1], rs[:, t:t + 1], half[:], ALU.pow).then_inc(S["rstd_ready"], 1)

            with pool.Fori(0, LAYERS) as l:
                def wait(name, n):
                    pool.wait_ge(S[name], START + l * PER[name] + n)

                def settled():
                    pool.sem_inc(pool_passed, 1)

                def rsqrt(n):
                    i = n % (2 * NT)
                    wait("stats_ready", n + 1)
                    settled()
                    pool.tensor_scalar(rs[:, i:i + 1], mv[:, i, 1:2], EPS, None, ALU.add).then_inc(S["var_eps"], 1)
                    wait("var_eps", n + 1)
                    pool.tensor_tensor(rs[:, i:i + 1], rs[:, i:i + 1], half[:], ALU.pow).then_inc(S["rstd_ready"], 1)

                def rest(n):
                    wait("piece_hi", n + 1)
                    raw, hi, lo = piece_parts(n)
                    pool.tensor_tensor(lo, raw, hi.bitcast(F32), ALU.subtract).then_inc(S["piece_split"], 1)

                def norm(i):
                    wait("recip_ready", i + 1)
                    settled()
                    buf, r = prob[:, i % 3, 0:N], rnorm[:, i % 4:i % 4 + 1]
                    pool.tensor_scalar(buf, buf, r, 1.0, ALU.mult, ALU.mult).then_inc(S["probs_ready"], 1)

                def h_rest(c, half_):
                    wait("h_relu", 2 * c + half_ + 1)
                    pool.tensor_tensor(hT_lo[:, c % 2, 2 * half_:2 * half_ + 2, :], h32[:, half_],
                                       hT_hi[:, c % 2, 2 * half_:2 * half_ + 2, :].bitcast(F32), ALU.subtract)\
                        .then_inc(S["h_split"], 1)

                wait("h_relu", 0)
                settled()
                pool.tensor_copy(bias[:], bias_all[:, :, bass.ds(l, 1), :].rearrange("p k o t -> p k (o t)")).then_inc(S["bias_cur"], 1)
                for n in range(2):
                    rest(n)
                rsqrt(NT - 1)
                for n in range(2, 4):
                    rest(n)
                wait("y_turned", NT)
                settled()
                for b in range(3):
                    pool.memset(prob[:, b, N:NP], 0.0).then_inc(S["pads_zero"], 1)
                norm(0)
                norm(1)
                for h in range(H):
                    for g in range(GROUPS):
                        if g < GROUPS - 1:
                            norm(NT * h + 2 * g + 2)
                        for r in range(5):
                            for n in pieces(h, g, r):
                                rest(n)
                        if h == H - 1 and g:
                            rsqrt(NT + 2 * g - 2)
                            rsqrt(NT + 2 * g - 1)
                        if g < GROUPS - 1:
                            norm(NT * h + 2 * g + 3)
                    if h < H - 1:
                        norm(NT * (h + 1))
                        norm(NT * (h + 1) + 1)
                for n in range(2):
                    rest(4 * H + KT + n)
                rsqrt(2 * NT - 2)
                rsqrt(2 * NT - 1)
                for c in range(GROUPS):
                    h_rest(c, 0)
                    h_rest(c, 1)
                    if c == 0:
                        for n in range(2, KT):
                            rest(4 * H + KT + n)
                    if c:
                        for t in (2 * c - 2, 2 * c - 1):
                            rsqrt(2 * NT + t)
                rsqrt(3 * NT - 2)

            pool.wait_ge(S["m2_ready"], START + LAYERS * NT)
            pool.memset(prob[:, :, N:NP], 0.0).then_inc(pad_zero, 1)
            for n in range(2 * NT):
                i = n % 4
                pool.wait_ge(fstats, n + 1)
                pool.tensor_scalar(rs[:, i:i + 1], mv[:, i, 1:2], EPS, None, ALU.add).then_inc(fvar, 1)
                pool.wait_ge(fvar, n + 1)
                pool.tensor_tensor(rs[:, i:i + 1], rs[:, i:i + 1], half[:], ALU.pow).then_inc(frstd, 1)

        @block.scalar
        def _(act):
            act.wait_ge(sin_ready, 1)
            act.activation(sin_a[:], sin_a[:], ACT.Sin).then_inc(emb_ready, 1)
            act.wait_ge(hraw, 1)
            act.wait_ge(hsilu, 1)
            act.activation(cpart32[:], ps[0:C16, 0:NP], ACT.Exp, bias=f_b1[:, 1:2], scale=-1.0).then_inc(hexp, 1)
            for i in range(3):
                act.wait_ge(rchain, i + 1)
                act.activation(row_part[i][:], row_raw[:], ACT.Copy).then_inc(row_parts, 1)
            act.wait_ge(cond_raw, 1)
            act.activation(cpart[0][:], ps[0:C16, 3 * 512:3 * 512 + NP], ACT.Copy).then_inc(cond_hi, 1)

            act.wait_ge(eplan, 2)
            flag = act.value_load(grow_i[0:1, NG:NG + 1], min_val=0, max_val=1)
            with act.If(flag < 1):
                def distance(group, j):
                    act.activation(dist[:, j % 2, :], iota_h[:], ACT.Abs, bias=eT[:, 0, GK - 1, group], scale=-1.0).then_inc(a_dist, 1)

                distance(slice(0, 1), 0)
                with act.Fori(0, NG // UNROLL_G) as i:
                    for j in range(UNROLL_G):
                        act.wait_ge(a_onehot, START + i * UNROLL_G + j)
                        act.sem_inc(act_passed, 1)
                        distance(bass.ds(i * UNROLL_G + j + 1, 1), j + 1)
                        act.wait_ge(a_dist, START + i * UNROLL_G + j + 1)
                        act.wait_ge(e_sum, START + i * UNROLL_G + j - AHEAD)
                        act.activation(onehot[:, j % SBUFS, GK - 1, :], dist[:, j % 2, :], ACT.Relu, bias=1.0, scale=-1.0)\
                           .then_inc(a_onehot, 1)

            for t in range(NT):
                if t == 0:
                    act.wait_ge(tables_done, 1)
                    act.wait_ge(flag_read, 1)
                    act.wait_ge(iota_set, 7)
                if t >= 2:
                    act.wait_ge(mask_done, t - 1)
                act.activation(lnt[:, t % 2, :], CW[:, 0, t, :], ACT.Ln, bias=tiny[:]).then_inc(mask_ln, 1)
            act.wait_ge(w_stored, 16)

            with act.Fori(0, LAYERS) as l:
                def wait(name, n):
                    act.wait_ge(S[name], START + l * PER[name] + n)

                def y_hi_(n):
                    t = n % NT
                    wait("y_turned", n + 1)
                    act.activation(yT_hi[:, :, nt(t)], bank(5 + n % 2).rearrange("p (k c) -> p k c", k=KT),
                                   ACT.Copy).then_inc(S["y_hi"], 1)

                def qk_hi_(h, c):
                    wait("qk_ready", GROUPS * h + c + 1)
                    b = qk_bank(h, c)
                    act.activation(q_hi[:, pair(c)], bank(b, 0, PAIR), ACT.Identity, bias=bias[:, 0, h:h + 1])
                    act.activation(k_hi[:, pair(c)], bank(b, PAIR, 512), ACT.Identity, bias=bias[:, 1, h:h + 1])\
                       .then_inc(S["qk_hi"], 1)

                def v_hi_(h, c):
                    wait("v_ready", GROUPS * h + c + 1)
                    act.activation(v_hi[:, 2 * c:2 * c + 2, :], bank(v_bank(h, c), 0, PAIR).rearrange("p (t c) -> p t c", t=2),
                                   ACT.Copy).then_inc(S["v_hi"], 1)

                def exp(i):
                    wait("masked", i + 1)
                    buf = prob[:, i % 3, 0:N]
                    act.activation(buf, buf, ACT.Exp, bias=nmax[:, i % 4:i % 4 + 1], scale=-1.0,
                                   accum_out=rsum[:, i % 4:i % 4 + 1]).then_inc(S["exped"], 1)

                def pt_hi_(h, g, r):
                    n = (GROUPS * h + g) * 5 + r
                    wait("turned", n + 1)
                    if r == 0:
                        wait("o_ready", GROUPS * h + g)
                    o, i = round_view(PT_hi, n, r)
                    act.activation(o, i, ACT.Copy).then_inc(S["pt_hi"], 1)

                def o_hi_(h, g):
                    wait("o_ready", GROUPS * h + g + 1)
                    wait("wo_ready", NT * h + 2 * g)
                    act.activation(oT_hi[:], bank(7, 0, PAIR), ACT.Copy).then_inc(S["o_hi"], 1)

                def relu(c, half_):
                    n = 2 * c + half_
                    wait("h_ready", n + 1)
                    if c:
                        wait("h_split", n - 1)
                    if c >= 2:
                        wait("m2_ready", 2 * (c - 1))
                    for i in range(2):
                        t = 2 * half_ + i
                        for o in (h32[:, half_, i, :], hT_hi[:, c % 2, t, :]):
                            m = act.activation(o, bank(2 + half_, i * PAIR, (i + 1) * PAIR), ACT.Relu, bias=bias[:, 2, t:t + 1])
                    m.then_inc(S["h_relu"], 1)

                def piece_hi(n):
                    if n >= 4 * H:
                        if n < 4 * H + KT:
                            wait("masked", H * NT)
                        else:
                            wait("o_ready", H * GROUPS)
                    elif n % 4 < 3:
                        wait(("qk_ready", "qk_ready", "v_ready")[n % 4], GROUPS * (n // 4))
                    else:
                        wait("wo_ready", NT * (n // 4))
                    act.wait_ge(piece_in[n % 2], l * 8 * PER["piece_split"] + 16 * (n // 2 + 1))
                    raw, hi, _ = piece_parts(n)
                    act.activation(hi, raw, ACT.Copy).then_inc(S["piece_hi"], 1)

                piece_hi(0)
                piece_hi(1)
                wait("m2_ready", 0)
                for t in range(NT):
                    y_hi_(t)
                    if t in (1, 3):
                        piece_hi(2 + t // 2)
                    if t == 3:
                        wait("bias_cur", 1)
                    if t % 2 and t >= 3:
                        qk_hi_(0, (t - 3) // 2)
                qk_hi_(0, GROUPS - 1)
                v_hi_(0, 0)
                exp(0)
                exp(1)
                v_hi_(0, 1)
                for h in range(H):
                    for g in range(GROUPS):
                        last, more = g == GROUPS - 1, h < H - 1
                        i = NT * h + 2 * g + 2
                        if g:
                            o_hi_(h, g - 1)
                            exp(i - 1)
                        for r in range(5):
                            pt_hi_(h, g, r)
                            if last and more:
                                qk_hi_(h + 1, r)
                            if r == 2 and not last:
                                exp(i)
                            if v_slot(h, g, r):
                                v_hi_(h, v_slot(h, g, r))
                            for n in pieces(h, g, r):
                                piece_hi(n)
                    o_hi_(h, GROUPS - 1)
                    if h < H - 1:
                        exp(NT * (h + 1))
                        exp(NT * (h + 1) + 1)
                        v_hi_(h + 1, 0)
                wait("v_ready", H * GROUPS)
                y_hi_(NT)
                y_hi_(NT + 1)
                for n in range(2):
                    piece_hi(4 * H + KT + n)
                for c in range(GROUPS):
                    relu(c, 0)
                    if c < GROUPS - 1:
                        y_hi_(NT + 2 * c + 2)
                    relu(c, 1)
                    if c < GROUPS - 1:
                        y_hi_(NT + 2 * c + 3)
                    if c == 0:
                        for n in range(2, KT):
                            piece_hi(4 * H + KT + n)

            for t in range(KT):
                act.wait_ge(lw_turned, t + 1)
                act.activation(lw_hi[:, t, :], bank(5 + t % 2), ACT.Copy).then_inc(lw_hi_done, 1)
            for t in range(NT):
                act.wait_ge(x1_turned, t + 1)
                act.activation(yT_hi[:, :, nt(t)], bank(5 + t % 2).rearrange("p (k c) -> p k c", k=KT), ACT.Copy)\
                   .then_inc(x1_hi, 1)
                if t:
                    act.wait_ge(z_ready, t)
                    act.activation(z_hi[:, t - 1, :], bank(3 + (t - 1) % 2), ACT.Copy).then_inc(z_hi_done, 1)
            act.wait_ge(z_ready, NT)
            act.activation(z_hi[:, NT - 1, :], bank(3 + (NT - 1) % 2), ACT.Copy).then_inc(z_hi_done, 1)
            for j in range(NT):
                for r, (lo, hi) in enumerate(WT_ROUNDS):
                    n = 3 * j + r
                    act.wait_ge(wt_turned, n + 1)
                    if j >= 2:
                        act.wait_ge(agg_ready, j - 1)
                    act.activation(WT_hi[:, j % 2, lo:hi, :], bank(5 + n % 2, 0, (hi - lo) * P).rearrange("p (k c) -> p k c", c=P),
                                   ACT.Copy).then_inc(wt_hi_done, 1)

        @block.vector
        def _(dve):
            dve.memset(sin_a[:, N:NP], 0.0).then_inc(pre_set, 1)
            dve.memset(f_w2[:], 0.0).then_inc(pre_set, 1)
            dve.memset(cstack[SLOTS * C16:STACK, :], 1.0).then_inc(dchain, 1)
            dve.memset(src_i[:], -1).then_inc(pre_set, 1)
            dve.memset(ef[:, 3, :], 0.0).then_inc(pre_set, 1)
            link_n = [1]

            def link(m):
                link_n[0] += 1
                m.then_inc(dchain, 1)
                dve.wait_ge(dchain, link_n[0])

            dve.memset(hcond[:], 0.0)
            link(dve.memset(fcol[0:32, 1:3], 0.0))
            dve.memset(hcond[32:33, :], 1.0)
            dve.memset(fcol[32:64, 1:2], 0.25)
            link(dve.memset(fcol[32:64, 2:3], TWO_PI / 4))
            dve.wait_ge(iota_set, 3)
            link(dve.tensor_scalar(fcol[:, 0:1], fcol_i[:], TWO_PI / 16.0, None, ALU.mult))
            dve.wait_ge(noise_in, 16)
            link(dve.tensor_scalar(sin_a[:], sin_a[:], fcol[:, 0:1], None, ALU.mult))
            link(dve.tensor_scalar(sin_b[:], sin_a[:], 1.0 / TWO_PI, None, ALU.mult))
            link(dve.tensor_scalar(sin_b[:], sin_b[:], fcol[:, 1:2], None, ALU.add))
            link(dve.tensor_scalar(sin_b[:], sin_b[:], MAGIC, None, ALU.add))

            dve.wait_ge(edge_in, 16 * 7)
            dve.tensor_copy(ef[:, 0, :], src_i[:])
            link(dve.tensor_copy(ef[:, 2, :], dst_i[:]))
            link(dve.tensor_reduce(gcol[:, 0:1], ef[:, 2, :], AX.X, ALU.min))
            link(dve.tensor_scalar(gcol[:, 0:1], gcol[:, 0:1], float(N - WIN), None, ALU.min))
            link(dve.tensor_scalar(ef[:, 1, :], ef[:, 2, :], gcol[:, 0:1], None, ALU.subtract))
            dve.tensor_reduce(gcol[:, 1:2], ef[:, 1, :], AX.X, ALU.max).then_inc(edges_ready, 1)

            link(dve.tensor_scalar(sin_b[:], sin_b[:], -MAGIC, None, ALU.add))
            for c in TURN:
                link(dve.scalar_tensor_tensor(out=sin_a[:], in0=sin_b[:], scalar=-c, in1=sin_a[:], op0=ALU.mult, op1=ALU.add))
            link(dve.tensor_scalar(sin_a[:], sin_a[:], fcol[:, 2:3], PI_IN, ALU.add, ALU.min))
            dve.tensor_scalar(sin_a[:], sin_a[:], -PI_IN, None, ALU.max).then_inc(sin_ready, 1)

            dve.wait_ge(rows_in, 16 * (KINDS + CKINDS))
            dve.tensor_scalar(row_raw[0:2, :], row_raw[0:2, :], 1.0, None, ALU.add).then_inc(rchain, 1)
            dve.wait_ge(f_in, 16 * 4)
            dve.tensor_scalar(f_b1[:, 1:2], f_b1[:, 0:1], -1.0, None, ALU.mult).then_inc(hsilu, 1)

            dve.wait_ge(iota_set, 4)
            dve.tensor_copy(iota_h[:], iota_i[:])
            link(dve.memset(eT[:], -1.0))
            dve.wait_ge(edges_turned, 1)
            cols = GK * NG
            by_tile = dict(k=2, b=GK)
            dve.tensor_copy(eT[:, 0:2, :, 0:NG], bank(6, 0, 2 * cols).rearrange("p (k b g) -> p k b g", **by_tile))
            dve.tensor_copy(bias_all[:].rearrange("p k l t -> p (k l t)"), bank(7, 2 * cols, 2 * cols + BIAS_ROWS))
            dve.tensor_copy(grow[:].rearrange("o k g -> o (k g)"), ps[0:1, 6 * 512 + 2 * cols:6 * 512 + 2 * cols + 2 * NG])
            link(dve.tensor_copy(eT[:, 2:4, :, 0:NG], bank(7, 0, 2 * cols).rearrange("p (k b g) -> p k b g", **by_tile)))
            weight = eT[:, 3, :, 0:NG]
            parts = [wpart[:, i].rearrange("p g b -> p b g") for i in range(3)]
            link(dve.tensor_copy(parts[0], weight))
            link(dve.tensor_tensor(wres[:], weight, parts[0], ALU.subtract))
            link(dve.tensor_copy(parts[1], wres[:]))
            link(dve.tensor_tensor(wres[:], wres[:], parts[1], ALU.subtract))
            dve.tensor_copy(parts[2], wres[:]).then_inc(eplan, 1)
            link(dve.tensor_reduce(viol[:], grow[:, 1, :], AX.X, ALU.max))
            link(dve.tensor_copy(grow_i[:, 0:NG], grow[:, 0, :]))
            dve.tensor_scalar(grow_i[:, NG:NG + 1], viol[:], float(WIN), None, ALU.is_ge).then_inc(eplan, 1)
            dve.wait_ge(eplan, 2)

            dve.wait_ge(hexp, 1)
            dve.tensor_scalar(sin_b[0:C16, :], ps[0:C16, 0:NP], f_b1[:, 0:1], None, ALU.add)
            link(dve.tensor_scalar(cpart32[:], cpart32[:], 1.0, None, ALU.add))
            link(dve.reciprocal(cpart32[:], cpart32[:]))
            dve.tensor_tensor(hcond[0:C16, :], sin_b[0:C16, :], cpart32[:], ALU.mult).then_inc(hsilu, 1)

            def window(c, first):
                off = eT[:, 1, :, first].rearrange("p b g -> p g b")
                dve.tensor_tensor(win[:, c, :, 0, :].rearrange("p (g b) w -> p g b w", b=GK),
                                  iota_h[:, 0:WIN].unsqueeze(1).unsqueeze(1).to_broadcast([P, CHUNK_G, GK, WIN]),
                                  off.unsqueeze(3).to_broadcast([P, CHUNK_G, GK, WIN]), ALU.is_equal)\
                   .then_inc(e_win, 1)

            def sources(j, b, group):
                m = dve.tensor_scalar(onehot[:, j % SBUFS, b, :], iota_h[:], eT[:, 0, b, group], None, ALU.is_equal)
                if b == GK - 2:
                    m.then_inc(e_onehot, 1)

            flag = dve.value_load(grow_i[0:1, NG:NG + 1], min_val=0, max_val=1)
            with dve.If(flag < 1):
                window(0, slice(0, CHUNK_G))
                for j in range(AHEAD):
                    for b in range(GK - 1):
                        sources(j, b, slice(j, j + 1))

            dve.wait_ge(cond_hi, 1)
            link(dve.tensor_tensor(cpart32[:], ps[0:C16, 3 * 512:3 * 512 + NP], cpart[0][:], ALU.subtract))
            link(dve.tensor_copy(cpart[1][:], cpart32[:]))
            link(dve.tensor_tensor(cpart32[:], cpart32[:], cpart[1][:], ALU.subtract))
            dve.tensor_copy(cpart[2][:], cpart32[:]).then_inc(cond_parts, 1)
            dve.wait_ge(cond_parts, 1)
            dve.memset(x[:, NT - 1, :], 0.0).then_inc(pre_set, 1)
            dve.wait_ge(table_zero, 2)

            flag = dve.value_load(grow_i[0:1, NG:NG + 1], min_val=0, max_val=1)
            with dve.If(flag < 1):
                with dve.Fori(0, NG // UNROLL_G) as i:
                    for j in range(UNROLL_G):
                        dve.wait_ge(e_sum, START + i * UNROLL_G + j + 1)
                        base = dve.value_load(grow_i[0:1, bass.ds(i * UNROLL_G + j, 1)], min_val=0, max_val=N - WIN)
                        sums = ps[:, (j % 2) * 3 * 512:(j % 2) * 3 * 512 + NT * 4 * WIN].rearrange("p (t k w) -> p k t w", k=4, w=WIN)
                        both = CW[:, :, :, bass.ds(base, WIN)]
                        only = CW[:, 1, :, bass.ds(base, WIN)]
                        at = START + i * 3 * UNROLL_G + 3 * j
                        dve.wait_ge(e_chain, at)
                        dve.tensor_tensor(both, both, sums[:, 0:2], ALU.add).then_inc(e_chain, 1)
                        ahead = bass.ds(i * UNROLL_G + j + AHEAD, 1)
                        sources(j + AHEAD, 0, ahead)
                        dve.wait_ge(e_chain, at + 1)
                        dve.tensor_tensor(only, only, sums[:, 2], ALU.add).then_inc(e_chain, 1)
                        sources(j + AHEAD, 1, ahead)
                        dve.wait_ge(e_chain, at + 2)
                        dve.tensor_tensor(only, only, sums[:, 3], ALU.add).then_inc(e_chain, 1)
                        if j == 0:
                            window(1, bass.ds(i * UNROLL_G + CHUNK_G, CHUNK_G))
                        if j == CHUNK_G:
                            window(0, bass.ds(i * UNROLL_G + UNROLL_G, CHUNK_G))
                dve.wait_ge(e_chain, START + 3 * NG)
            with dve.Else():
                with dve.Fori(0, NT) as s:
                    with dve.Fori(0, NG) as g:
                        for b in range(GK):
                            step = s * NG * GK + g * GK + b
                            dve.wait_ge(g_chain, START + 3 * step)
                            dve.tensor_scalar(oh_src[:], iota_h[:, bass.ds(s * P, P)], eT[:, 0, b, bass.ds(g, 1)],
                                              None, ALU.is_equal)
                            dve.tensor_scalar(oh_dst[:, 0, :], iota_h[:, 0:N], eT[:, 2, b, bass.ds(g, 1)],
                                              None, ALU.is_equal).then_inc(g_chain, 1)
                            dve.wait_ge(g_chain, START + 3 * step + 1)
                            for part in range(3):
                                m = dve.tensor_tensor(oh_dst[:, 1 + part, :], oh_dst[:, 0, :],
                                                      wpart[:, part, bass.ds(g, 1), b].to_broadcast([P, N]), ALU.mult)
                            m.then_inc(g_onehot, 1)
                            dve.wait_ge(g_sum, step + 1)
                            for k in range(2):
                                dst = CW[:, k, bass.ds(s, 1), :].rearrange("p o n -> p (o n)")
                                dve.tensor_tensor(dst, dst, ps[:, k * 1536:k * 1536 + N], ALU.add).then_inc(g_chain, 1)
                dve.wait_ge(g_chain, START + 3 * NT * ET)
            dve.memset(viol[:], 0.0).then_inc(tables_done, 1)

            def absences(t):
                if t >= 2:
                    dve.wait_ge(mask_done, t - 1)
                dve.tensor_scalar(absent[:, t % 2, :], CW[:, 0, t, :], 0.0, ABSENT, ALU.is_equal, ALU.mult).then_inc(mask_in, 1)

            dve.wait_ge(x_in, 32)
            absences(0)
            for t in range(NT):
                if t + 1 < NT:
                    absences(t + 1)
                if t < NT - 1:
                    dve.bn_stats(bn[:, t % 2, :], x[:, t, :]).then_inc(S["bn_done"], 1)
                dve.wait_ge(mask_in, t + 1)
                dve.wait_ge(mask_ln, t + 1)
                dve.scalar_tensor_tensor(out=L[:, t, :], in0=lnt[:, t % 2, :], scalar=1.0 / SCALE,
                                         in1=absent[:, t % 2, :], op0=ALU.mult, op1=ALU.add).then_inc(mask_done, 1)
                if t < NT - 1:
                    dve.wait_ge(S["bn_done"], START + t + 1)
                    dve.bn_aggr(mv[:, t, :], bn[:, t % 2, :]).then_inc(S["stats_ready"], 1)
            dve.wait_ge(mask_done, NT)

            with dve.Fori(0, LAYERS) as l:
                def wait(name, n):
                    dve.wait_ge(S[name], START + l * PER[name] + n)

                def settled():
                    dve.sem_inc(dve_passed, 1)

                def stats(n):
                    if n < NT:
                        wait("x_mlp", n - NT + 1)
                    elif n < 2 * NT:
                        wait("x_added", (H - 1) * NT + n % NT + 1)
                    else:
                        wait("x_mlp", n % NT + 1)
                    dve.bn_stats(bn[:, n % 2, :], x[:, n % NT, :]).then_inc(S["bn_done"], 1)
                    wait("bn_done", n + 1)
                    settled()
                    dve.bn_aggr(mv[:, n % (2 * NT), :], bn[:, n % 2, :]).then_inc(S["stats_ready"], 1)

                def rows_of(n):
                    if n < NT:
                        return y1[:, n % 3, :], 3 * (n % 2)
                    return y2[:, n % 2, :], 0

                def center(n):
                    y, b = rows_of(n)
                    wait("cond_ready", n + 1)
                    if n < NT and n >= 3:
                        wait("y_turned", n - 2)
                    elif n >= NT + 2:
                        wait("y_turned", n - 1)
                    dve.scalar_tensor_tensor(out=y, in0=x[:, n % NT, :], scalar=mv[:, n, 0:1], in1=bank(b),
                                             op0=ALU.subtract, op1=ALU.mult).then_inc(S["centered"], 1)

                def norm(n):
                    y, b = rows_of(n)
                    wait("centered", n + 1)
                    wait("rstd_ready", n + 1)
                    dve.scalar_tensor_tensor(out=y, in0=y, scalar=rs[:, n:n + 1], in1=bank(b + 1),
                                             op0=ALU.mult, op1=ALU.add).then_inc(S["y_ready"], 1)

                def y_lo_(n):
                    wait("y_hi", n + 1)
                    dve.tensor_tensor(yT_lo[:, :, nt(n % NT)], bank(5 + n % 2).rearrange("p (k c) -> p k c", k=KT),
                                      yT_hi[:, :, nt(n % NT)].bitcast(F32), ALU.subtract).then_inc(S["y_split"], 1)

                def qk_lo_(h, c):
                    wait("qk_hi", GROUPS * h + c + 1)
                    b = qk_bank(h, c)
                    for i, (hi, lo) in enumerate(((q_hi, q_lo), (k_hi, k_lo))):
                        m = dve.scalar_tensor_tensor(out=lo[:, pair(c)], in0=bank(b, i * PAIR, (i + 1) * PAIR),
                                                     scalar=bias[:, i, h:h + 1], in1=hi[:, pair(c)].bitcast(F32),
                                                     op0=ALU.add, op1=ALU.subtract)
                    m.then_inc(S["qk_split"], 1)

                def v_lo_(h, c):
                    wait("v_hi", GROUPS * h + c + 1)
                    dve.tensor_tensor(v_lo[:, 2 * c:2 * c + 2, :], bank(v_bank(h, c), 0, PAIR).rearrange("p (t c) -> p t c", t=2),
                                      v_hi[:, 2 * c:2 * c + 2, :].bitcast(F32), ALU.subtract).then_inc(S["v_split"], 1)

                def mask(i):
                    wait("scores_ready", i + 1)
                    if i >= 3:
                        g, j = divmod(i - 3, 2)
                        wait("turned", 5 * g + (5 if j else 3))
                    settled()
                    off = (i % 2) * N
                    dve.tensor_tensor_reduce(prob[:, i % 3, 0:N], ps[:, off:off + N], L[:, i % NT, :], -SCALE, BIG,
                                             ALU.add, ALU.min, nmax[:, i % 4:i % 4 + 1]).then_inc(S["masked"], 1)

                def recip(i):
                    r = slice(i % 4, i % 4 + 1)
                    wait("exped", i + 1)
                    dve.reciprocal(rinv[:, r], rsum[:, r]).then_inc(S["inverted"], 1)
                    wait("inverted", i + 1)
                    dve.scalar_tensor_tensor(out=rnorm[:, r], in0=nmax[:, r], scalar=-ABSENT * SCALE * 0.1, in1=rinv[:, r],
                                             op0=ALU.is_lt, op1=ALU.mult).then_inc(S["recip_ready"], 1)

                def pt_lo_(h, g, r):
                    n = (GROUPS * h + g) * 5 + r
                    wait("pt_hi", n + 1)
                    hi, i = round_view(PT_hi, n, r)
                    lo, _ = round_view(PT_lo, n, r)
                    dve.tensor_tensor(lo, i, hi.bitcast(F32), ALU.subtract).then_inc(S["pt_split"], 1)

                def o_lo_(h, g):
                    wait("o_hi", GROUPS * h + g + 1)
                    dve.tensor_tensor(oT_lo[:], bank(7, 0, PAIR), oT_hi[:].bitcast(F32), ALU.subtract).then_inc(S["o_split"], 1)

                def add_wo(h, t):
                    i = NT * h + t
                    wait("wo_ready", i + 1)
                    if h:
                        wait("x_added", i - NT + 1)
                    dve.tensor_tensor(x[:, t, :], bank(7), x[:, t, :], ALU.add).then_inc(S["x_added"], 1)

                def add_mlp(t):
                    wait("m2_ready", t + 1)
                    dve.tensor_tensor(x[:, t, :], bank(4 + 3 * (t % 2)), x[:, t, :], ALU.add).then_inc(S["x_mlp"], 1)

                for t in range(2):
                    center(t)
                    norm(t)
                for t in range(NT):
                    if t + 2 < NT:
                        center(t + 2)
                    if t == 4:
                        wait("bias_cur", 1)
                    if t % 2 == 0 and t >= 4:
                        qk_lo_(0, (t - 4) // 2)
                    y_lo_(t)
                    if t + 2 < NT:
                        norm(t + 2)
                    if t == 3:
                        stats(NT - 1)
                qk_lo_(0, GROUPS - 2)
                qk_lo_(0, GROUPS - 1)
                v_lo_(0, 0)
                mask(0)
                mask(1)
                recip(0)
                v_lo_(0, 1)
                for h in range(H):
                    for g in range(GROUPS):
                        last, more = g == GROUPS - 1, h < H - 1
                        i = NT * h + 2 * g + 2
                        if g:
                            o_lo_(h, g - 1)
                        recip(i - 1)
                        for r in range(5):
                            pt_lo_(h, g, r)
                            if r == 0 and last and not more:
                                center(NT)
                            if last and more:
                                qk_lo_(h + 1, r)
                            if v_slot(h, g, r):
                                v_lo_(h, v_slot(h, g, r))
                            if r == 1 and last and not more:
                                norm(NT)
                            if g and r in (0, 2):
                                add_wo(h, 2 * g - 2 + r // 2)
                            if r == 2 and not last:
                                recip(i)
                            if r == 1 and not last:
                                mask(i)
                        if not last:
                            mask(i + 1)
                        elif not more:
                            center(NT + 1)
                            norm(NT + 1)
                        if g and not more:
                            stats(NT + 2 * g - 2)
                            stats(NT + 2 * g - 1)
                    o_lo_(h, GROUPS - 1)
                    if h < H - 1:
                        mask(NT * (h + 1))
                        add_wo(h, NT - 2)
                        recip(NT * (h + 1))
                        mask(NT * (h + 1) + 1)
                        v_lo_(h + 1, 0)
                        add_wo(h, NT - 1)
                y_lo_(NT)
                y_lo_(NT + 1)
                add_wo(H - 1, NT - 2)
                center(NT + 2)
                norm(NT + 2)
                add_wo(H - 1, NT - 1)
                for t in (NT - 2, NT - 1):
                    stats(NT + t)
                for c in range(GROUPS):
                    if c < GROUPS - 1:
                        for n in (NT + 2 * c + 2, NT + 2 * c + 3):
                            if n + 1 < 2 * NT:
                                center(n + 1)
                            y_lo_(n)
                            if n + 1 < 2 * NT:
                                norm(n + 1)
                    if c:
                        for t in (2 * c - 2, 2 * c - 1):
                            add_mlp(t)
                            stats(2 * NT + t)
                add_mlp(NT - 2)
                stats(3 * NT - 2)
                add_mlp(NT - 1)

            fn = [0]

            def flink(m):
                fn[0] += 1
                m.then_inc(fchain, 1)
                dve.wait_ge(fchain, fn[0])

            def fstat(n):
                flink(dve.bn_stats(bn[:, n % 2, :], x[:, n % NT, :]))
                dve.bn_aggr(mv[:, n % 4, :], bn[:, n % 2, :]).then_inc(fstats, 1)

            def residual(t):
                n = P if t < NT - 1 else LAST
                flink(dve.tensor_tensor(x[0:n, t, :], x[0:n, t, :], x0[0:n, t, :], ALU.add))
                fstat(t)

            def norm_x1(t):
                dve.wait_ge(frstd, t + 1)
                dve.tensor_scalar(x[:, t, :], x[:, t, :], mv[:, t % 4, 0:1], rs[:, t % 4:t % 4 + 1], ALU.subtract, ALU.mult)\
                   .then_inc(x1_ready, 1)

            def z_lo_(t):
                dve.wait_ge(z_hi_done, t + 1)
                dve.tensor_tensor(z_lo[:, t, :], bank(3 + t % 2), z_hi[:, t, :].bitcast(F32), ALU.subtract).then_inc(z_split, 1)

            dve.wait_ge(S["x_mlp"], START + LAYERS * NT)
            dve.wait_ge(x0_in, 32)
            residual(0)
            for t in range(KT):
                dve.wait_ge(lw_hi_done, t + 1)
                dve.tensor_tensor(lw_lo[:, t, :], bank(5 + t % 2), lw_hi[:, t, :].bitcast(F32), ALU.subtract).then_inc(lw_split, 1)
                if t == 1:
                    norm_x1(0)
                    residual(1)
            norm_x1(1)
            residual(2)
            for t in range(NT):
                if t and t + 3 < NT:
                    residual(t + 3)
                dve.wait_ge(x1_hi, t + 1)
                dve.tensor_tensor(yT_lo[:, :, nt(t)], bank(5 + t % 2).rearrange("p (k c) -> p k c", k=KT),
                                  yT_hi[:, :, nt(t)].bitcast(F32), ALU.subtract).then_inc(x1_split, 1)
                if t == 0:
                    residual(3)
                if t + 2 < NT:
                    norm_x1(t + 2)
                if t:
                    z_lo_(t - 1)
            z_lo_(NT - 1)

            def result(j):
                dve.wait_ge(frstd, NT + j + 1)
                if j >= 2:
                    dve.wait_ge(stored[j % 2], 16 * (j // 2))
                n = NT + j
                dve.tensor_scalar(res[:, j % 2, :], x[:, j, :], mv[:, n % 4, 0:1], rs[:, n % 4:n % 4 + 1],
                                  ALU.subtract, ALU.mult).then_inc(res_ready, 1)

            def aggregated(j):
                dve.wait_ge(agg_ready, j + 1)
                m = dve.tensor_tensor(x[:, j, :], bank(j % 2), x[:, j, :], ALU.add)
                m.then_inc(agg_added, 1)
                dve.wait_ge(agg_added, j + 1)
                fstat(NT + j)

            for j in range(NT):
                for r, (lo, hi) in enumerate(WT_ROUNDS):
                    n = 3 * j + r
                    dve.wait_ge(wt_hi_done, n + 1)
                    dve.tensor_tensor(WT_lo[:, j % 2, lo:hi, :], bank(5 + n % 2, 0, (hi - lo) * P).rearrange("p (k c) -> p k c", c=P),
                                      WT_hi[:, j % 2, lo:hi, :].bitcast(F32), ALU.subtract).then_inc(wt_split, 1)
                if j:
                    aggregated(j - 1)
                    result(j - 1)
            aggregated(NT - 1)
            result(NT - 1)

        @block.tensor
        def _(pe):
            def mm(o, a, b, start, stop):
                return pe.matmul(o, a, b, start=start, stop=stop)

            def mm3(o, a_hi, a_lo, b_hi, b_lo, start, stop):
                mm(o, a_hi, b_hi, start, False)
                mm(o, a_hi, b_lo, False, False)
                return mm(o, a_lo, b_hi, False, stop)

            pe.wait_ge(f_in, 16 * 4)
            pe.wait_ge(emb_ready, 1)
            for lo, hi in NCHUNKS:
                m = mm(ps[0:C16, lo:hi], f_w1[:], sin_a[:, lo:hi], True, True)
            m.then_inc(hraw, 1)
            pe.wait_ge(edges_ready, 1)
            pe.wait_ge(iota_set, 6)
            cols = GK * NG
            for kind in range(4):
                for b in range(GK):
                    at = (6 + kind // 2) * 512 + (kind % 2) * cols + b * NG
                    pe.transpose(ps[:, at:at + NG], ef[:, kind, b * P:(b + 1) * P], ident[0:NG, 0:NG])
            pe.wait_ge(bias_in, 48)
            pe.transpose(bank(7, 2 * cols, 2 * cols + BIAS_ROWS), bias_rows[:], ident[0:BIAS_ROWS, 0:BIAS_ROWS])
            for i in range(2):
                at = 6 * 512 + 2 * cols + i * NG
                m = pe.transpose(ps[0:1, at:at + NG], gcol[:, i:i + 1], ident[0:NG, 0:NG])
            m.then_inc(edges_turned, 1)
            pe.wait_ge(hsilu, 2)
            for lo, hi in NCHUNKS:
                m = mm(ps[0:C16, 3 * 512 + lo:3 * 512 + hi], f_w2[:], hcond[:, lo:hi], True, True)
            m.then_inc(cond_raw, 1)

            pe.wait_ge(eplan, 2)
            pe.wait_ge(cond_parts, 1)
            flag = pe.value_load(grow_i[0:1, NG:NG + 1], min_val=0, max_val=1)
            with pe.If(flag < 1):
                with pe.Fori(0, NG // UNROLL_G) as i:
                    for j in range(UNROLL_G):
                        c, gl = divmod(j, CHUNK_G)
                        if gl == 0:
                            pe.wait_ge(e_parts, i * 2 + c + 1)
                        pe.wait_ge(e_onehot, i * UNROLL_G + j + 1)
                        pe.wait_ge(a_onehot, START + i * UNROLL_G + j + 1)
                        pe.wait_ge(e_chain, START + i * 3 * UNROLL_G + 3 * (j - 1))
                        for s in range(NT):
                            for b in range(GK):
                                at = (j % 2) * 3 * 512 + s * 4 * WIN
                                m = mm(ps[:, at:at + 4 * WIN], onehot[:, j % SBUFS, b, nt(s)],
                                       win[:, c, gl * GK + b].rearrange("p k w -> p (k w)"), b == 0, b == GK - 1)
                        m.then_inc(e_sum, 1)
            with pe.Else():
                with pe.Fori(0, NT) as s:
                    with pe.Fori(0, NG) as g:
                        for b in range(GK):
                            step = s * NG * GK + g * GK + b
                            pe.wait_ge(g_onehot, step + 1)
                            pe.wait_ge(g_chain, START + 3 * step)
                            for lo, hi in ((0, 512), (512, 1024), (1024, N)):
                                mm(ps[:, lo:hi], oh_src[:], oh_dst[:, 0, lo:hi], True, True)
                                for part in range(3):
                                    m = mm(ps[:, 1536 + lo:1536 + hi], oh_src[:], oh_dst[:, 1 + part, lo:hi],
                                           part == 0, part == 2)
                            m.then_inc(g_sum, 1)
            pe.wait_ge(cstack_in, 16 * SLOTS)
            pe.wait_ge(tables_done, 1)

            with pe.Fori(0, LAYERS) as l:
                m_last = [("x_mlp", 0)]

                def wait(name, n):
                    pe.wait_ge(S[name], START + l * PER[name] + n)

                def take_m(name, n):
                    wait(*m_last[0])
                    m_last[0] = (name, n)

                def cond(n):
                    b = 3 * (n % 2) if n < NT else 0
                    if n == 0:
                        wait("y_ready", 0)
                    elif n == 1:
                        wait("h_relu", 0)
                        wait("x_mlp", -1)
                    elif n < NT:
                        wait("y_ready", n - 1)
                    elif n == NT:
                        wait("masked", H * NT)
                    else:
                        wait("y_ready", n)
                    for i, kind in enumerate((S1, B1) if n < NT else (S2, B2)):
                        m = mm(bank(b + i), cstack[:, nt(n % NT)], stacks[:, kind, :], True, True)
                    m.then_inc(S["cond_ready"], 1)

                def turn_y(n):
                    wait("y_ready", n + 1)
                    if n < NT - 2:
                        cond(n + 2)
                    elif NT < n < 2 * NT - 1:
                        cond(n + 1)
                    if n in (NT, NT + 1):
                        wait("pt_split", PER["pt_split"] - 1 + n - NT)
                    else:
                        wait("y_split", max(n - 1, 0))
                    y = y1[:, n % 3, :] if n < NT else y2[:, n % 2, :]
                    for k in range(KT):
                        m = pe.transpose(bank(5 + n % 2, k * P, (k + 1) * P), y[:, k * P:(k + 1) * P], ident[:])
                    m.then_inc(S["y_turned"], 1)

                def qk(h, c):
                    if h == 0:
                        wait("y_split", 2 * c + 2)
                        wait("qk_split", max(c - 1, 0))
                        if c < 2:
                            wait(("h_relu", "x_mlp")[c], 0)
                    elif c < 3:
                        wait("masked", NT * h)
                    else:
                        wait("qk_split", GROUPS * h + c - 2)
                    if c == 0:
                        wait("piece_split", 4 * h + 2)
                    for i in range(2):
                        o = bank(qk_bank(h, c), i * PAIR, (i + 1) * PAIR)
                        for k in range(KT):
                            m = mm3(o, wqkv_hi[:, i, k, :], wqkv_lo[:, i, k, :], yT_hi[:, k, pair(c)], yT_lo[:, k, pair(c)],
                                    k == 0, k == KT - 1)
                    m.then_inc(S["qk_ready"], 1)

                def values(h, c):
                    if c:
                        take_m("v_split", GROUPS * h + c + 1)
                    elif h == 0:
                        wait("y_split", NT)
                    else:
                        wait("pt_split", PER["pt_split"] // H * h)
                    if c == 0:
                        wait("piece_split", 4 * h + 3)
                    for j in range(2):
                        t = 2 * c + j
                        o = bank(v_bank(h, c), j * P, (j + 1) * P)
                        mm(o, cstack[:, nt(t)], stacks[:, BV, h * DH:(h + 1) * DH], True, False)
                        for k in range(KT):
                            m = mm3(o, yT_hi[:, k, nt(t)], yT_lo[:, k, nt(t)], wqkv_hi[:, 2, k, :], wqkv_lo[:, 2, k, :],
                                    False, k == KT - 1)
                    m.then_inc(S["v_ready"], 1)

                def scores(i, chunks):
                    for b in chunks:
                        if b in (0, 2, 3):
                            wait("masked", i if b == 2 else max(i - 1, 0))
                        lo, hi = max(b * 512, (i % 2) * N), min((b + 1) * 512, (i % 2 + 1) * N)
                        off = (i % 2) * N
                        m = mm3(ps[:, lo:hi], q_hi[:, nt(i % NT)], q_lo[:, nt(i % NT)], k_hi[:, lo - off:hi - off],
                                k_lo[:, lo - off:hi - off], True, True)
                    return m

                def scores_a(h, t, part):
                    i = NT * h + t
                    if part == 0:
                        scores(i, (0, 1) if t % 2 == 0 else (3, 4))
                    else:
                        scores(i, (2,)).then_inc(S["scores_ready"], 1)

                def turn(h, g, r):
                    n = (GROUPS * h + g) * 5 + r
                    if r in (0, 2):
                        wait("probs_ready", NT * h + 2 * g + (1 if r == 0 else 2))
                    if n < 2:
                        wait("y_split", NT - 1 + n)
                    else:
                        wait("pt_split", n - 1)
                    if g == 0 and r == 1:
                        wait("v_split", GROUPS * h + 1)
                    for at, (j, d) in enumerate(ROUNDS[r]):
                        m = pe.transpose(bank(5 + n % 2, at * P, (at + 1) * P), prob[:, (NT * h + 2 * g + j) % 3, d * P:(d + 1) * P],
                                         ident[:])
                    m.then_inc(S["turned"], 1)

                def out_heads(h, g):
                    take_m("o_split", GROUPS * h + g + 1)
                    if g == 0:
                        wait("v_split", GROUPS * (h + 1))
                    order = (8, 9, 0, 1, 2, 3, 4, 5, 6, 7)
                    for d in order:
                        if d in (8, 0, 4):
                            wait("pt_split", (GROUPS * h + g) * 5 + {8: 3, 0: 4, 4: 5}[d])
                        m = mm3(bank(7, 0, PAIR), v_hi[:, d, :], v_lo[:, d, :], PT_hi[:, d, :], PT_lo[:, d, :],
                                d == order[0], d == order[-1])
                    m.then_inc(S["o_ready"], 1)

                def project(h, g, j):
                    t = 2 * g + j
                    take_m("x_added", NT * h + t + 1)
                    if j == 0:
                        wait("o_split", GROUPS * h + g + 1)
                    if g == 0 and j == 0:
                        wait("piece_split", 4 * h + 4)
                    cols = slice(j * P, (j + 1) * P)
                    if h == 0:
                        mm(bank(7), cstack[:, nt(t)], stacks[:, BO, :], True, False)
                    mm3(bank(7), oT_hi[:, cols], oT_lo[:, cols], wo_hi[:], wo_lo[:], h > 0, True).then_inc(S["wo_ready"], 1)

                def hidden(c, half_):
                    n = 2 * c + half_
                    if c:
                        wait("h_relu", n - 1)
                    if half_ == 0:
                        wait("y_split", NT + 2 * c + 2)
                    if n == 0:
                        wait("piece_split", 4 * H + KT)
                    for i in range(2):
                        t = 2 * half_ + i
                        for k in range(KT):
                            m = mm3(bank(2 + half_, i * PAIR, (i + 1) * PAIR), mw_hi[0][:, k, nt(t)], mw_lo[0][:, k, nt(t)],
                                    yT_hi[:, k, pair(c)], yT_lo[:, k, pair(c)], k == 0, k == KT - 1)
                    m.then_inc(S["h_ready"], 1)

                def mlp_out(t):
                    c, j = divmod(t, 2)
                    if j:
                        take_m("x_mlp", t + 1)
                    elif t:
                        wait("x_mlp", t - 1)
                    if j == 0:
                        wait("h_split", 2 * c + 2)
                    if t == 0:
                        wait("piece_split", 4 * H + 2 * KT)
                    o = bank(4 + 3 * j)
                    mm(o, cstack[:, nt(t)], stacks[:, MB2, :], True, False)
                    for k in range(KT):
                        m = mm3(o, hT_hi[:, c % 2, k, nt(j)], hT_lo[:, c % 2, k, nt(j)], mw_hi[1][:, k, :], mw_lo[1][:, k, :],
                                False, k == KT - 1)
                    m.then_inc(S["m2_ready"], 1)

                pe.wait_ge(stacks1_in, l * 16 * 2 + 16 * 2)
                cond(0)
                cond(1)
                for t in range(NT):
                    turn_y(t)
                    if t == 2:
                        qk(0, 0)
                    if t % 2 and t >= 5:
                        qk(0, (t - 3) // 2)
                qk(0, GROUPS - 1)
                values(0, 0)
                pe.wait_ge(stacks2_in, l * 16 * 3 + 16 * 3)
                wait("qk_split", GROUPS)
                wait("pads_zero", 3)
                for t in range(2):
                    scores_a(0, t, 0)
                    scores_a(0, t, 1)
                values(0, 1)
                for h in range(H):
                    for g in range(GROUPS):
                        last, more = g == GROUPS - 1, h < H - 1
                        t = 2 * g + 2
                        if g:
                            out_heads(h, g - 1)
                        for r in range(5):
                            turn(h, g, r)
                            if g and r == 2:
                                project(h, g - 1, 1)
                            if last and more:
                                qk(h + 1, r)
                            elif last:
                                if r == 0:
                                    cond(NT)
                                if r == 4:
                                    cond(NT + 1)
                            elif r < 4:
                                scores_a(h, t + r // 2, r % 2)
                            if v_slot(h, g, r):
                                values(h, v_slot(h, g, r))
                            if g and r == 0:
                                project(h, g - 1, 0)
                    out_heads(h, GROUPS - 1)
                    if more:
                        wait("qk_split", GROUPS * (h + 2))
                        scores_a(h + 1, 0, 0)
                        scores_a(h + 1, 0, 1)
                        project(h, GROUPS - 1, 0)
                        scores_a(h + 1, 1, 0)
                        scores_a(h + 1, 1, 1)
                        values(h + 1, 0)
                        project(h, GROUPS - 1, 1)
                turn_y(NT)
                turn_y(NT + 1)
                project(H - 1, GROUPS - 1, 0)
                project(H - 1, GROUPS - 1, 1)
                for c in range(GROUPS):
                    hidden(c, 0)
                    if c < GROUPS - 1:
                        turn_y(NT + 2 * c + 2)
                    hidden(c, 1)
                    if c < GROUPS - 1:
                        turn_y(NT + 2 * c + 3)
                    if c:
                        mlp_out(2 * c - 2)
                        mlp_out(2 * c - 1)
                mlp_out(NT - 2)
                mlp_out(NT - 1)

            pe.wait_ge(lw_in, 16)
            pe.wait_ge(S["y_split"], START + LAYERS * PER["y_split"])
            for t in range(KT):
                if t >= 2:
                    pe.wait_ge(lw_split, t - 1)
                for o in range(KT):
                    m = pe.transpose(bank(5 + t % 2, o * P, (o + 1) * P), lw_raw[:, o, t * P:(t + 1) * P], ident[:])
                m.then_inc(lw_turned, 1)

            def turn_x1(t):
                pe.wait_ge(x1_ready, t + 1)
                if t < 2:
                    pe.wait_ge(lw_split, KT - 1 + t)
                else:
                    pe.wait_ge(x1_split, t - 1)
                for k in range(KT):
                    m = pe.transpose(bank(5 + t % 2, k * P, (k + 1) * P), x[:, t, k * P:(k + 1) * P], ident[:])
                m.then_inc(x1_turned, 1)

            turn_x1(0)
            turn_x1(1)
            for t in range(NT):
                pe.wait_ge(x1_split, t + 1)
                if t >= 2:
                    pe.wait_ge(z_split, t - 1)
                for k in range(KT):
                    m = mm3(bank(3 + t % 2), yT_hi[:, k, nt(t)], yT_lo[:, k, nt(t)], lw_hi[:, k, :], lw_lo[:, k, :], k == 0, k == KT - 1)
                m.then_inc(z_ready, 1)
                if t + 2 < NT:
                    turn_x1(t + 2)

            def turn_w(j, r):
                n = 3 * j + r
                lo, hi = WT_ROUNDS[r]
                if r == 0:
                    pe.wait_ge(wt_in[j % 3], 16 * (j // 3 + 1))
                if n < 2:
                    pe.wait_ge(x1_split, NT - 1 + n)
                else:
                    pe.wait_ge(wt_split, n - 1)
                for d in range(lo, hi):
                    m = pe.transpose(bank(5 + n % 2, (d - lo) * P, (d - lo + 1) * P), prob[:, j % 3, d * P:(d + 1) * P], ident[:])
                m.then_inc(wt_turned, 1)

            pe.wait_ge(pad_zero, 1)
            for r in range(3):
                turn_w(0, r)
            pe.wait_ge(z_split, NT)
            for j in range(NT):
                if j >= 2:
                    pe.wait_ge(agg_added, j - 1)
                for r, (lo, hi) in enumerate(WT_ROUNDS):
                    if j + 1 < NT:
                        turn_w(j + 1, r)
                    pe.wait_ge(wt_split, 3 * j + r + 1)
                    for d in range(lo, hi):
                        m = mm3(bank(j % 2), WT_hi[:, j % 2, d, :], WT_lo[:, j % 2, d, :], z_hi[:, d, :], z_lo[:, d, :],
                                d == 0, d == NT - 1)
                m.then_inc(agg_ready, 1)


_INS = ["x", "src", "dst", "edge_weight", "node_vec1"] + ["L0_gnn_" + n for n in (
    "f_w1", "f_b1", "f_w2", "f_b2", "s1_w", "s1_b", "b1_w", "b1_b", "wq", "bq", "wk", "bk", "wv", "bv", "wo", "bo",
    "s2_w", "s2_b", "b2_w", "b2_b", "m_w1", "m_b1", "m_w2", "m_b2")] + ["L1_gnn_weight"]


def kernel(**inputs):
    import numpy as _np
    import concourse.bacc as _bacc
    from concourse import mybir as _mybir
    from concourse.bass_utils import run_bass_kernel_spmd as _run

    nc = _bacc.Bacc("TRN2", target_bir_lowering=False, num_devices=1)
    arrays = {name: _np.ascontiguousarray(inputs[name]) for name in _INS}
    T = {name: nc.dram_tensor(f"in_{name}_dram", a.shape, _mybir.dt.from_np(a.dtype), kind="ExternalInput").ap()
         for name, a in arrays.items()}
    out = nc.dram_tensor("out_0_dram", (N, D), F32, kind="ExternalOutput").ap()
    build(nc, T, out)
    r = _run(nc, [{f"in_{name}_dram": a for name, a in arrays.items()}], core_ids=[0])
    return r.results[0]["out_0_dram"]
```
